# Optimizing a Trainium2 kernel written in Bass

```python
import numpy as np
import jax
import jax.numpy as jnp

def _softmax(x, axis=-1):
    return jax.nn.softmax(x, axis=axis)

def _gelu(x):
    return jax.nn.gelu(x, approximate=True)

def _silu(x):
    return jax.nn.silu(x)

def _sigmoid(x):
    return jax.nn.sigmoid(x)

def _layernorm(x, axis=-1, eps=1e-05):
    m = jnp.mean(x, axis=axis, keepdims=True)
    v = jnp.var(x, axis=axis, keepdims=True)
    return (x - m) / jnp.sqrt(v + eps)

def _scatter_add(tgt, idx, src, axis=0):
    return tgt.at[idx].add(src)

def _segment_sum(src, seg, n):
    return jax.ops.segment_sum(src, seg, n)
kernel_name = 'mk_adj_resnorm_d4_adj_r2_1c5449'

def setup_inputs(seed: int=0):
    np.random.seed(seed)
    _w = jnp.asarray

    def _rec_inputs():
        import jax
        import jax.numpy as jnp
        _gk = jax.random.key(seed)
        x = -0.0003929 + 0.9999 * jax.random.normal(jax.random.fold_in(_gk, 1), (64, 128, 256), jnp.float32)
        _w = (1.0 + jnp.arange(128, dtype=jnp.float32)) ** (-0.5)
        _w = _w / _w.mean()
        _pij = jnp.clip(0.015625 * _w[:, None] * _w[None, :], 0.0, 1.0)
        _a = jax.random.uniform(jax.random.fold_in(_gk, 2), (64, 128, 128)) < _pij
        _a = jnp.logical_or(_a, jnp.eye(128, dtype=bool))
        _af = _a.astype(jnp.float32)
        _af = _af * jax.random.uniform(jax.random.fold_in(_gk, 3), (64, 128, 128), jnp.float32, 0.05, 1)
        adj = _af
        _nm = jnp.ones((64, 128), dtype=bool)
        nodemask = _nm
        return (x, adj, nodemask)
    x, adj, nodemask = _rec_inputs()

    def _L0_gnn_setup():
        import jax, jax.numpy as jnp
        import numpy as np
        EPS = 1e-06
        key = jax.random.key(seed)
        k1, k2, k3 = jax.random.split(key, 3)
        B, N, F, O = (8, 2048, 256, 256)
        x = jax.random.normal(k1, (B, N, F), dtype=jnp.float32)
        adj = jax.random.uniform(k2, (B, N, N), dtype=jnp.float32)
        W = jax.random.normal(k3, (O, 2 * F), dtype=jnp.float32) * (1.0 / np.sqrt(2 * F))
        return {'x': x, 'adj': adj, 'W': W}
    _L0_gnn_all = _L0_gnn_setup()
    _L0_gnn_in = {k: v for k, v in _L0_gnn_all.items() if k in ('W',)}
    del _L0_gnn_all

    def _L1_gnn_setup():
        import jax, jax.numpy as jnp
        import numpy as np
        B, N, D = (8, 1024, 256)
        key = jax.random.key(seed)
        ks = jax.random.split(key, 8)
        scale = 0.5 / np.sqrt(D)
        x = jax.random.normal(ks[0], (B, N, D), dtype=jnp.float32)
        adj = jax.random.uniform(ks[1], (B, N, N), dtype=jnp.float32)
        Wq_w = jax.random.normal(ks[2], (D, D), dtype=jnp.float32) * scale
        Wk_w = jax.random.normal(ks[3], (D, D), dtype=jnp.float32) * scale
        Wv_w = jax.random.normal(ks[4], (D, D), dtype=jnp.float32) * scale
        Wq_b = jnp.zeros((D,), dtype=jnp.float32)
        Wk_b = jnp.zeros((D,), dtype=jnp.float32)
        Wv_b = jnp.zeros((D,), dtype=jnp.float32)
        return {'x': x, 'adj': adj, 'Wq_w': Wq_w, 'Wq_b': Wq_b, 'Wk_w': Wk_w, 'Wk_b': Wk_b, 'Wv_w': Wv_w, 'Wv_b': Wv_b}
    _L1_gnn_all = _L1_gnn_setup()
    _L1_gnn_in = {k: v for k, v in _L1_gnn_all.items() if k in ('Wq_w', 'Wq_b', 'Wk_w', 'Wk_b', 'Wv_w', 'Wv_b')}
    del _L1_gnn_all

    def _L2_gnn_setup():
        import jax, jax.numpy as jnp
        import numpy as np
        HEADS = 8
        DIM_HEAD = 64
        LA = 0.33
        LD = 0.33
        LG = 0.33
        key = jax.random.key(seed)
        ks = jax.random.split(key, 6)
        B, N, D = (4, 512, 256)
        inner = HEADS * DIM_HEAD
        x = jax.random.normal(ks[0], (B, N, D), jnp.float32)
        mask = jax.random.uniform(ks[1], (B, N)) < 0.9
        adjacency_mat = (jax.random.uniform(ks[2], (B, N, N)) < 0.05).astype(jnp.float32)
        distance_mat = jax.random.uniform(ks[3], (B, N, N), jnp.float32) * 5.0
        W_qkv = jax.random.normal(ks[4], (D, inner * 3), jnp.float32) * 0.02
        W_out = jax.random.normal(ks[5], (inner, D), jnp.float32) * 0.02
        b_out = jnp.zeros((D,), jnp.float32)
        return {'x': x, 'mask': mask, 'adjacency_mat': adjacency_mat, 'distance_mat': distance_mat, 'W_qkv': W_qkv, 'W_out': W_out, 'b_out': b_out}
    _L2_gnn_all = _L2_gnn_setup()
    _L2_gnn_in = {k: v for k, v in _L2_gnn_all.items() if k in ('W_qkv', 'W_out', 'b_out')}
    del _L2_gnn_all

    def _L3_gnn_setup():
        import jax, jax.numpy as jnp
        import numpy as np
        B, N, DIN, DOUT, K = (4, 1024, 256, 256, 3)
        key = jax.random.key(seed)
        ks = jax.random.split(key, 8)
        X = jax.random.normal(ks[0], (B, N, DIN), dtype=jnp.float32)
        A = jax.random.uniform(ks[1], (B, N, N), dtype=jnp.float32)
        Wv = jax.random.normal(ks[2], (DIN, DOUT), dtype=jnp.float32) * 0.02
        bv = jax.random.normal(ks[3], (DOUT,), dtype=jnp.float32) * 0.02
        aw = jax.random.normal(ks[4], (2 * DOUT, 1), dtype=jnp.float32) * 0.05
        ab = jax.random.normal(ks[5], (1,), dtype=jnp.float32) * 0.05
        Wk = jax.random.normal(ks[6], (K, DIN, DOUT), dtype=jnp.float32) * 0.02
        bk = jax.random.normal(ks[7], (K, DOUT), dtype=jnp.float32) * 0.02
        return {'X': X, 'A': A, 'Wv': Wv, 'bv': bv, 'aw': aw, 'ab': ab, 'Wk': Wk, 'bk': bk}
    _L3_gnn_all = _L3_gnn_setup()
    _L3_gnn_in = {k: v for k, v in _L3_gnn_all.items() if k in ('Wv', 'bv', 'aw', 'ab', 'Wk', 'bk')}
    del _L3_gnn_all
    return {'x': x, 'adj': adj, 'nodemask': nodemask, 'L0_gnn_W': _L0_gnn_in['W'], 'L1_gnn_Wq_w': _L1_gnn_in['Wq_w'], 'L1_gnn_Wq_b': _L1_gnn_in['Wq_b'], 'L1_gnn_Wk_w': _L1_gnn_in['Wk_w'], 'L1_gnn_Wk_b': _L1_gnn_in['Wk_b'], 'L1_gnn_Wv_w': _L1_gnn_in['Wv_w'], 'L1_gnn_Wv_b': _L1_gnn_in['Wv_b'], 'L2_gnn_W_qkv': _L2_gnn_in['W_qkv'], 'L2_gnn_W_out': _L2_gnn_in['W_out'], 'L2_gnn_b_out': _L2_gnn_in['b_out'], 'L3_gnn_Wv': _L3_gnn_in['Wv'], 'L3_gnn_bv': _L3_gnn_in['bv'], 'L3_gnn_aw': _L3_gnn_in['aw'], 'L3_gnn_ab': _L3_gnn_in['ab'], 'L3_gnn_Wk': _L3_gnn_in['Wk'], 'L3_gnn_bk': _L3_gnn_in['bk']}

def reference(x, adj, nodemask, L0_gnn_W, L1_gnn_Wq_w, L1_gnn_Wq_b, L1_gnn_Wk_w, L1_gnn_Wk_b, L1_gnn_Wv_w, L1_gnn_Wv_b, L2_gnn_W_qkv, L2_gnn_W_out, L2_gnn_b_out, L3_gnn_Wv, L3_gnn_bv, L3_gnn_aw, L3_gnn_ab, L3_gnn_Wk, L3_gnn_bk):
    import jax
    import jax.numpy as jnp

    def _L0_gnn_ref(x, adj, W):
        import jax, jax.numpy as jnp
        import numpy as np
        EPS = 1e-06
        deg = jnp.sum(adj, axis=-1, keepdims=True)
        agg = jnp.einsum('bij,bjf->bif', adj, x) / jnp.maximum(deg, EPS)
        cat = jnp.concatenate([x, agg], axis=2)
        out = jnp.einsum('bnf,of->bno', cat, W)
        return jax.nn.relu(out)

    def _L1_gnn_ref(x, adj, Wq_w, Wq_b, Wk_w, Wk_b, Wv_w, Wv_b):
        import jax, jax.numpy as jnp
        import numpy as np
        B, N, D = (8, 1024, 256)
        query = jnp.einsum('bnd,od->bno', x, Wq_w) + Wq_b
        keyt = jnp.einsum('bnd,od->bno', x, Wk_w) + Wk_b
        value = jnp.einsum('bnd,od->bno', x, Wv_w) + Wv_b
        weight = jnp.einsum('bqd,bkd->bqk', query, keyt)
        weight = adj * jnp.exp(weight)
        weight = weight / jnp.sum(weight, axis=2, keepdims=True)
        return jnp.einsum('bqk,bkd->bqd', weight, value)

    def _L2_gnn_ref(x, mask, adjacency_mat, distance_mat, W_qkv, W_out, b_out):
        import jax, jax.numpy as jnp
        import numpy as np
        HEADS = 8
        DIM_HEAD = 64
        LA = 0.33
        LD = 0.33
        LG = 0.33
        B, N, _ = x.shape
        scale = DIM_HEAD ** (-0.5)
        qkv = (x @ W_qkv).reshape(B, N, HEADS, 3, DIM_HEAD)
        q, k, v = (jnp.transpose(qkv[..., i, :], (0, 2, 1, 3)) for i in range(3))
        dots = jnp.einsum('bhid,bhjd->bhij', q, k) * scale
        big = jnp.finfo(dots.dtype).max
        m2 = mask[:, None, :, None] & mask[:, None, None, :]
        dots = jnp.where(m2, dots, -big)
        attn = jax.nn.softmax(dots, axis=-1) * LA
        adj = jnp.where(m2, adjacency_mat[:, None], 0.0)
        dist = jnp.where(m2, distance_mat[:, None], big)
        attn = attn + LG * adj + LD * jnp.exp(-dist)
        out = jnp.einsum('bhij,bhjd->bhid', attn, v)
        out = jnp.transpose(out, (0, 2, 1, 3)).reshape(B, N, HEADS * DIM_HEAD)
        return out @ W_out + b_out

    def _L3_gnn_ref(X, A, Wv, bv, aw, ab, Wk, bk):
        import jax, jax.numpy as jnp
        import numpy as np
        B, N, DIN, DOUT, K = (4, 1024, 256, 256, 3)
        d = Wv.shape[1]
        Xw = X @ Wv + bv
        sj = Xw @ aw[:d, 0]
        si = Xw @ aw[d:, 0]
        e = jax.nn.leaky_relu(sj[:, None, :] + si[:, :, None] + ab[0], negative_slope=0.2)
        alpha_matrix = A * jnp.exp(e)
        transition = alpha_matrix / (jnp.sum(alpha_matrix, axis=-1, keepdims=True) + 1e-12)
        H = jnp.zeros(X.shape[:-1] + (d,), dtype=X.dtype)
        Xk = X
        for k in range(Wk.shape[0]):
            H = H + Xk @ Wk[k] + bk[k]
            Xk = jnp.einsum('bij,bjd->bid', transition, Xk)
        return jax.nn.relu(H)
    x = _layernorm(x + _L0_gnn_ref(x, adj, L0_gnn_W), axis=-1)
    x = _layernorm(x + _L1_gnn_ref(x, adj, L1_gnn_Wq_w, L1_gnn_Wq_b, L1_gnn_Wk_w, L1_gnn_Wk_b, L1_gnn_Wv_w, L1_gnn_Wv_b), axis=-1)
    x = _layernorm(x + _L2_gnn_ref(x, nodemask, adj, adj, L2_gnn_W_qkv, L2_gnn_W_out, L2_gnn_b_out), axis=-1)
    x = _layernorm(x + _L3_gnn_ref(x, adj, L3_gnn_Wv, L3_gnn_bv, L3_gnn_aw, L3_gnn_ab, L3_gnn_Wk, L3_gnn_bk), axis=-1)
    return x

_drawn_inputs = setup_inputs


def setup_inputs(seed=0):
    import zlib

    import numpy as np

    out = dict(_drawn_inputs(seed))
    spreads = {'L1_gnn_Wq_b': (0.0, 0.1),
     'L1_gnn_Wk_b': (0.0, 2.0),
     'L1_gnn_Wv_b': (0.0, 0.1),
     'L2_gnn_b_out': (0.0, 0.1)}
    factors = {'L3_gnn_Wv': 4.144, 'L3_gnn_bv': 27.732, 'L3_gnn_aw': 5.187}
    for name, (base, spread) in spreads.items():
        noise = np.random.default_rng([zlib.crc32(name.encode()), seed]).standard_normal(out[name].shape)
        drawn = base * np.exp(spread * noise) if base else spread * noise
        out[name] = jnp.asarray(drawn.astype(out[name].dtype))
    for name, factor in factors.items():
        out[name] = (out[name] * factor).astype(out[name].dtype)
    return out
```

```python
from contextlib import ExitStack

import numpy as np

import concourse.bass as bass
from concourse import mybir

F32 = mybir.dt.float32
F32R = mybir.dt.float32r
U8 = mybir.dt.uint8
ALU = mybir.AluOpType
ACT = mybir.ActivationFunctionType
AX = mybir.AxisListType

N = 128
D = 256
C = D // 128
G = 2
HEADS, DH = 8, 64
INNER = HEADS * DH
HOPS = 3
LA = LD = LG = 0.33
EPS_DEG, EPS_LN, EPS_ROW = 1e-6, 1e-5, 1e-12
BIG = float(np.finfo(np.float32).max)
SLOPE = 0.2
STAGE = {"m": 0, "a": 1, "h": 2, "k": 3}

PRODUCTS = [
    ("h_xT", 0), ("k_xT", 1), ("h_q0", 2), ("h_k0", 3), ("a_xT", 4), ("h_q1", 5), ("h_k1", 0), ("k_sj", 1),
    ("k_y20", 2), ("k_y21", 3), ("a_G", 4), ("h_S0e", 5), ("h_S0o", 0), ("m_nT", 1), ("h_v0", 2), ("h_v1", 3),
    ("a_S", 4), ("h_S1e", 5), ("h_S1o", 0), ("k_T", 1), ("a_v", 2), ("k_y010", 6), ("k_y011", 7),
    ("h_T0e", 3), ("h_T0o", 4), ("a_PV0", 5), ("a_PV1", 0), ("m_xT", 1), ("h_T1e", 2), ("h_T1o", 3),
    ("h_PV0", 4), ("h_PV1", 5), ("h_out", 0), ("m_xW0", 6), ("m_xW1", 7),
]
BANK = dict(PRODUCTS)
LAST_READ = {"m_xW0": "m_ag0", "m_xW1": "m_ag1", "k_y010": "k_TT0", "k_y011": "k_TT1"}

READS = [n for n, _ in PRODUCTS] + ["m_ag0", "m_ag1", "k_Ty0", "k_Ty1", "k_TT0", "k_TT1"]
OTHER = """x0_in adj0_in adj2_in adj3_in mrow_in mcol_in y_out
m_xhi a_xhi h_xhi k_xhi a_Ghi h_ohi0 h_ohi1
m_deg m_adjn m_h m_mv m_ve m_rstd x1_made x0_copy adjT_copy
a_p a_rden a_h a_mv a_ve a_rstd x2_made x1_bias
h_mrow h_m2 h_mneg h_ex h_sum h_mix h_nmx0 h_nmx1 h_e0 h_e1 h_r h_p0 h_p1
h_h h_mv h_ve h_rstd x3_made x2_bias
k_leaky k_e k_w k_den k_tr k_sum k_h k_mv k_ve k_rstd y_made x3_copy
ident halves setup_in setup_sum setup_mm setup_ev setup_hi setup_lo setup_c gate""".split()



def former(product, stages, before):
    names = [n for n, _ in PRODUCTS]
    i = names.index(product)
    for n in reversed(names[:i]):
        if BANK[n] == BANK[product] and n[0] in stages:
            return n, 0
    for n in reversed(names):
        if before and BANK[n] == BANK[product] and n[0] in before:
            return n, 1
    return None, 0


def build(nc, x, adj, mask, maskT, wm, wq, wk, wvT, bv, columns, wqkv, wout, bout, wkvT, kab, wk3, bk3, out):
    pairs = x.shape[0] // G
    steps = pairs + len(STAGE) - 1

    def stages_at(t):
        return "".join(s for s, n in STAGE.items() if 0 <= t - n < pairs)

    with ExitStack() as ctx:
        def sb(name, *shape, dt=F32):
            return ctx.enter_context(nc.sbuf_tensor(name, [128, *shape], dt))

        S = {}
        for n in READS:
            S[n + "_made"] = ctx.enter_context(nc.semaphore(n + "_made"))
            S[n + "_read"] = ctx.enter_context(nc.semaphore(n + "_read"))
        for n in OTHER:
            S[n] = ctx.enter_context(nc.semaphore(n))
        bank = [ctx.enter_context(nc.psum_tensor(f"bank{b}", [128, 512], F32)) for b in range(8)]

        def parts(name, *shape):
            return sb(name + "_hi", *shape, dt=F32R), sb(name + "_lo", *shape, dt=F32R)

        Wm = parts("Wm", C, 2 * D)
        A = parts("A", C, D)
        Wrow = parts("Wrow", C, 128)
        Wv = parts("Wv", C, D)
        Wqkv = parts("Wqkv", C, 3, INNER)
        Wo = parts("Wo", INNER // 128, D)
        Wy2 = parts("Wy2", C, D + 2)
        Wy01 = parts("Wy01", C, 2 * D)
        Wsj = parts("Wsj", C, 128)

        ident = sb("identity", 128)
        minus_half = sb("minus_half", G)
        u_col = sb("u_col", C)
        cq_col = sb("cq_col", 1)
        ke_col = sb("ke_col", 1)
        kab_col = sb("kab_col", 1)
        vec_in = sb("vec_in", 5, C)
        bv_bc = sb("bv_bc", D)
        bout_bc = sb("bout_bc", D)
        bk3_in = sb("bk3_in", HOPS, D)
        bk3_bc = sb("bk3_bc", D)

        x0, x0c, x1, x1b, x2, x2b, x3, x3c = (sb(n, G, D) for n in "x0 x0c x1 x1b x2 x2b x3 x3c".split())
        hh = {s: sb("h_" + s, G, D) for s in "mahk"}
        stats = {s: sb("stats_" + s, G, 6) for s in "mahk"}
        mv = {s: sb("mv_" + s, G, 2) for s in "mahk"}
        ve = {s: sb("ve_" + s, G) for s in "mahk"}
        rstd = {s: sb("rstd_" + s, G) for s in "mahk"}
        xT = {s: parts("xT_" + s, C, G * N) for s in "mahk"}
        adj0, adj2, adj3, adjn, adjT, adjnT = (sb(n, G, N) for n in "adj0 adj2 adj3 adjn adjT adjnT".split())
        deg, degmax, rdeg = sb("deg", G), sb("degmax", G), sb("rdeg", G)
        my = sb("my", G, D)
        GT = parts("GT", C, G * N)
        ae, ap = sb("ae", G, N), sb("ap", G, N)
        av = sb("av", G, D + 1)
        arden = sb("arden", G)
        mrow8, mcol8 = sb("mrow8", G, N, dt=U8), sb("mcol8", G, dt=U8)
        mrow, mcol = sb("mrow", G, N), sb("mcol", G)
        m2, mneg, ex, exs, mix = (sb(n, G, N) for n in "m2 mneg ex exs mix".split())
        hmx, hnmx, hden, hr = (sb(n, G, HEADS) for n in "hmx hnmx hden hr".split())
        work = sb("work", 7168)
        qT = work[:, 0:1024].rearrange("p (m n) -> p m n", m=4)
        kT = work[:, 1024:2048].rearrange("p (m n) -> p m n", m=4)
        hv = work[:, 2048:3072].rearrange("p (g f) -> p g f", g=G)
        hs = work[:, 3072:5120].rearrange("p (g h n) -> p g h n", g=G, h=HEADS)
        pT = work[:, 5120:7168].rearrange("p (g h n) -> p g h n", g=G, h=HEADS)
        oT = parts("oT", G, INNER // 128, N)
        ky2 = sb("ky2", G, D + 2)
        ky1 = sb("ky1", G, D)
        kz, kl, kw, kt, kT_ = (sb(n, G, N) for n in "kz kl kw ktr kT_".split())
        kden, kden2, krden = sb("kden", G), sb("kden2", G), sb("krden", G)
        ksum = sb("ksum", G, D)
        y = sb("y", G, D)
        stage3 = sb("stage3", 1536)

        wm_in = work[:, 0:1024].rearrange("p (c n) -> p c n", c=C)
        wq_in = work[:, 1024:1536].rearrange("p (c n) -> p c n", c=C)
        wk_in = work[:, 1536:2048].rearrange("p (c n) -> p c n", c=C)
        wv_in = work[:, 2048:2560].rearrange("p (c n) -> p c n", c=C)
        wkv_in = work[:, 2560:3072].rearrange("p (c n) -> p c n", c=C)
        wqkv_in = work[:, 3072:6144].rearrange("p (c i n) -> p c i n", c=C, i=3)
        wo_in = work[:, 6144:7168].rearrange("p (c n) -> p c n", c=4)
        wk3_in = stage3[:, :].rearrange("p (k c n) -> p k c n", k=HOPS, c=C)
        bq_in, bk_in, kbv_in, awj_in, awi_in = (vec_in[:, i].unsqueeze(2) for i in range(5))

        xg = x.rearrange("(p g) n f -> p n g f", g=G)
        og = out.rearrange("(p g) n f -> p n g f", g=G)
        adjg = adj.rearrange("(p g) n j -> p n g j", g=G)
        mrowg = mask.rearrange("(p g) n -> p (g n)", g=G)
        mcolg = maskT.rearrange("n (p g) -> p n g", g=G)

        def had(t, stage):
            return not isinstance(t, int) or t > STAGE[stage]

        block = ctx.enter_context(nc.Block())

        @block.sync
        def _(sp):
            def load_x0(p):
                sp.dma_start(x0[:], xg[p]).then_inc(S["x0_in"], 16)

            def load_adj(tile, name, p):
                sp.dma_start(tile[:], adjg[p]).then_inc(S[name], 16)

            def load_mask(p):
                sp.dma_start(mrow8[:], mrowg[p].unsqueeze(0).broadcast_to([128, G * N]).rearrange("q (g n) -> q g n", g=G)).then_inc(S["mrow_in"], 16)
                sp.dma_start(mcol8[:], mcolg[p]).then_inc(S["mcol_in"], 16)

            def weight(dst, src):
                sp.dma_start(dst, src).then_inc(S["setup_in"], 16)

            load_x0(0)
            load_adj(adj0, "adj0_in", 0)
            for src, dst in ((wm, wm_in), (wq, wq_in), (wk, wk_in)):
                weight(dst, src.rearrange("(c p) n -> p c n", p=128))
            weight(vec_in[:], columns)
            weight(kab_col[:], kab.unsqueeze(0).broadcast_to([128, 1]))
            for src, dst in ((wkvT, wkv_in), (wvT, wv_in), (wout, wo_in)):
                weight(dst, src.rearrange("(c p) n -> p c n", p=128))
            weight(wqkv_in, wqkv.rearrange("(c p) (i n) -> p c i n", p=128, i=3))
            for k in range(HOPS):
                weight(wk3_in[:, k], wk3[k].rearrange("(c p) n -> p c n", p=128))
                weight(bk3_in[:, k], bk3[k:k + 1, :].broadcast_to([128, D]))
            weight(bv_bc[:], bv.unsqueeze(0).broadcast_to([128, D]))
            weight(bout_bc[:], bout.unsqueeze(0).broadcast_to([128, D]))
            load_adj(adj2, "adj2_in", 0)
            load_mask(0)
            load_adj(adj3, "adj3_in", 0)

            def gate():
                sp.sem_inc(S["gate"], 1)

            def step(t, stages, more):
                if "h" in stages and "h" in more:
                    p = t - 2
                    sp.wait_ge(S["h_ex"], p + 1)
                    gate()
                    sp.wait_ge(S["h_sum"], p + 1)
                    gate()
                    load_adj(adj2, "adj2_in", p + 1)
                    sp.wait_ge(S["h_mrow"], 2 * (p + 1))
                    gate()
                    load_mask(p + 1)
                if "m" in stages and "m" in more:
                    sp.wait_ge(S["m_adjn"], t + 1)
                    gate()
                    load_adj(adj0, "adj0_in", t + 1)
                if "k" in stages:
                    p = t - 3
                    if "k" in more:
                        sp.wait_ge(S["k_w"], 2 * (p + 1))
                        gate()
                        load_adj(adj3, "adj3_in", p + 1)
                if "m" in stages and "m" in more:
                    sp.wait_ge(S["m_xT_made"], t + 1)
                    gate()
                    sp.wait_ge(S["x0_copy"], t + 1)
                    gate()
                    load_x0(t + 1)
                if "k" in stages:
                    p = t - 3
                    sp.wait_ge(S["y_made"], p + 1)
                    gate()
                    sp.dma_start(og[p], y[:]).then_inc(S["y_out"], 16)

            for t in range(4):
                step(t, stages_at(t), "mahk")
            with sp.Fori(4, pairs - 1) as t:
                step(t, "mahk", "mahk")
            for t in range(pairs - 1, steps):
                more = "".join(s for s, n in STAGE.items() if t + 1 - n < pairs)
                step(t, stages_at(t), more)
            sp.wait_ge(S["y_out"], 16 * pairs)

        n_setup_loads = 3 + 1 + 1 + 3 + 1 + 2 * HOPS + 2

        @block.gpsimd
        def _(pool):
            pool.memset(ident[:], 0.0).then_inc(S["ident"], 1)
            pool.memset(minus_half[:], -0.5).then_inc(S["halves"], 1)
            pool.memset(av[:], 1.0).then_inc(S["halves"], 1)
            pool.wait_ge(S["ident"], 1)
            pool.affine_select(out=ident[:], in_=ident[:], compare_op=ALU.not_equal, fill=1.0, base=0,
                               pattern=[[-1, 128]], channel_multiplier=1).then_inc(S["ident"], 1)
            pool.wait_ge(S["halves"], 2)
            pool.wait_ge(S["setup_in"], 16 * n_setup_loads)

            def gate():
                pool.sem_inc(S["gate"], 1)

            def inv_std(s, p):
                pool.wait_ge(S[s + "_mv"], 2 * (p + 1))
                if had(p, "m"):
                    pool.wait_ge(S[s + "_rstd"], p)
                gate()
                pool.tensor_scalar(ve[s][:], mv[s][:, :, 1], EPS_LN, None, ALU.add).then_inc(S[s + "_ve"], 1)
                pool.wait_ge(S[s + "_ve"], p + 1)
                pool.tensor_tensor(rstd[s][:], ve[s][:], minus_half[:], ALU.pow).then_inc(S[s + "_rstd"], 1)

            def step(t, stages):
                def later(s):
                    return had(t, s)

                if "h" in stages:
                    p = t - 2
                    pool.wait_ge(S["x2_made"], 2 * (p + 1))
                    if later("h"):
                        pool.wait_ge(S["h_h"], p)
                    pool.tensor_tensor(x2b[:], x2[:], bout_bc[:].unsqueeze(1).broadcast_to([128, G, D]), ALU.add).then_inc(S["x2_bias"], 1)
                if "k" in stages:
                    p = t - 3
                    pool.wait_ge(S["x3_made"], 2 * (p + 1))
                    if later("k"):
                        pool.wait_ge(S["k_h"], 2 * p)
                    gate()
                    pool.tensor_copy(x3c[:], x3[:]).then_inc(S["x3_copy"], 1)
                if "h" in stages:
                    p = t - 2
                    pool.wait_ge(S["mrow_in"], 16 * (p + 1))
                    pool.wait_ge(S["mcol_in"], 16 * (p + 1))
                    if later("h"):
                        pool.wait_ge(S["h_m2"], 2 * p)
                    gate()
                    pool.tensor_copy(mrow[:], mrow8[:]).then_inc(S["h_mrow"], 1)
                    pool.tensor_copy(mcol[:], mcol8[:]).then_inc(S["h_mrow"], 1)
                    pool.wait_ge(S["h_mrow"], 2 * (p + 1))
                    if later("h"):
                        pool.wait_ge(S["h_mneg"], p)
                        pool.wait_ge(S["h_mix"], p)
                    gate()
                    for g in range(G):
                        pool.tensor_scalar(m2[:, g], mrow[:, g], mcol[:, g:g + 1], None, ALU.mult).then_inc(S["h_m2"], 1)
                    pool.wait_ge(S["h_m2"], 2 * (p + 1))
                    if later("h"):
                        pool.wait_ge(S["h_S1o_read"], p)
                    gate()
                    pool.tensor_scalar(mneg[:], m2[:], BIG, BIG, ALU.mult, ALU.subtract).then_inc(S["h_mneg"], 1)
                    pool.wait_ge(S["h_ex"], p + 1)
                    pool.tensor_tensor(exs[:], ex[:], adj2[:], ALU.add).then_inc(S["h_sum"], 1)
                    pool.wait_ge(S["h_sum"], p + 1)
                    if later("h"):
                        pool.wait_ge(S["h_p1"], p)
                    pool.tensor_tensor(mix[:], exs[:], m2[:], ALU.mult).then_inc(S["h_mix"], 1)
                if "a" in stages:
                    p = t - 1
                    pool.wait_ge(S["x1_made"], 2 * (p + 1))
                    if later("a"):
                        pool.wait_ge(S["a_h"], 2 * p)
                    pool.tensor_tensor(x1b[:], x1[:], bv_bc[:].unsqueeze(1).broadcast_to([128, G, D]), ALU.add).then_inc(S["x1_bias"], 1)
                if "m" in stages:
                    pool.wait_ge(S["x0_in"], 16 * (t + 1))
                    if later("m"):
                        pool.wait_ge(S["m_h"], 2 * t)
                    gate()
                    pool.tensor_copy(x0c[:], x0[:]).then_inc(S["x0_copy"], 1)
                if "m" in stages:
                    pool.wait_ge(S["m_nT_read"], t + 1)
                    if "a" in stages:
                        pool.wait_ge(S["a_p"], t)
                    gate()
                    pool.tensor_copy(adjT[:], adjnT[:]).then_inc(S["adjT_copy"], 1)
                if "a" in stages:
                    inv_std("a", t - 1)
                if "k" in stages:
                    inv_std("k", t - 3)
                if "h" in stages:
                    inv_std("h", t - 2)
                if "m" in stages:
                    inv_std("m", t)

            for t in range(4):
                step(t, stages_at(t))
            with pool.Fori(4, pairs) as t:
                step(t, "mahk")
            for t in range(pairs, steps):
                step(t, stages_at(t))

        @block.tensor
        def _(pe):
            def product3(o, lhs, rhs, first=True, last=True, skip=False):
                pe.matmul(o, lhs[0], rhs[0], start=first, stop=False, skip_group_check=skip)
                pe.matmul(o, lhs[0], rhs[1], start=False, stop=False, skip_group_check=skip)
                return pe.matmul(o, lhs[1], rhs[0], start=False, stop=last, skip_group_check=skip)

            pe.wait_ge(S["ident"], 2)
            pe.wait_ge(S["setup_in"], 16 * n_setup_loads)
            for c in range(C):
                for o in range(C):
                    pe.matmul(bank[0][:, c * D:(c + 1) * D], wq_in[:, o, c * 128:(c + 1) * 128], wk_in[:, o],
                              start=o == 0, stop=o == C - 1)
            for c in range(C):
                for o in range(C):
                    pe.matmul(bank[1][:, c * 128:(c + 1) * 128], wq_in[:, o, c * 128:(c + 1) * 128],
                              bk_in[:, o].broadcast_to([128, 128]), start=o == 0, stop=o == C - 1)
            for c in range(C):
                for o in range(C):
                    pe.matmul(bank[1][:, D + c * 128:D + (c + 1) * 128], wkv_in[:, o, c * 128:(c + 1) * 128],
                              awj_in[:, o].broadcast_to([128, 128]), start=o == 0, stop=o == C - 1)
            for c in range(C):
                for o in range(C):
                    pe.matmul(bank[2][:, c:c + 1], wk_in[:, o, c * 128:(c + 1) * 128], bq_in[:, o],
                              start=o == 0, stop=o == C - 1)
                for o in range(C):
                    pe.matmul(bank[2][:, C + c:C + c + 1], wkv_in[:, o, c * 128:(c + 1) * 128], awi_in[:, o],
                              start=o == 0, stop=o == C - 1)
            for o in range(C):
                pe.matmul(bank[2][:, 2 * C:2 * C + 1], bq_in[:, o].broadcast_to([128, 128]), bk_in[:, o],
                          start=o == 0, stop=o == C - 1)
            for i, v in enumerate((awj_in, awi_in)):
                for o in range(C):
                    mm = pe.matmul(bank[2][:, 2 * C + 1:2 * C + 2], kbv_in[:, o].broadcast_to([128, 128]), v[:, o],
                                   start=i == 0 and o == 0, stop=i == 1 and o == C - 1)
            mm.then_inc(S["setup_mm"], 1)
            pe.wait_ge(S["setup_ev"], 4)
            pe.wait_ge(S["setup_hi"], 9)
            pe.wait_ge(S["setup_lo"], 9)

            def step(t, stages, before):
                def made(s):
                    return t - STAGE[s] + 1

                def free(name):
                    old, ago = former(name, stages, before)
                    return old and (S[LAST_READ.get(old, old) + "_read"], made(old[0]) - ago)

                def bank_of(name):
                    return bank[BANK[name]]

                def transposes(s, src):
                    if was := free(s + "_xT"):
                        pe.wait_ge(*was)
                    b = bank_of(s + "_xT").rearrange("p (c g n) -> p c g n", c=C, g=G)
                    for c in range(C):
                        for g in range(G):
                            mm = pe.transpose(b[:, c, g], src[:, g, c * 128:(c + 1) * 128], ident[:])
                    mm.then_inc(S[s + "_xT_made"], 1)

                def part(pair, *index):
                    return tuple(q[index] for q in pair)

                def node_part(s, c, g):
                    return part(xT[s], slice(None), c, slice(g * N, (g + 1) * N))

                def heads_qk(name, i, half):
                    if was := free(name):
                        pe.wait_ge(*was)
                    b = bank_of(name).rearrange("p (m n) -> p m n", m=2)
                    for m in range(2):
                        col = (2 * half + m) * 128
                        for c in range(C):
                            mm = product3(b[:, m], part(Wqkv, slice(None), c, i, slice(col, col + 128)),
                                          part(xT["h"], slice(None), c), c == 0, c == C - 1)
                    mm.then_inc(S[name + "_made"], 1)

                def heads_scores(g):
                    if was := free(f"h_S{g}e"):
                        pe.wait_ge(*was)
                    be = bank_of(f"h_S{g}e")
                    if was := free(f"h_S{g}o"):
                        pe.wait_ge(*was)
                    bo = bank_of(f"h_S{g}o")
                    for m in range(HEADS // 2):
                        for odd, b in ((0, be), (1, bo)):
                            rows = slice(64 * odd, 64 * odd + 64)
                            mm = pe.matmul(b[:, m * N:(m + 1) * N], qT[rows, m, g * N:(g + 1) * N],
                                           kT[rows, m, g * N:(g + 1) * N], start=True, stop=True)
                            if m == HEADS // 2 - 1:
                                mm.then_inc(S[f"h_S{g}{'eo'[odd]}_made"], 1)

                def heads_transpose(g):
                    for half in "eo":
                        if was := free(f"h_T{g}{half}"):
                            pe.wait_ge(*was)
                        b = bank_of(f"h_T{g}{half}")
                        pe.wait_ge(S[f"h_p{g}"], made("h"))
                        for m in range(4):
                            mm = pe.transpose(b[:, m * N:(m + 1) * N], hs[:, g, 4 * "eo".index(half) + m], ident[:])
                        mm.then_inc(S[f"h_T{g}{half}_made"], 1)

                def heads_values(g):
                    if was := free(f"h_PV{g}"):
                        pe.wait_ge(*was)
                    b = bank_of(f"h_PV{g}")
                    pe.wait_ge(S[f"h_T{g}e_read"], made("h"))
                    pe.wait_ge(S[f"h_T{g}o_read"], made("h"))
                    for m in range(HEADS // 2):
                        for odd in range(2):
                            h = 2 * m + odd
                            mm = pe.matmul(b[64 * odd:64 * odd + 64, m * N:(m + 1) * N],
                                           hv[:, g, h * DH:(h + 1) * DH], pT[:, g, 4 * odd + m],
                                           start=True, stop=True)
                    mm.then_inc(S[f"h_PV{g}_made"], 1)

                if "h" in stages:
                    pe.wait_ge(S["x2_made"], 2 * made("h"))
                    transposes("h", x2)
                if "k" in stages:
                    pe.wait_ge(S["x3_made"], 2 * made("k"))
                    transposes("k", x3)
                if "h" in stages:
                    pe.wait_ge(S["h_xT_read"], made("h"))
                    heads_qk("h_q0", 0, 0)
                    heads_qk("h_k0", 1, 0)
                if "a" in stages:
                    pe.wait_ge(S["x1_made"], 2 * made("a"))
                    transposes("a", x1)
                if "h" in stages:
                    heads_qk("h_q1", 0, 1)
                    heads_qk("h_k1", 1, 1)
                if "k" in stages:
                    if was := free("k_sj"):
                        pe.wait_ge(*was)
                    b = bank_of("k_sj")
                    pe.wait_ge(S["k_xT_read"], made("k"))
                    for c in range(C):
                        mm = product3(b[:, 0:G * N], part(Wsj, slice(None), c), part(xT["k"], slice(None), c), c == 0, c == C - 1)
                    mm.then_inc(S["k_sj_made"], 1)
                    for g in range(G):
                        if was := free(f"k_y2{g}"):
                            pe.wait_ge(*was)
                        b = bank_of(f"k_y2{g}")
                        for c in range(C):
                            mm = product3(b[:, 0:D + 2], node_part("k", c, g), part(Wy2, slice(None), c), c == 0, c == C - 1)
                        mm.then_inc(S[f"k_y2{g}_made"], 1)
                if "a" in stages:
                    if was := free("a_G"):
                        pe.wait_ge(*was)
                    b = bank_of("a_G").rearrange("p (c n) -> p c n", c=C)
                    pe.wait_ge(S["a_xT_read"], made("a"))
                    for o in range(C):
                        for c in range(C):
                            mm = product3(b[:, o], part(A, slice(None), c, slice(o * 128, (o + 1) * 128)),
                                          part(xT["a"], slice(None), c), c == 0, c == C - 1)
                    mm.then_inc(S["a_G_made"], 1)
                if "h" in stages:
                    for n in ("h_q0", "h_q1", "h_k0", "h_k1"):
                        pe.wait_ge(S[n + "_read"], made("h"))
                    heads_scores(0)
                if "m" in stages:
                    if was := free("m_nT"):
                        pe.wait_ge(*was)
                    b = bank_of("m_nT")
                    pe.wait_ge(S["m_adjn"], made("m"))
                    for g in range(G):
                        mm = pe.transpose(b[:, g * N:(g + 1) * N], adjn[:, g], ident[:])
                    mm.then_inc(S["m_nT_made"], 1)
                if "h" in stages:
                    for g in range(G):
                        if was := free(f"h_v{g}"):
                            pe.wait_ge(*was)
                        b = bank_of(f"h_v{g}")
                        for c in range(C):
                            mm = product3(b[:], node_part("h", c, g), part(Wqkv, slice(None), c, 2), c == 0, c == C - 1)
                        mm.then_inc(S[f"h_v{g}_made"], 1)
                if "a" in stages:
                    if was := free("a_S"):
                        pe.wait_ge(*was)
                    b = bank_of("a_S")
                    for c in range(C):
                        product3(b[:, 0:G * N], part(Wrow, slice(None), c), part(xT["a"], slice(None), c), c == 0, False, True)
                    pe.wait_ge(S["a_G_read"], made("a"))
                    for g in range(G):
                        for c in range(C):
                            mm = product3(b[:, g * N:(g + 1) * N], node_part("a", c, g),
                                          part(GT, slice(None), c, slice(g * N, (g + 1) * N)), False,
                                          c == C - 1, True)
                    mm.then_inc(S["a_S_made"], 1)
                if "h" in stages:
                    heads_scores(1)
                if "k" in stages:
                    if was := free("k_T"):
                        pe.wait_ge(*was)
                    b = bank_of("k_T")
                    pe.wait_ge(S["k_tr"], 2 * made("k"))
                    for g in range(G):
                        mm = pe.transpose(b[:, g * N:(g + 1) * N], kt[:, g], ident[:])
                    mm.then_inc(S["k_T_made"], 1)
                if "a" in stages:
                    if was := free("a_v"):
                        pe.wait_ge(*was)
                    b = bank_of("a_v")
                    for g in range(G):
                        for c in range(C):
                            mm = product3(b[:, g * D:(g + 1) * D], node_part("a", c, g), part(Wv, slice(None), c), c == 0, c == C - 1)
                    mm.then_inc(S["a_v_made"], 1)
                if "k" in stages:
                    for g in range(G):
                        if was := free(f"k_y01{g}"):
                            pe.wait_ge(*was)
                        b = bank_of(f"k_y01{g}")
                        for c in range(C):
                            mm = product3(b[:], node_part("k", c, g), part(Wy01, slice(None), c), c == 0, c == C - 1)
                        mm.then_inc(S[f"k_y01{g}_made"], 1)
                if "h" in stages:
                    heads_transpose(0)
                if "a" in stages:
                    for g in range(G):
                        if was := free(f"a_PV{g}"):
                            pe.wait_ge(*was)
                        b = bank_of(f"a_PV{g}")
                        pe.wait_ge(S["a_p"], made("a"))
                        pe.wait_ge(S["a_v_read"], made("a"))
                        pe.matmul(b[:, 0:D + 1], ap[:, g], av[:, g], start=True, stop=True).then_inc(S[f"a_PV{g}_made"], 1)
                if "k" in stages:
                    pe.wait_ge(S["k_T_read"], made("k"))
                    for g in range(G):
                        pe.wait_ge(S[f"k_y2{g}_read"], made("k"))
                        pe.matmul(bank[BANK[f"k_y01{g}"]][:, D:2 * D], kT_[:, g], ky2[:, g, 0:D], start=False, stop=True,
                                  skip_group_check=True).then_inc(S[f"k_Ty{g}_made"], 1)
                if "m" in stages:
                    pe.wait_ge(S["x0_in"], 16 * made("m"))
                    transposes("m", x0)
                if "h" in stages:
                    heads_transpose(1)
                    pe.wait_ge(S["h_v0_read"], made("h"))
                    pe.wait_ge(S["h_v1_read"], made("h"))
                    heads_values(0)
                if "k" in stages:
                    for g in range(G):
                        pe.wait_ge(S[f"k_Ty{g}_read"], made("k"))
                        pe.matmul(bank[BANK[f"k_y01{g}"]][:, 0:D], kT_[:, g], ky1[:, g], start=False, stop=True,
                                  skip_group_check=True).then_inc(S[f"k_TT{g}_made"], 1)
                if "h" in stages:
                    heads_values(1)
                    if was := free("h_out"):
                        pe.wait_ge(*was)
                    b = bank_of("h_out")
                    for g in range(G):
                        pe.wait_ge(S[f"h_PV{g}_read"], made("h"))
                        for m in range(INNER // 128):
                            mm = product3(b[:, g * D:(g + 1) * D], part(oT, slice(None), g, m), part(Wo, slice(None), m),
                                          m == 0, m == INNER // 128 - 1)
                    mm.then_inc(S["h_out_made"], 1)
                if "m" in stages:
                    for g in range(G):
                        if was := free(f"m_xW{g}"):
                            pe.wait_ge(*was)
                        b = bank_of(f"m_xW{g}")
                        pe.wait_ge(S["m_xT_read"], made("m"))
                        for c in range(C):
                            mm = product3(b[:], node_part("m", c, g), part(Wm, slice(None), c), c == 0, c == C - 1)
                        mm.then_inc(S[f"m_xW{g}_made"], 1)
                if "m" in stages:
                    pe.wait_ge(S["m_nT_read"], made("m"))
                    for g in range(G):
                        pe.wait_ge(S[f"m_xW{g}_read"], made("m"))
                        pe.matmul(bank[BANK[f"m_xW{g}"]][:, 0:D], adjnT[:, g], my[:, g], start=False, stop=True,
                                  skip_group_check=True).then_inc(S[f"m_ag{g}_made"], 1)

            for t in range(4):
                step(t, stages_at(t), stages_at(t - 1) if t else None)
            with pe.Fori(4, pairs) as t:
                step(t, "mahk", "mahk")
            for t in range(pairs, steps):
                step(t, stages_at(t), stages_at(t - 1))

        @block.scalar
        def _(act):
            def copy(dst, src):
                return act.activation(dst, src, ACT.Copy)

            act.wait_ge(S["setup_in"], 16 * n_setup_loads)
            for pair, src in ((Wm, wm_in), (Wv, wv_in), (Wqkv, wqkv_in)):
                copy(pair[0][:], src).then_inc(S["setup_hi"], 1)
            act.activation(Wo[0][:], wo_in, ACT.Copy, scale=LA).then_inc(S["setup_hi"], 1)
            for i in range(2):
                copy(Wy01[0][:, :, i * D:(i + 1) * D], wk3_in[:, i]).then_inc(S["setup_c"], 1)
            act.wait_ge(S["setup_mm"], 1)
            act.wait_ge(S["setup_ev"], 4)
            copy(A[0][:], bank[0][:].rearrange("p (c n) -> p c n", c=C)).then_inc(S["setup_hi"], 1)
            copy(Wrow[0][:], bank[1][:, 0:D].rearrange("p (c n) -> p c n", c=C)).then_inc(S["setup_hi"], 1)
            copy(Wsj[0][:], bank[1][:, D:2 * D].rearrange("p (c n) -> p c n", c=C)).then_inc(S["setup_hi"], 1)
            copy(Wy2[0][:, :, 0:D], wk3_in[:, 2]).then_inc(S["setup_hi"], 1)
            for i in range(2):
                copy(Wy2[0][:, :, D + i:D + i + 1], bank[2][:, C:2 * C].unsqueeze(2)).then_inc(S["setup_c"], 1)
            act.wait_ge(S["setup_c"], 4)
            act.activation(ve["m"][:, 0:1], minus_half[:, 0:1], ACT.Copy).then_inc(S["setup_hi"], 1)

            def step(t, stages):
                def made(s):
                    return t - STAGE[s] + 1

                def later(s):
                    return had(t, s)

                def hi_of_x(s, last_use):
                    act.wait_ge(S[s + "_xT_made"], made(s))
                    if later(s):
                        act.wait_ge(S[last_use + "_made"], made(s) - 1)
                    copy(xT[s][0][:], bank[BANK[s + "_xT"]][:].rearrange("p (c n) -> p c n", c=C)).then_inc(S[s + "_xhi"], 1)

                def exps(g):
                    for h in range(HEADS):
                        if h == 0:
                            act.wait_ge(S[f"h_nmx{g}"], made("h"))
                        act.activation(hs[:, g, h], hs[:, g, h], ACT.Exp, bias=hnmx[:, g, h:h + 1], scale=DH ** -0.5,
                                       accum_out=hden[:, g, h:h + 1]).then_inc(S[f"h_e{g}"], 1)

                def copy_T(g):
                    if later("h"):
                        act.wait_ge(S[f"h_PV{g}_made"], made("h") - 1)
                    for i, half in enumerate("eo"):
                        act.wait_ge(S[f"h_T{g}{half}_made"], made("h"))
                        copy(pT[:, g, 4 * i:4 * i + 4], bank[BANK[f"h_T{g}{half}"]][:].rearrange("p (m n) -> p m n", m=4)).then_inc(S[f"h_T{g}{half}_read"], 1)

                def hi_of_o(g):
                    act.wait_ge(S[f"h_PV{g}_made"], made("h"))
                    if later("h"):
                        act.wait_ge(S["h_out_made"], made("h") - 1)
                    copy(oT[0][:, g], bank[BANK[f"h_PV{g}"]][:].rearrange("p (m n) -> p m n", m=4)).then_inc(S[f"h_ohi{g}"], 1)

                if "h" in stages:
                    hi_of_x("h", "h_v1")
                if "k" in stages:
                    hi_of_x("k", "k_y011")
                if "h" in stages:
                    act.wait_ge(S["adj2_in"], 16 * made("h"))
                    if later("h"):
                        act.wait_ge(S["h_sum"], made("h") - 1)
                    act.activation(ex[:], adj2[:], ACT.Exp, scale=-1.0).then_inc(S["h_ex"], 1)
                if "h" in stages:
                    act.wait_ge(S["h_q0_made"], made("h"))
                    if later("h"):
                        act.wait_ge(S["h_S1o_made"], made("h") - 1)
                        act.wait_ge(S["h_S1e_made"], made("h") - 1)
                    copy(qT[:, 0:2], bank[BANK["h_q0"]][:].rearrange("p (m n) -> p m n", m=2)).then_inc(S["h_q0_read"], 1)
                if "a" in stages:
                    hi_of_x("a", "a_v")
                if "h" in stages:
                    act.wait_ge(S["h_q1_made"], made("h"))
                    copy(qT[:, 2:4], bank[BANK["h_q1"]][:].rearrange("p (m n) -> p m n", m=2)).then_inc(S["h_q1_read"], 1)
                if "k" in stages:
                    for g in range(G):
                        act.wait_ge(S[f"k_y2{g}_made"], made("k"))
                        if later("k"):
                            act.wait_ge(S[f"k_Ty{g}_made"], made("k") - 1)
                            act.wait_ge(S["k_sj_read"], made("k") - 1)
                        copy(ky2[:, g], bank[BANK[f"k_y2{g}"]][:, 0:D + 2]).then_inc(S[f"k_y2{g}_read"], 1)
                if "k" in stages:
                    act.wait_ge(S["k_leaky"], made("k"))
                    act.activation(kz[:], kl[:], ACT.Exp).then_inc(S["k_e"], 1)
                if "a" in stages:
                    act.wait_ge(S["a_G_made"], made("a"))
                    if later("a"):
                        act.wait_ge(S["a_S_made"], made("a") - 1)
                    for c in range(C):
                        act.activation(GT[0][:, c], bank[BANK["a_G"]][:, c * G * N:(c + 1) * G * N], ACT.Identity,
                                       bias=u_col[:, c:c + 1]).then_inc(S["a_Ghi"], 1)
                if "m" in stages:
                    act.wait_ge(S["m_nT_made"], made("m"))
                    if later("m"):
                        act.wait_ge(S["m_ag1_made"], made("m") - 1)
                        act.wait_ge(S["adjT_copy"], made("m") - 1)
                    copy(adjnT[:], bank[BANK["m_nT"]][:, 0:G * N].rearrange("p (g n) -> p g n", g=G)).then_inc(S["m_nT_read"], 1)
                if "h" in stages:
                    exps(0)
                    for g in range(G):
                        act.wait_ge(S[f"h_v{g}_made"], made("h"))
                        if later("h"):
                            act.wait_ge(S[f"h_PV{g}_made"], made("h") - 1)
                        copy(hv[:, g], bank[BANK[f"h_v{g}"]][:]).then_inc(S[f"h_v{g}_read"], 1)
                if "a" in stages:
                    act.wait_ge(S["a_S_made"], made("a"))
                    if later("a"):
                        act.wait_ge(S["a_p"], made("a") - 1)
                    act.activation(ae[:], bank[BANK["a_S"]][:, 0:G * N].rearrange("p (g n) -> p g n", g=G), ACT.Exp,
                                   bias=cq_col[:, 0:1]).then_inc(S["a_S_read"], 1)
                if "k" in stages:
                    act.wait_ge(S["k_T_made"], made("k"))
                    if later("k"):
                        act.wait_ge(S["k_TT1_made"], made("k") - 1)
                    copy(kT_[:], bank[BANK["k_T"]][:, 0:G * N].rearrange("p (g n) -> p g n", g=G)).then_inc(S["k_T_read"], 1)
                if "a" in stages:
                    act.wait_ge(S["a_v_made"], made("a"))
                    if later("a"):
                        act.wait_ge(S["a_PV1_made"], made("a") - 1)
                    copy(av[:, :, 0:D], bank[BANK["a_v"]][:].rearrange("p (g n) -> p g n", g=G)).then_inc(S["a_v_read"], 1)
                if "h" in stages:
                    exps(1)
                if "h" in stages:
                    copy_T(0)
                if "k" in stages:
                    for g in range(G):
                        act.wait_ge(S[f"k_Ty{g}_made"], made("k"))
                        if later("k"):
                            act.wait_ge(S[f"k_TT{g}_made"], made("k") - 1)
                        copy(ky1[:, g], bank[BANK[f"k_y01{g}"]][:, D:2 * D]).then_inc(S[f"k_Ty{g}_read"], 1)
                if "m" in stages:
                    hi_of_x("m", "m_xW1")
                if "h" in stages:
                    copy_T(1)
                    hi_of_o(0)
                    hi_of_o(1)
                if "m" in stages:
                    for g in range(G):
                        act.wait_ge(S[f"m_xW{g}_made"], made("m"))
                        if later("m"):
                            act.wait_ge(S[f"m_ag{g}_made"], made("m") - 1)
                        copy(my[:, g], bank[BANK[f"m_xW{g}"]][:, D:2 * D]).then_inc(S[f"m_xW{g}_read"], 1)

            for t in range(4):
                step(t, stages_at(t))
            with act.Fori(4, pairs) as t:
                step(t, "mahk")
            for t in range(pairs, steps):
                step(t, stages_at(t))

        @block.vector
        def _(dve):
            def gate():
                dve.sem_inc(S["gate"], 1)

            def as_f32(t):
                return t.bitcast(F32)

            dve.wait_ge(S["setup_in"], 16 * n_setup_loads)
            dve.tensor_tensor(bk3_bc[:], bk3_in[:, 0], bk3_in[:, 1], ALU.add).then_inc(S["setup_sum"], 1)
            dve.wait_ge(S["setup_sum"], 1)
            dve.tensor_tensor(bk3_bc[:], bk3_bc[:], bk3_in[:, 2], ALU.add).then_inc(S["setup_sum"], 1)
            dve.wait_ge(S["setup_mm"], 1)
            dve.tensor_copy(u_col[:], bank[2][:, 0:C]).then_inc(S["setup_ev"], 1)
            dve.tensor_copy(cq_col[:], bank[2][:, 2 * C:2 * C + 1]).then_inc(S["setup_ev"], 1)
            dve.tensor_scalar(ke_col[:], bank[2][:, 2 * C + 1:2 * C + 2], kab_col[:, 0:1], None, ALU.add).then_inc(S["setup_ev"], 1)
            dve.wait_ge(S["setup_ev"], 3)
            dve.tensor_copy(kden[:, 0:1], ke_col[:]).then_inc(S["setup_ev"], 1)
            dve.wait_ge(S["setup_hi"], 9)
            def lo(pair, src, *index):
                return dve.tensor_tensor(pair[1][index], src, as_f32(pair[0][index]), ALU.subtract)
            every = slice(None)
            for pair, src in ((Wm, wm_in), (Wv, wv_in), (Wqkv, wqkv_in)):
                lo(pair, src, every).then_inc(S["setup_lo"], 1)
            dve.scalar_tensor_tensor(out=Wo[1][:], in0=wo_in, scalar=LA, in1=as_f32(Wo[0][:]), op0=ALU.mult,
                                     op1=ALU.subtract).then_inc(S["setup_lo"], 1)
            lo(Wy01, wk3_in[:, 0], every, every, slice(0, D))
            lo(Wy01, wk3_in[:, 1], every, every, slice(D, 2 * D))
            lo(A, bank[0][:].rearrange("p (c n) -> p c n", c=C), every).then_inc(S["setup_lo"], 1)
            lo(Wrow, bank[1][:, 0:D].rearrange("p (c n) -> p c n", c=C), every).then_inc(S["setup_lo"], 1)
            lo(Wsj, bank[1][:, D:2 * D].rearrange("p (c n) -> p c n", c=C), every).then_inc(S["setup_lo"], 1)
            lo(Wy2, wk3_in[:, 2], every, every, slice(0, D)).then_inc(S["setup_lo"], 1)
            for i in range(2):
                last = lo(Wy2, bank[2][:, C:2 * C].unsqueeze(2), every, every, slice(D + i, D + i + 1))
            last.then_inc(S["setup_lo"], 1)

            def step(t, stages):
                def made(s):
                    return t - STAGE[s] + 1

                def later(s):
                    return had(t, s)

                def lo_of_x(s):
                    dve.wait_ge(S[s + "_xhi"], made(s))
                    dve.tensor_tensor(xT[s][1][:], bank[BANK[s + "_xT"]][:].rearrange("p (c n) -> p c n", c=C),
                                      as_f32(xT[s][0][:]), ALU.subtract).then_inc(S[s + "_xT_read"], 1)

                def normalize(s, dst, signal):
                    for g in range(G):
                        dve.tensor_scalar(dst[:, g], hh[s][:, g], mv[s][:, g, 0:1], rstd[s][:, g:g + 1],
                                          ALU.subtract, ALU.mult).then_inc(S[signal], 1)

                def heads_max(g):
                    dve.wait_ge(S["h_mneg"], made("h"))
                    if later("h"):
                        dve.wait_ge(S[f"h_T{g}o_made"], made("h") - 1)
                        dve.wait_ge(S[f"h_nmx{g}"], made("h") - 1)
                    for odd, half in enumerate("eo"):
                        dve.wait_ge(S[f"h_S{g}{half}_made"], made("h"))
                        gate()
                        for m in range(4):
                            h = 4 * odd + m
                            last = dve.tensor_tensor_reduce(hs[:, g, h], bank[BANK[f"h_S{g}{half}"]][:, m * N:(m + 1) * N],
                                                            mneg[:, g], 1.0, -BIG, ALU.add, ALU.max, hmx[:, g, h:h + 1])
                        last.then_inc(S[f"h_S{g}{half}_read"], 1)
                    dve.wait_ge(S[f"h_S{g}o_read"], made("h"))
                    dve.tensor_scalar(hnmx[:, g], hmx[:, g], -(DH ** -0.5), None, ALU.mult).then_inc(S[f"h_nmx{g}"], 1)

                def heads_mix(g):
                    dve.wait_ge(S[f"h_e{g}"], HEADS * made("h"))
                    dve.reciprocal(hr[:, g], hden[:, g]).then_inc(S["h_r"], 1)
                    dve.wait_ge(S["h_r"], 2 * (made("h") - 1) + g + 1)
                    dve.wait_ge(S["h_mix"], made("h"))
                    for h in range(HEADS):
                        last = dve.scalar_tensor_tensor(out=hs[:, g, h], in0=hs[:, g, h], scalar=hr[:, g, h:h + 1],
                                                        in1=mix[:, g], op0=ALU.mult, op1=ALU.add)
                    last.then_inc(S[f"h_p{g}"], 1)

                def lo_of_o(g):
                    dve.wait_ge(S[f"h_ohi{g}"], made("h"))
                    dve.tensor_tensor(oT[1][:, g], bank[BANK[f"h_PV{g}"]][:].rearrange("p (m n) -> p m n", m=4),
                                      as_f32(oT[0][:, g]), ALU.subtract).then_inc(S[f"h_PV{g}_read"], 1)

                def hops_sum(g):
                    dve.wait_ge(S["x3_copy"], made("k"))
                    dve.wait_ge(S[f"k_TT{g}_made"], made("k"))
                    dve.tensor_tensor(ksum[:, g], bank[BANK[f"k_y01{g}"]][:, 0:D], bk3_bc[:], ALU.add).then_inc(S[f"k_TT{g}_read"], 1)
                    dve.wait_ge(S[f"k_TT{g}_read"], made("k"))
                    dve.scalar_tensor_tensor(out=hh["k"][:, g], in0=ksum[:, g], scalar=0.0, in1=x3c[:, g],
                                             op0=ALU.max, op1=ALU.add).then_inc(S["k_sum"], 1)
                    dve.wait_ge(S["k_sum"], 2 * (made("k") - 1) + g + 1)
                    dve.bn_stats(stats["k"][:, g], hh["k"][:, g]).then_inc(S["k_h"], 1)
                    dve.wait_ge(S["k_h"], 2 * (made("k") - 1) + g + 1)
                    gate()
                    dve.bn_aggr(mv["k"][:, g], stats["k"][:, g]).then_inc(S["k_mv"], 1)

                if "h" in stages:
                    lo_of_x("h")
                if "k" in stages:
                    lo_of_x("k")
                if "a" in stages:
                    dve.wait_ge(S["m_rstd"], made("a"))
                    if later("a"):
                        dve.wait_ge(S["a_xT_made"], made("a") - 1)
                        dve.wait_ge(S["x1_bias"], made("a") - 1)
                    normalize("m", x1, "x1_made")
                if "m" in stages:
                    dve.wait_ge(S["adj0_in"], 16 * made("m"))
                    dve.tensor_reduce(deg[:], adj0[:], AX.X, ALU.add).then_inc(S["m_deg"], 1)
                    dve.wait_ge(S["m_deg"], 3 * (made("m") - 1) + 1)
                    dve.tensor_scalar(degmax[:], deg[:], EPS_DEG, None, ALU.max).then_inc(S["m_deg"], 1)
                    dve.wait_ge(S["m_deg"], 3 * (made("m") - 1) + 2)
                    dve.reciprocal(rdeg[:], degmax[:]).then_inc(S["m_deg"], 1)
                    dve.wait_ge(S["m_deg"], 3 * made("m"))
                    if later("m"):
                        dve.wait_ge(S["m_nT_made"], made("m") - 1)
                    for g in range(G):
                        last = dve.tensor_scalar(adjn[:, g], adj0[:, g], rdeg[:, g:g + 1], None, ALU.mult)
                    last.then_inc(S["m_adjn"], 1)
                if "h" in stages:
                    dve.wait_ge(S["h_k0_made"], made("h"))
                    if later("h"):
                        dve.wait_ge(S["h_S1o_made"], made("h") - 1)
                        dve.wait_ge(S["h_S1e_made"], made("h") - 1)
                    dve.tensor_copy(kT[:, 0:2], bank[BANK["h_k0"]][:].rearrange("p (m n) -> p m n", m=2)).then_inc(S["h_k0_read"], 1)
                if "a" in stages:
                    lo_of_x("a")
                if "h" in stages:
                    dve.wait_ge(S["h_k1_made"], made("h"))
                    dve.tensor_copy(kT[:, 2:4], bank[BANK["h_k1"]][:].rearrange("p (m n) -> p m n", m=2)).then_inc(S["h_k1_read"], 1)
                if "k" in stages:
                    dve.wait_ge(S["k_sj_made"], made("k"))
                    if later("k"):
                        dve.wait_ge(S["k_w"], 2 * (made("k") - 1))
                    for g in range(G):
                        dve.wait_ge(S[f"k_y2{g}_read"], made("k"))
                        last = dve.tensor_scalar(kw[:, g], bank[BANK["k_sj"]][:, g * N:(g + 1) * N], ky2[:, g, D:D + 1],
                                                 ke_col[:, 0:1], ALU.add, ALU.add)
                    last.then_inc(S["k_sj_read"], 1)
                    dve.wait_ge(S["k_sj_read"], made("k"))
                    if later("k"):
                        dve.wait_ge(S["k_e"], made("k") - 1)
                    dve.scalar_tensor_tensor(out=kl[:], in0=kw[:], scalar=SLOPE, in1=kw[:], op0=ALU.mult,
                                             op1=ALU.max).then_inc(S["k_leaky"], 1)
                if "a" in stages:
                    dve.wait_ge(S["a_Ghi"], C * made("a"))
                    for c in range(C):
                        last = dve.scalar_tensor_tensor(out=GT[1][:, c], in0=bank[BANK["a_G"]][:, c * G * N:(c + 1) * G * N],
                                                        scalar=u_col[:, c:c + 1], in1=as_f32(GT[0][:, c]), op0=ALU.add,
                                                        op1=ALU.subtract)
                    last.then_inc(S["a_G_read"], 1)
                if "k" in stages:
                    dve.wait_ge(S["k_e"], made("k"))
                    dve.wait_ge(S["adj3_in"], 16 * made("k"))
                    gate()
                    for g in range(G):
                        dve.tensor_tensor_reduce(kw[:, g], kz[:, g], adj3[:, g], 1.0, 0.0, ALU.mult, ALU.add,
                                                 kden[:, g:g + 1]).then_inc(S["k_w"], 1)
                    dve.wait_ge(S["k_w"], 2 * made("k"))
                    dve.tensor_scalar(kden2[:], kden[:], EPS_ROW, None, ALU.add).then_inc(S["k_den"], 1)
                    dve.wait_ge(S["k_den"], 2 * made("k") - 1)
                    dve.reciprocal(krden[:], kden2[:]).then_inc(S["k_den"], 1)
                    dve.wait_ge(S["k_den"], 2 * made("k"))
                    if later("k"):
                        dve.wait_ge(S["k_T_made"], made("k") - 1)
                    for g in range(G):
                        dve.tensor_scalar(kt[:, g], kw[:, g], krden[:, g:g + 1], None, ALU.mult).then_inc(S["k_tr"], 1)
                if "h" in stages:
                    heads_max(0)
                if "h" in stages:
                    heads_mix(0)
                if "a" in stages:
                    dve.wait_ge(S["a_S_read"], made("a"))
                    dve.wait_ge(S["adjT_copy"], made("a"))
                    if later("a"):
                        dve.wait_ge(S["a_PV1_made"], made("a") - 1)
                    dve.tensor_tensor(ap[:], ae[:], adjT[:], ALU.mult).then_inc(S["a_p"], 1)
                if "h" in stages:
                    heads_max(1)
                if "h" in stages:
                    heads_mix(1)
                if "a" in stages:
                    dve.wait_ge(S["x1_bias"], made("a"))
                    for g in range(G):
                        dve.wait_ge(S[f"a_PV{g}_made"], made("a"))
                        dve.reciprocal(arden[:, g:g + 1], bank[BANK[f"a_PV{g}"]][:, D:D + 1]).then_inc(S["a_rden"], 1)
                        dve.wait_ge(S["a_rden"], 2 * (made("a") - 1) + g + 1)
                        dve.scalar_tensor_tensor(out=hh["a"][:, g], in0=bank[BANK[f"a_PV{g}"]][:, 0:D],
                                                 scalar=arden[:, g:g + 1], in1=x1b[:, g], op0=ALU.mult,
                                                 op1=ALU.add).then_inc(S[f"a_PV{g}_read"], 1)
                        dve.wait_ge(S[f"a_PV{g}_read"], made("a"))
                        dve.bn_stats(stats["a"][:, g], hh["a"][:, g]).then_inc(S["a_h"], 1)
                        dve.wait_ge(S["a_h"], 2 * (made("a") - 1) + g + 1)
                        gate()
                        dve.bn_aggr(mv["a"][:, g], stats["a"][:, g]).then_inc(S["a_mv"], 1)
                if "m" in stages:
                    lo_of_x("m")
                if "a" in stages:
                    if "h" in stages:
                        dve.wait_ge(S["h_xT_made"], made("h"))
                        dve.wait_ge(S["x2_bias"], made("h"))
                    dve.wait_ge(S["a_rstd"], made("a"))
                    normalize("a", x2, "x2_made")
                if "h" in stages:
                    lo_of_o(0)
                if "k" in stages:
                    hops_sum(0)
                if "h" in stages:
                    lo_of_o(1)
                if "k" in stages:
                    hops_sum(1)
                if "h" in stages:
                    dve.wait_ge(S["x2_bias"], made("h"))
                    dve.wait_ge(S["h_out_made"], made("h"))
                    dve.tensor_tensor(hh["h"][:], bank[BANK["h_out"]][:].rearrange("p (g n) -> p g n", g=G), x2b[:],
                                      ALU.add).then_inc(S["h_out_read"], 1)
                    dve.wait_ge(S["h_out_read"], made("h"))
                    for g in range(G):
                        last = dve.bn_stats(stats["h"][:, g], hh["h"][:, g])
                    last.then_inc(S["h_h"], 1)
                    dve.wait_ge(S["h_h"], made("h"))
                    gate()
                    for g in range(G):
                        dve.bn_aggr(mv["h"][:, g], stats["h"][:, g]).then_inc(S["h_mv"], 1)
                if "k" in stages:
                    if later("k"):
                        dve.wait_ge(S["y_out"], 16 * (made("k") - 1))
                    dve.wait_ge(S["k_rstd"], made("k"))
                    for g in range(G):
                        last = dve.tensor_scalar(y[:, g], hh["k"][:, g], mv["k"][:, g, 0:1], rstd["k"][:, g:g + 1],
                                                 ALU.subtract, ALU.mult)
                    last.then_inc(S["y_made"], 1)
                if "h" in stages:
                    dve.wait_ge(S["h_rstd"], made("h"))
                    if "k" in stages:
                        dve.wait_ge(S["k_xT_made"], made("k"))
                        dve.wait_ge(S["x3_copy"], made("k"))
                    normalize("h", x3, "x3_made")
                if "m" in stages:
                    dve.wait_ge(S["x0_copy"], made("m"))
                    for g in range(G):
                        dve.wait_ge(S[f"m_ag{g}_made"], made("m"))
                        dve.scalar_tensor_tensor(out=hh["m"][:, g], in0=bank[BANK[f"m_xW{g}"]][:, 0:D], scalar=0.0,
                                                 in1=x0c[:, g], op0=ALU.max, op1=ALU.add).then_inc(S[f"m_ag{g}_read"], 1)
                        dve.wait_ge(S[f"m_ag{g}_read"], made("m"))
                        dve.bn_stats(stats["m"][:, g], hh["m"][:, g]).then_inc(S["m_h"], 1)
                        dve.wait_ge(S["m_h"], 2 * (made("m") - 1) + g + 1)
                        gate()
                        dve.bn_aggr(mv["m"][:, g], stats["m"][:, g]).then_inc(S["m_mv"], 1)

            for t in range(4):
                step(t, stages_at(t))
            with dve.Fori(4, pairs) as t:
                step(t, "mahk")
            for t in range(pairs, steps):
                step(t, stages_at(t))


ARGS = ["x", "adj", "nodemask", "nodemask_T", "L0_gnn_W", "L1_gnn_Wq_w", "L1_gnn_Wk_w", "L1_gnn_Wv_w", "L1_gnn_Wv_b",
        "columns", "L2_gnn_W_qkv", "L2_gnn_W_out", "L2_gnn_b_out", "L3_gnn_Wv", "L3_gnn_ab", "L3_gnn_Wk", "L3_gnn_bk"]


def kernel(**inputs):
    import concourse.bacc as bacc
    from concourse.bass_utils import run_bass_kernel_spmd

    a = {n: np.asarray(v) for n, v in inputs.items()}
    a["nodemask"] = a["nodemask"].view(np.uint8)
    a["nodemask_T"] = a["nodemask"].T
    aw = a["L3_gnn_aw"][:, 0]
    vectors = (a["L1_gnn_Wq_b"], a["L1_gnn_Wk_b"], a["L3_gnn_bv"], aw[:D], aw[D:])
    a["columns"] = np.stack([v.reshape(C, 128) for v in vectors]).transpose(2, 0, 1)
    w = a["L0_gnn_W"]
    a["L0_gnn_W"] = np.concatenate([w[:, :D].T, w[:, D:].T], axis=1)
    a["L1_gnn_Wv_w"] = a["L1_gnn_Wv_w"].T
    a["L3_gnn_Wv"] = a["L3_gnn_Wv"].T
    a["L2_gnn_W_qkv"] = a["L2_gnn_W_qkv"].reshape(D, HEADS, 3, DH).transpose(0, 2, 1, 3).reshape(D, 3 * INNER)

    nc = bacc.Bacc("TRN2", target_bir_lowering=False, num_devices=1)
    arrays, args = {}, []
    for n in ARGS:
        arrays[f"in_{n}"] = np.ascontiguousarray(a[n])
        args.append(nc.dram_tensor(f"in_{n}", a[n].shape, mybir.dt.from_np(a[n].dtype), kind="ExternalInput").ap())
    out = nc.dram_tensor("out_0", a["x"].shape, F32, kind="ExternalOutput").ap()
    build(nc, *args, out)
    return run_bass_kernel_spmd(nc, [arrays], core_ids=[0]).results[0]["out_0"]
```

```python
from contextlib import ExitStack

import numpy as np

import concourse.bass as bass
from concourse import mybir

F32 = mybir.dt.float32
F32R = mybir.dt.float32r
U8 = mybir.dt.uint8
ALU = mybir.AluOpType
ACT = mybir.ActivationFunctionType
AX = mybir.AxisListType

N = 128
D = 256
C = D // 128
G = 2
HEADS, DH = 8, 64
INNER = HEADS * DH
HOPS = 3
LA = LD = LG = 0.33
EPS_DEG, EPS_LN, EPS_ROW = 1e-6, 1e-5, 1e-12
BIG = float(np.finfo(np.float32).max)
SLOPE = 0.2
STAGE = {"m": 0, "a": 1, "h": 2, "k": 3}

PRODUCTS = [
    ("h_k0", 0), ("h_q0", 3), ("h_k1", 0), ("h_q1", 5), ("h_v0", 0), ("k_xT", 1), ("h_S0e", 5), ("h_S0o", 3),
    ("h_v1", 4), ("a_xT", 7), ("h_S1e", 1), ("h_S1o", 2), ("k_y20", 5), ("k_y21", 0), ("a_G", 3), ("k_y010", 4),
    ("a_v", 2), ("k_sj", 6), ("h_T0e", 5), ("a_S", 3), ("k_y011", 0), ("m_xW0", 6), ("h_T0o", 3), ("a_PV0", 5),
    ("a_PV1", 1), ("h_T1e", 2), ("h_T1o", 3), ("h_PV0", 7), ("m_xW1", 2), ("k_T", 3), ("h_PV1", 5), ("h_out", 7),
    ("a_x2T", 3),
]
BANK = dict(PRODUCTS)
LAST_READ = {"m_xW0": "m_ag0", "m_xW1": "m_ag1", "k_y010": "k_TT0", "k_y011": "k_TT1"}

READS = [n for n, _ in PRODUCTS] + ["m_ag0", "m_ag1", "k_Ty0", "k_Ty1", "k_TT0", "k_TT1"]
OTHER = """x0_in x0T_in adj0_in adj0T_in adj1T_in adj2_in adj3_in mrow_in mcol_in y_out
a_x2hi m_xhi m_xlo a_xhi a_xlo k_xhi h_ohi0 h_ohi1
m_deg m_sum m_h m_mv m_ve m_rstd x1_made
a_p a_rden a_h a_mv a_ve a_rstd x2_made x1_bias
h_mrow h_m2 h_mneg h_ex h_sum h_mix h_nmx0 h_nmx1 h_e0 h_e1 h_r0 h_r1 h_p0 h_p1
h_h h_mv h_ve h_rstd x3_made x2_bias
k_leaky k_e k_w k_den k_tr k_sum k_h k_mv k_ve k_rstd y_made
ident halves setup_in setup_sum setup_mm setup_ev setup_hi setup_lo setup_c gate""".split()


def former(product, stages, before):
    names = [n for n, _ in PRODUCTS]
    i = names.index(product)
    for n in reversed(names[:i]):
        if BANK[n] == BANK[product] and n[0] in stages:
            return n, 0
    for n in reversed(names):
        if before and BANK[n] == BANK[product] and n[0] in before:
            return n, 1
    return None, 0


def build(nc, x, xt, adj, adjt, mask, maskT, wm, wq, wk, wvT, bv, columns, wqkv, wout, bout, wkvT, kab, wk3, bk3, out):
    pairs = x.shape[0] // G
    steps = pairs + len(STAGE) - 1

    def stages_at(t):
        return "".join(s for s, n in STAGE.items() if 0 <= t - n < pairs)

    with ExitStack() as ctx:
        def sb(name, *shape, dt=F32):
            return ctx.enter_context(nc.sbuf_tensor(name, [128, *shape], dt))

        S = {}
        for n in READS:
            S[n + "_made"] = ctx.enter_context(nc.semaphore(n + "_made"))
            S[n + "_read"] = ctx.enter_context(nc.semaphore(n + "_read"))
        for n in OTHER:
            S[n] = ctx.enter_context(nc.semaphore(n))
        bank = [ctx.enter_context(nc.psum_tensor(f"bank{b}", [128, 512], F32)) for b in range(8)]

        def parts(name, *shape):
            return sb(name + "_hi", *shape, dt=F32R), sb(name + "_lo", *shape, dt=F32R)

        Wm = parts("Wm", C, 2 * D)
        A = parts("A", C, D)
        Wrow = parts("Wrow", C, 128)
        Wv = parts("Wv", C, D)
        Wqkv = parts("Wqkv", C, 3, INNER)
        Wo = parts("Wo", INNER // 128, D)
        Wy2 = parts("Wy2", C, D + 2)
        Wy01 = parts("Wy01", C, 2 * D)
        Wsj = parts("Wsj", C, 128)

        ident = sb("identity", 128)
        minus_half = sb("minus_half", G)
        u_col = sb("u_col", C)
        cq_col = sb("cq_col", 1)
        ke_col = sb("ke_col", 1)
        kab_col = sb("kab_col", 1)
        vec_in = sb("vec_in", 5, C)
        bv_bc = sb("bv_bc", D)
        bout_bc = sb("bout_bc", D)
        bk3_in = sb("bk3_in", HOPS, D)
        bk3_bc = sb("bk3_bc", D)

        x0, x1, x1b, x2, x2b, x3 = (sb(n, G, D) for n in "x0 x1 x1b x2 x2b x3".split())
        hh = {s: sb("h_" + s, G, D) for s in "mahk"}
        stats = {s: sb("stats_" + s, G, 6) for s in "mahk"}
        mv = {s: sb("mv_" + s, G, 2) for s in "mahk"}
        ve = {s: sb("ve_" + s, G) for s in "mahk"}
        rstd = {s: sb("rstd_" + s, G) for s in "mahk"}
        xT = {s: parts("xT_" + s, C, G * N) for s in "mahk"}
        x0T, x1T = sb("x0T", C, G * N), sb("x1T", C, G * N)
        adj0, adj0T, adj1T, adj2, adj3 = (sb(n, G, N) for n in "adj0 adj0T adj1T adj2 adj3".split())
        deg, degmax, rdeg = sb("deg", G), sb("degmax", G), sb("rdeg", G)
        msum, my = sb("msum", G, D), sb("my", G, 2 * D)
        GT = sb("GT", C, G * N)
        ae, ap = sb("ae", G, N), sb("ap", G, N)
        av = sb("av", G, D + 1)
        arden = sb("arden", G)
        mrow8, mcol8 = sb("mrow8", G, N, dt=U8), sb("mcol8", G, dt=U8)
        mrow, mcol = sb("mrow", G, N), sb("mcol", G)
        m2, mneg, ex, exs, mix = (sb(n, G, N) for n in "m2 mneg ex exs mix".split())
        hmx, hnmx, hden, hr = (sb(n, G, HEADS) for n in "hmx hnmx hden hr".split())
        work = sb("work", 7168)
        qT = work[:, 0:1024].rearrange("p (m n) -> p m n", m=4)
        kT = work[:, 1024:2048].rearrange("p (m n) -> p m n", m=4)
        hv = work[:, 2048:3072].rearrange("p (g f) -> p g f", g=G)
        hs = work[:, 3072:5120].rearrange("p (g h n) -> p g h n", g=G, h=HEADS)
        pT = work[:, 5120:7168].rearrange("p (g h n) -> p g h n", g=G, h=HEADS)
        oT = parts("oT", G, INNER // 128, N)
        ky2 = sb("ky2", G, D + 2)
        ky1 = sb("ky1", G, D)
        kz, kl, kw, kt, kT_ = (sb(n, G, N) for n in "kz kl kw ktr kT_".split())
        kden, kden2, krden = sb("kden", G), sb("kden2", G), sb("krden", G)
        ksum = sb("ksum", G, D)
        y = sb("y", G, D)
        stage3 = sb("stage3", 1536)

        wm_in = work[:, 0:1024].rearrange("p (c n) -> p c n", c=C)
        wq_in = work[:, 1024:1536].rearrange("p (c n) -> p c n", c=C)
        wk_in = work[:, 1536:2048].rearrange("p (c n) -> p c n", c=C)
        wv_in = work[:, 2048:2560].rearrange("p (c n) -> p c n", c=C)
        wkv_in = work[:, 2560:3072].rearrange("p (c n) -> p c n", c=C)
        wqkv_in = work[:, 3072:6144].rearrange("p (c i n) -> p c i n", c=C, i=3)
        wo_in = work[:, 6144:7168].rearrange("p (c n) -> p c n", c=4)
        wk3_in = stage3[:, :].rearrange("p (k c n) -> p k c n", k=HOPS, c=C)
        bq_in, bk_in, kbv_in, awj_in, awi_in = (vec_in[:, i].unsqueeze(2) for i in range(5))

        xg = x.rearrange("(p g) n f -> p n g f", g=G)
        og = out.rearrange("(p g) n f -> p n g f", g=G)
        mrowg = mask.rearrange("(p g) n -> p (g n)", g=G)
        mcolg = maskT.rearrange("n (p g) -> p n g", g=G)

        every = slice(None)

        def as_f32(t):
            return t.bitcast(F32)

        def chunks(t):
            return t[:].rearrange("p (c n) -> p c n", c=2)

        def by_four(t):
            return t[:].rearrange("p (m n) -> p m n", m=4)

        def had(t, stage):
            return not isinstance(t, int) or t > STAGE[stage]

        block = ctx.enter_context(nc.Block())

        @block.sync
        def _(sp):
            def load_x0(p):
                sp.dma_start(x0[:], xg[p]).then_inc(S["x0_in"], 16)

            def load_x0T(p):
                sp.dma_start(x0T[:].rearrange("p c n -> p (c n)"), xt[p]).then_inc(S["x0T_in"], 16)

            def load_adj(tile, name, p, array=adj):
                sp.dma_start(tile[:].rearrange("p g n -> p (g n)"), array[p]).then_inc(S[name], 16)

            def load_mask(p):
                sp.dma_start(mrow8[:], mrowg[p].unsqueeze(0).broadcast_to([128, G * N]).rearrange("q (g n) -> q g n", g=G)).then_inc(S["mrow_in"], 16)
                sp.dma_start(mcol8[:], mcolg[p]).then_inc(S["mcol_in"], 16)

            def weight(dst, src):
                sp.dma_start(dst, src).then_inc(S["setup_in"], 16)

            load_x0T(0)
            load_adj(adj0, "adj0_in", 0)
            load_adj(adj0T, "adj0T_in", 0, adjt)
            load_x0(0)
            for src, dst in ((wm, wm_in), (wq, wq_in), (wk, wk_in)):
                weight(dst, src.rearrange("(c p) n -> p c n", p=128))
            weight(vec_in[:], columns)
            weight(kab_col[:], kab.unsqueeze(0).broadcast_to([128, 1]))
            for src, dst in ((wkvT, wkv_in), (wvT, wv_in), (wout, wo_in)):
                weight(dst, src.rearrange("(c p) n -> p c n", p=128))
            weight(wqkv_in, wqkv.rearrange("(c p) (i n) -> p c i n", p=128, i=3))
            for k in range(HOPS):
                weight(wk3_in[:, k], wk3[k].rearrange("(c p) n -> p c n", p=128))
                weight(bk3_in[:, k], bk3[k:k + 1, :].broadcast_to([128, D]))
            weight(bv_bc[:], bv.unsqueeze(0).broadcast_to([128, D]))
            weight(bout_bc[:], bout.unsqueeze(0).broadcast_to([128, D]))
            load_adj(adj1T, "adj1T_in", 0, adjt)
            load_adj(adj2, "adj2_in", 0)
            load_mask(0)
            load_adj(adj3, "adj3_in", 0)

            def gate():
                sp.sem_inc(S["gate"], 1)

            def step(t, stages, more):
                if "m" in stages and "m" in more:
                    sp.wait_ge(S["m_deg"], 3 * t + 1)
                    gate()
                    load_adj(adj0, "adj0_in", t + 1)
                if "h" in stages and "h" in more:
                    p = t - 2
                    sp.wait_ge(S["h_mrow"], 2 * (p + 1))
                    gate()
                    load_mask(p + 1)
                    sp.wait_ge(S["h_ex"], p + 1)
                    gate()
                    sp.wait_ge(S["h_sum"], p + 1)
                    gate()
                    load_adj(adj2, "adj2_in", p + 1)
                if "m" in stages and "m" in more:
                    sp.wait_ge(S["m_xhi"], t + 1)
                    gate()
                    sp.wait_ge(S["m_xlo"], t + 1)
                    gate()
                    load_x0T(t + 1)
                if "k" in stages and "k" in more:
                    p = t - 3
                    sp.wait_ge(S["k_w"], 2 * (p + 1))
                    gate()
                    load_adj(adj3, "adj3_in", p + 1)
                if "a" in stages and "a" in more:
                    p = t - 1
                    sp.wait_ge(S["a_p"], p + 1)
                    gate()
                    load_adj(adj1T, "adj1T_in", p + 1, adjt)
                if "m" in stages and "m" in more:
                    sp.wait_ge(S["m_ag1_made"], t + 1)
                    gate()
                    load_adj(adj0T, "adj0T_in", t + 1, adjt)
                    sp.wait_ge(S["m_sum"], 2 * (t + 1))
                    gate()
                    load_x0(t + 1)
                if "k" in stages:
                    p = t - 3
                    sp.wait_ge(S["y_made"], 2 * (p + 1))
                    gate()
                    sp.dma_start(og[p], y[:]).then_inc(S["y_out"], 16)

            for t in range(4):
                step(t, stages_at(t), "mahk")
            with sp.Fori(4, pairs - 1) as t:
                step(t, "mahk", "mahk")
            for t in range(pairs - 1, steps):
                more = "".join(s for s, n in STAGE.items() if t + 1 - n < pairs)
                step(t, stages_at(t), more)
            sp.wait_ge(S["y_out"], 16 * pairs)

        n_setup_loads = 3 + 1 + 1 + 3 + 1 + 2 * HOPS + 2

        @block.gpsimd
        def _(pool):
            pool.memset(ident[:], 0.0).then_inc(S["ident"], 1)
            pool.memset(minus_half[:], -0.5).then_inc(S["halves"], 1)
            pool.memset(av[:], 1.0).then_inc(S["halves"], 1)
            pool.wait_ge(S["ident"], 1)
            pool.affine_select(out=ident[:], in_=ident[:], compare_op=ALU.not_equal, fill=1.0, base=0,
                               pattern=[[-1, 128]], channel_multiplier=1).then_inc(S["ident"], 1)
            pool.wait_ge(S["halves"], 2)
            pool.wait_ge(S["setup_in"], 16 * n_setup_loads)

            def gate():
                pool.sem_inc(S["gate"], 1)

            def inv_std(s, n):
                pool.wait_ge(S[s + "_mv"], 2 * n)
                gate()
                pool.tensor_scalar(ve[s][:], mv[s][:, :, 1], EPS_LN, None, ALU.add).then_inc(S[s + "_ve"], 1)
                pool.wait_ge(S[s + "_ve"], n)
                pool.tensor_tensor(rstd[s][:], ve[s][:], minus_half[:], ALU.pow).then_inc(S[s + "_rstd"], 1)

            def step(t, stages):
                def made(s):
                    return t - STAGE[s] + 1

                def later(s):
                    return had(t, s)

                if "h" in stages:
                    pool.wait_ge(S["mrow_in"], 16 * made("h"))
                    pool.wait_ge(S["mcol_in"], 16 * made("h"))
                    if later("h"):
                        pool.wait_ge(S["h_mix"], made("h") - 1)
                        pool.wait_ge(S["h_mneg"], made("h") - 1)
                    gate()
                    pool.tensor_copy(mrow[:], mrow8[:]).then_inc(S["h_mrow"], 1)
                    pool.tensor_copy(mcol[:], mcol8[:]).then_inc(S["h_mrow"], 1)
                    pool.wait_ge(S["h_mrow"], 2 * made("h"))
                    gate()
                    for g in range(G):
                        pool.tensor_scalar(m2[:, g], mrow[:, g], mcol[:, g:g + 1], None, ALU.mult).then_inc(S["h_m2"], 1)
                if "a" in stages:
                    inv_std("m", made("a"))
                if "h" in stages:
                    pool.wait_ge(S["h_m2"], 2 * made("h"))
                    if later("h"):
                        pool.wait_ge(S["h_S1o_read"], made("h") - 1)
                    gate()
                    pool.tensor_scalar(mneg[:], m2[:], BIG, BIG, ALU.mult, ALU.subtract).then_inc(S["h_mneg"], 1)
                if "a" in stages:
                    pool.wait_ge(S["x1_made"], 2 * made("a"))
                    if later("a"):
                        pool.wait_ge(S["a_h"], 2 * (made("a") - 1))
                    pool.tensor_tensor(x1b[:], x1[:], bv_bc[:].unsqueeze(1).broadcast_to([128, G, D]), ALU.add).then_inc(S["x1_bias"], 1)
                if "m" in stages:
                    pool.wait_ge(S["m_xhi"], made("m"))
                    pool.tensor_tensor(xT["m"][1][:], x0T[:], as_f32(xT["m"][0][:]), ALU.subtract).then_inc(S["m_xlo"], 1)
                if "h" in stages:
                    pool.wait_ge(S["h_ex"], made("h"))
                    if later("h"):
                        pool.wait_ge(S["h_mix"], made("h") - 1)
                    pool.tensor_tensor(exs[:], ex[:], adj2[:], ALU.add).then_inc(S["h_sum"], 1)
                    pool.wait_ge(S["h_sum"], made("h"))
                    pool.wait_ge(S["h_m2"], 2 * made("h"))
                    if later("h"):
                        pool.wait_ge(S["h_p1"], 2 * (made("h") - 1))
                    pool.tensor_tensor(mix[:], exs[:], m2[:], ALU.mult).then_inc(S["h_mix"], 1)
                    pool.wait_ge(S["x2_made"], 2 * made("h"))
                    if later("h"):
                        pool.wait_ge(S["h_h"], 2 * (made("h") - 1))
                    pool.tensor_tensor(x2b[:], x2[:], bout_bc[:].unsqueeze(1).broadcast_to([128, G, D]), ALU.add).then_inc(S["x2_bias"], 1)
                if "a" in stages:
                    pool.wait_ge(S["a_S_read"], made("a"))
                    pool.wait_ge(S["adj1T_in"], 16 * made("a"))
                    if later("a"):
                        pool.wait_ge(S["a_PV1_made"], made("a") - 1)
                    pool.tensor_tensor(ap[:], ae[:], adj1T[:], ALU.mult).then_inc(S["a_p"], 1)
                    inv_std("a", made("a"))
                if "k" in stages:
                    inv_std("k", made("k"))
                if "h" in stages:
                    inv_std("h", made("h"))

            for t in range(4):
                step(t, stages_at(t))
            with pool.Fori(4, pairs) as t:
                step(t, "mahk")
            for t in range(pairs, steps):
                step(t, stages_at(t))

        @block.tensor
        def _(pe):
            def product3(o, lhs, rhs, first=True, last=True, skip=False):
                pe.matmul(o, lhs[0], rhs[0], start=first, stop=False, skip_group_check=skip)
                pe.matmul(o, lhs[0], rhs[1], start=False, stop=False, skip_group_check=skip)
                return pe.matmul(o, lhs[1], rhs[0], start=False, stop=last, skip_group_check=skip)

            pe.wait_ge(S["ident"], 2)
            pe.wait_ge(S["setup_in"], 16 * n_setup_loads)
            for c in range(C):
                for o in range(C):
                    pe.matmul(bank[0][:, c * D:(c + 1) * D], wq_in[:, o, c * 128:(c + 1) * 128], wk_in[:, o],
                              start=o == 0, stop=o == C - 1)
            for c in range(C):
                for o in range(C):
                    pe.matmul(bank[1][:, c * 128:(c + 1) * 128], wq_in[:, o, c * 128:(c + 1) * 128],
                              bk_in[:, o].broadcast_to([128, 128]), start=o == 0, stop=o == C - 1)
            for c in range(C):
                for o in range(C):
                    pe.matmul(bank[1][:, D + c * 128:D + (c + 1) * 128], wkv_in[:, o, c * 128:(c + 1) * 128],
                              awj_in[:, o].broadcast_to([128, 128]), start=o == 0, stop=o == C - 1)
            for c in range(C):
                for o in range(C):
                    pe.matmul(bank[2][:, c:c + 1], wk_in[:, o, c * 128:(c + 1) * 128], bq_in[:, o],
                              start=o == 0, stop=o == C - 1)
                for o in range(C):
                    pe.matmul(bank[2][:, C + c:C + c + 1], wkv_in[:, o, c * 128:(c + 1) * 128], awi_in[:, o],
                              start=o == 0, stop=o == C - 1)
            for o in range(C):
                pe.matmul(bank[2][:, 2 * C:2 * C + 1], bq_in[:, o].broadcast_to([128, 128]), bk_in[:, o],
                          start=o == 0, stop=o == C - 1)
            for i, v in enumerate((awj_in, awi_in)):
                for o in range(C):
                    mm = pe.matmul(bank[2][:, 2 * C + 1:2 * C + 2], kbv_in[:, o].broadcast_to([128, 128]), v[:, o],
                                   start=i == 0 and o == 0, stop=i == 1 and o == C - 1)
            mm.then_inc(S["setup_mm"], 1)
            pe.wait_ge(S["setup_ev"], 4)
            pe.wait_ge(S["setup_hi"], 9)
            pe.wait_ge(S["setup_lo"], 9)

            def step(t, stages, before):
                def made(s):
                    return t - STAGE[s] + 1

                def free(name):
                    old, ago = former(name, stages, before)
                    return old and (S[LAST_READ.get(old, old) + "_read"], made(old[0]) - ago)

                def bank_of(name):
                    return bank[BANK[name]]

                def claim(name):
                    if was := free(name):
                        pe.wait_ge(*was)

                def transposes(name, src):
                    if was := free(name):
                        pe.wait_ge(*was)
                    b = bank_of(name).rearrange("p (c g n) -> p c g n", c=C, g=G)
                    for c in range(C):
                        for g in range(G):
                            mm = pe.transpose(b[:, c, g], src[:, g, c * 128:(c + 1) * 128], ident[:])
                    mm.then_inc(S[name + "_made"], 1)

                def part(pair, *index):
                    return tuple(q[index] for q in pair)

                def node_part(s, c, g):
                    return part(xT[s], slice(None), c, slice(g * N, (g + 1) * N))

                def heads_qk(name, i, half):
                    if was := free(name):
                        pe.wait_ge(*was)
                    b = bank_of(name).rearrange("p (m n) -> p m n", m=2)
                    for m in range(2):
                        col = (2 * half + m) * 128
                        for c in range(C):
                            mm = product3(b[:, m], part(Wqkv, slice(None), c, i, slice(col, col + 128)),
                                          part(xT["h"], slice(None), c), c == 0, c == C - 1)
                    mm.then_inc(S[name + "_made"], 1)

                def heads_scores(g):
                    if was := free(f"h_S{g}e"):
                        pe.wait_ge(*was)
                    be = bank_of(f"h_S{g}e")
                    if was := free(f"h_S{g}o"):
                        pe.wait_ge(*was)
                    bo = bank_of(f"h_S{g}o")
                    for m in range(HEADS // 2):
                        for odd, b in ((0, be), (1, bo)):
                            rows = slice(64 * odd, 64 * odd + 64)
                            mm = pe.matmul(b[:, m * N:(m + 1) * N], qT[rows, m, g * N:(g + 1) * N],
                                           kT[rows, m, g * N:(g + 1) * N], start=True, stop=True)
                            if m == HEADS // 2 - 1:
                                mm.then_inc(S[f"h_S{g}{'eo'[odd]}_made"], 1)

                def heads_v(g):
                    for c in range(C):
                        mm = product3(bank_of(f"h_v{g}")[:], node_part("h", c, g), part(Wqkv, every, c, 2), c == 0, c == C - 1)
                    mm.then_inc(S[f"h_v{g}_made"], 1)

                def heads_transpose(g, i):
                    name = f"h_T{g}{'eo'[i]}"
                    if was := free(name):
                        pe.wait_ge(*was)
                    pe.wait_ge(S[f"h_p{g}"], 2 * (made("h") - 1) + i + 1)
                    for m in range(4):
                        mm = pe.transpose(bank_of(name)[:, m * N:(m + 1) * N], hs[:, g, 4 * i + m], ident[:])
                    mm.then_inc(S[name + "_made"], 1)

                def heads_values(g):
                    if was := free(f"h_PV{g}"):
                        pe.wait_ge(*was)
                    b = bank_of(f"h_PV{g}")
                    pe.wait_ge(S[f"h_T{g}e_read"], made("h"))
                    pe.wait_ge(S[f"h_T{g}o_read"], made("h"))
                    for m in range(HEADS // 2):
                        for odd in range(2):
                            h = 2 * m + odd
                            mm = pe.matmul(b[64 * odd:64 * odd + 64, m * N:(m + 1) * N],
                                           hv[:, g, h * DH:(h + 1) * DH], pT[:, g, 4 * odd + m],
                                           start=True, stop=True)
                    mm.then_inc(S[f"h_PV{g}_made"], 1)

                def heads_out(g):
                    pe.wait_ge(S[f"h_PV{g}_read"], made("h"))
                    for m in range(INNER // 128):
                        mm = product3(bank_of("h_out")[:, g * D:(g + 1) * D], part(oT, every, g, m), part(Wo, every, m),
                                      m == 0, m == INNER // 128 - 1)
                    if g == G - 1:
                        mm.then_inc(S["h_out_made"], 1)

                def hop_two(g):
                    for c in range(C):
                        mm = product3(bank_of(f"k_y2{g}")[:, 0:D + 2], node_part("k", c, g), part(Wy2, every, c), c == 0, c == C - 1)
                    mm.then_inc(S[f"k_y2{g}_made"], 1)

                def hops_zero_one(g):
                    for c in range(C):
                        mm = product3(bank_of(f"k_y01{g}")[:], node_part("k", c, g), part(Wy01, every, c), c == 0, c == C - 1)
                    mm.then_inc(S[f"k_y01{g}_made"], 1)

                def hop(g, name, ready, columns, features):
                    pe.wait_ge(S[ready], made("k"))
                    pe.matmul(bank_of(f"k_y01{g}")[:, columns], kT_[:, g], features[:, g, 0:D], start=False, stop=True,
                              skip_group_check=True).then_inc(S[f"{name}{g}_made"], 1)

                def mean_weights(g):
                    for c in range(C):
                        mm = product3(bank_of(f"m_xW{g}")[:], node_part("m", c, g), part(Wm, every, c), c == 0, c == C - 1)
                    mm.then_inc(S[f"m_xW{g}_made"], 1)

                if "h" in stages:
                    pe.wait_ge(S["a_x2T_read"], made("h"))
                    heads_qk("h_k0", 1, 0)
                    heads_qk("h_q0", 0, 0)
                    heads_qk("h_k1", 1, 1)
                    heads_qk("h_q1", 0, 1)
                    claim("h_v0")
                    heads_v(0)
                if "k" in stages:
                    pe.wait_ge(S["x3_made"], 2 * made("k"))
                    transposes("k_xT", x3)
                if "h" in stages:
                    for n in ("h_q0", "h_q1", "h_k0", "h_k1"):
                        pe.wait_ge(S[n + "_read"], made("h"))
                    heads_scores(0)
                    claim("h_v1")
                    heads_v(1)
                if "a" in stages:
                    pe.wait_ge(S["x1_made"], 2 * made("a"))
                    transposes("a_xT", x1)
                if "h" in stages:
                    heads_scores(1)
                if "k" in stages:
                    claim("k_y20")
                    pe.wait_ge(S["k_xT_read"], made("k"))
                    hop_two(0)
                    claim("k_y21")
                    hop_two(1)
                if "a" in stages:
                    claim("a_G")
                    pe.wait_ge(S["a_xlo"], made("a"))
                    for o in range(C):
                        for c in range(C):
                            mm = product3(bank_of("a_G")[:, o * G * N:(o + 1) * G * N], part(A, every, c, slice(o * 128, (o + 1) * 128)),
                                          part(xT["a"], every, c), c == 0, c == C - 1)
                    mm.then_inc(S["a_G_made"], 1)
                if "k" in stages:
                    claim("k_y010")
                    hops_zero_one(0)
                if "a" in stages:
                    claim("a_v")
                    for g in range(G):
                        for c in range(C):
                            mm = product3(bank_of("a_v")[:, g * D:(g + 1) * D], node_part("a", c, g), part(Wv, every, c), c == 0, c == C - 1)
                    mm.then_inc(S["a_v_made"], 1)
                if "k" in stages:
                    claim("k_sj")
                    for c in range(C):
                        mm = product3(bank_of("k_sj")[:, 0:G * N], part(Wsj, every, c), part(xT["k"], every, c), c == 0, c == C - 1)
                    mm.then_inc(S["k_sj_made"], 1)
                if "h" in stages:
                    heads_transpose(0, 0)
                if "a" in stages:
                    claim("a_S")
                    b = bank_of("a_S")
                    for c in range(C):
                        product3(b[:, 0:G * N], part(Wrow, every, c), part(xT["a"], every, c), c == 0, False, True)
                    pe.wait_ge(S["a_xT_read"], made("a"))
                    pe.wait_ge(S["a_G_read"], made("a"))
                    for g in range(G):
                        for c in range(C):
                            mm = pe.matmul(b[:, g * N:(g + 1) * N], x1T[:, c, g * N:(g + 1) * N], GT[:, c, g * N:(g + 1) * N],
                                           start=False, stop=c == C - 1, skip_group_check=True)
                    mm.then_inc(S["a_S_made"], 1)
                if "k" in stages:
                    claim("k_y011")
                    hops_zero_one(1)
                if "m" in stages:
                    claim("m_xW0")
                    pe.wait_ge(S["m_xlo"], made("m"))
                    mean_weights(0)
                if "h" in stages:
                    heads_transpose(0, 1)
                if "a" in stages:
                    claim("a_PV0")
                    pe.wait_ge(S["a_p"], made("a"))
                    pe.wait_ge(S["a_v_read"], made("a"))
                    pe.matmul(bank_of("a_PV0")[:, 0:D + 1], ap[:, 0], av[:, 0], start=True, stop=True).then_inc(S["a_PV0_made"], 1)
                    claim("a_PV1")
                    pe.matmul(bank_of("a_PV1")[:, 0:D + 1], ap[:, 1], av[:, 1], start=True, stop=True).then_inc(S["a_PV1_made"], 1)
                if "h" in stages:
                    heads_transpose(1, 0)
                    heads_transpose(1, 1)
                    pe.wait_ge(S["h_v0_read"], made("h"))
                    heads_values(0)
                if "m" in stages:
                    claim("m_xW1")
                    mean_weights(1)
                if "k" in stages:
                    claim("k_T")
                    pe.wait_ge(S["k_tr"], 2 * made("k"))
                    for g in range(G):
                        mm = pe.transpose(bank_of("k_T")[:, g * N:(g + 1) * N], kt[:, g], ident[:])
                    mm.then_inc(S["k_T_made"], 1)
                if "h" in stages:
                    pe.wait_ge(S["h_v1_read"], made("h"))
                    heads_values(1)
                if "k" in stages:
                    pe.wait_ge(S["k_T_read"], made("k"))
                    hop(0, "k_Ty", "k_y20_read", slice(D, 2 * D), ky2)
                    hop(1, "k_Ty", "k_y21_read", slice(D, 2 * D), ky2)
                if "m" in stages:
                    pe.wait_ge(S["adj0T_in"], 16 * made("m"))
                    pe.wait_ge(S["m_xW0_read"], made("m"))
                    pe.matmul(bank_of("m_xW0")[:, D:2 * D], adj0T[:, 0], my[:, 0, D:2 * D], start=True, stop=True,
                              skip_group_check=True).then_inc(S["m_ag0_made"], 1)
                if "k" in stages:
                    hop(0, "k_TT", "k_Ty0_read", slice(0, D), ky1)
                    hop(1, "k_TT", "k_Ty1_read", slice(0, D), ky1)
                if "h" in stages:
                    claim("h_out")
                    heads_out(0)
                if "a" in stages:
                    pe.wait_ge(S["x2_made"], 2 * made("a"))
                    transposes("a_x2T", x2)
                if "h" in stages:
                    heads_out(1)
                if "m" in stages:
                    pe.wait_ge(S["m_xW1_read"], made("m"))
                    pe.matmul(bank_of("m_xW1")[:, D:2 * D], adj0T[:, 1], my[:, 1, D:2 * D], start=True, stop=True,
                              skip_group_check=True).then_inc(S["m_ag1_made"], 1)

            for t in range(4):
                step(t, stages_at(t), stages_at(t - 1) if t else None)
            with pe.Fori(4, pairs) as t:
                step(t, "mahk", "mahk")
            for t in range(pairs, steps):
                step(t, stages_at(t), stages_at(t - 1))

        @block.scalar
        def _(act):
            def copy(dst, src):
                return act.activation(dst, src, ACT.Copy)

            act.wait_ge(S["setup_in"], 16 * n_setup_loads)
            for pair, src in ((Wm, wm_in), (Wv, wv_in), (Wqkv, wqkv_in)):
                copy(pair[0][:], src).then_inc(S["setup_hi"], 1)
            act.activation(Wo[0][:], wo_in, ACT.Copy, scale=LA).then_inc(S["setup_hi"], 1)
            for i in range(2):
                copy(Wy01[0][:, :, i * D:(i + 1) * D], wk3_in[:, i]).then_inc(S["setup_c"], 1)
            act.wait_ge(S["setup_mm"], 1)
            act.wait_ge(S["setup_ev"], 4)
            copy(A[0][:], bank[0][:].rearrange("p (c n) -> p c n", c=C)).then_inc(S["setup_hi"], 1)
            copy(Wrow[0][:], bank[1][:, 0:D].rearrange("p (c n) -> p c n", c=C)).then_inc(S["setup_hi"], 1)
            copy(Wsj[0][:], bank[1][:, D:2 * D].rearrange("p (c n) -> p c n", c=C)).then_inc(S["setup_hi"], 1)
            copy(Wy2[0][:, :, 0:D], wk3_in[:, 2]).then_inc(S["setup_hi"], 1)
            for i in range(2):
                copy(Wy2[0][:, :, D + i:D + i + 1], bank[2][:, C:2 * C].unsqueeze(2)).then_inc(S["setup_c"], 1)
            act.wait_ge(S["setup_c"], 4)
            act.activation(ve["m"][:, 0:1], minus_half[:, 0:1], ACT.Copy).then_inc(S["setup_hi"], 1)

            def step(t, stages):
                def made(s):
                    return t - STAGE[s] + 1

                def later(s):
                    return had(t, s)

                def heads_exp(g, i):
                    act.wait_ge(S[f"h_nmx{g}"], 2 * (made("h") - 1) + i + 1)
                    for h in range(4 * i, 4 * i + 4):
                        act.activation(hs[:, g, h], hs[:, g, h], ACT.Exp, bias=hnmx[:, g, h:h + 1], scale=DH ** -0.5,
                                       accum_out=hden[:, g, h:h + 1]).then_inc(S[f"h_e{g}"], 1)

                if "h" in stages:
                    act.wait_ge(S["h_k0_made"], made("h"))
                    if later("h"):
                        act.wait_ge(S["h_S1o_made"], made("h") - 1)
                        act.wait_ge(S["h_S1e_made"], made("h") - 1)
                    copy(kT[:, 0:2], chunks(bank[BANK["h_k0"]])).then_inc(S["h_k0_read"], 1)
                    act.wait_ge(S["adj2_in"], 16 * made("h"))
                    if later("h"):
                        act.wait_ge(S["h_sum"], made("h") - 1)
                    act.activation(ex[:], adj2[:], ACT.Exp, scale=-1.0).then_inc(S["h_ex"], 1)
                if "m" in stages:
                    act.wait_ge(S["x0T_in"], 16 * made("m"))
                    if later("m"):
                        act.wait_ge(S["m_xW1_made"], made("m") - 1)
                    copy(xT["m"][0][:], x0T[:]).then_inc(S["m_xhi"], 1)
                if "h" in stages:
                    act.wait_ge(S["h_q0_made"], made("h"))
                    if later("h"):
                        act.wait_ge(S["h_S1o_made"], made("h") - 1)
                        act.wait_ge(S["h_S1e_made"], made("h") - 1)
                    copy(qT[:, 0:2], chunks(bank[BANK["h_q0"]])).then_inc(S["h_q0_read"], 1)
                    act.wait_ge(S["h_k1_made"], made("h"))
                    if later("h"):
                        act.wait_ge(S["h_S1o_made"], made("h") - 1)
                        act.wait_ge(S["h_S1e_made"], made("h") - 1)
                    copy(kT[:, 2:4], chunks(bank[BANK["h_k1"]])).then_inc(S["h_k1_read"], 1)
                    act.wait_ge(S["h_q1_made"], made("h"))
                    if later("h"):
                        act.wait_ge(S["h_S1o_made"], made("h") - 1)
                        act.wait_ge(S["h_S1e_made"], made("h") - 1)
                    copy(qT[:, 2:4], chunks(bank[BANK["h_q1"]])).then_inc(S["h_q1_read"], 1)
                if "k" in stages:
                    act.wait_ge(S["k_xT_made"], made("k"))
                    if later("k"):
                        act.wait_ge(S["k_y011_made"], made("k") - 1)
                    copy(xT["k"][0][:], chunks(bank[BANK["k_xT"]])).then_inc(S["k_xhi"], 1)
                if "h" in stages:
                    act.wait_ge(S["h_v0_made"], made("h"))
                    if later("h"):
                        act.wait_ge(S["h_PV0_made"], made("h") - 1)
                    copy(hv[:, 0], bank[BANK["h_v0"]][:]).then_inc(S["h_v0_read"], 1)
                    act.wait_ge(S["h_v1_made"], made("h"))
                    if later("h"):
                        act.wait_ge(S["h_PV1_made"], made("h") - 1)
                    copy(hv[:, 1], bank[BANK["h_v1"]][:]).then_inc(S["h_v1_read"], 1)
                if "a" in stages:
                    act.wait_ge(S["a_xT_made"], made("a"))
                    if later("a"):
                        act.wait_ge(S["a_S_made"], made("a") - 1)
                    copy(xT["a"][0][:], chunks(bank[BANK["a_xT"]])).then_inc(S["a_xhi"], 1)
                if "h" in stages:
                    heads_exp(0, 0)
                    heads_exp(0, 1)
                if "a" in stages:
                    act.wait_ge(S["a_xlo"], made("a"))
                    if later("a"):
                        act.wait_ge(S["a_S_made"], made("a") - 1)
                    copy(x1T[:], chunks(bank[BANK["a_xT"]])).then_inc(S["a_xT_read"], 1)
                if "k" in stages:
                    act.wait_ge(S["k_y20_made"], made("k"))
                    if later("k"):
                        act.wait_ge(S["k_Ty0_made"], made("k") - 1)
                        act.wait_ge(S["k_sj_read"], made("k") - 1)
                    copy(ky2[:, 0], bank[BANK["k_y20"]][:, 0:D + 2]).then_inc(S["k_y20_read"], 1)
                if "a" in stages:
                    act.wait_ge(S["a_G_made"], made("a"))
                    if later("a"):
                        act.wait_ge(S["a_S_made"], made("a") - 1)
                    for c in range(C):
                        last = act.activation(GT[:, c], bank[BANK["a_G"]][:, c * G * N:(c + 1) * G * N], ACT.Identity, bias=u_col[:, c:c + 1])
                    last.then_inc(S["a_G_read"], 1)
                if "h" in stages:
                    heads_exp(1, 0)
                    heads_exp(1, 1)
                if "a" in stages:
                    act.wait_ge(S["a_S_made"], made("a"))
                    if later("a"):
                        act.wait_ge(S["a_p"], made("a") - 1)
                    act.activation(ae[:], bank[BANK["a_S"]][:, 0:G * N].rearrange("p (g n) -> p g n", g=G), ACT.Exp,
                                   bias=cq_col[:, 0:1]).then_inc(S["a_S_read"], 1)
                if "h" in stages:
                    if later("h"):
                        act.wait_ge(S["h_PV0_made"], made("h") - 1)
                    act.wait_ge(S["h_T0e_made"], made("h"))
                    copy(pT[:, 0, 0:4], by_four(bank[BANK["h_T0e"]])).then_inc(S["h_T0e_read"], 1)
                if "a" in stages:
                    act.wait_ge(S["a_v_made"], made("a"))
                    if later("a"):
                        act.wait_ge(S["a_PV1_made"], made("a") - 1)
                    copy(av[:, :, 0:D], bank[BANK["a_v"]][:].rearrange("p (g n) -> p g n", g=G)).then_inc(S["a_v_read"], 1)
                if "k" in stages:
                    act.wait_ge(S["k_leaky"], made("k"))
                    if later("k"):
                        act.wait_ge(S["k_w"], 2 * (made("k") - 1))
                    act.activation(kz[:], kl[:], ACT.Exp).then_inc(S["k_e"], 1)
                if "m" in stages:
                    act.wait_ge(S["m_xW0_made"], made("m"))
                    if later("m"):
                        act.wait_ge(S["m_sum"], 2 * (made("m") - 1))
                    copy(my[:, 0], bank[BANK["m_xW0"]][:]).then_inc(S["m_xW0_read"], 1)
                if "h" in stages:
                    if later("h"):
                        act.wait_ge(S["h_PV0_made"], made("h") - 1)
                    act.wait_ge(S["h_T0o_made"], made("h"))
                    copy(pT[:, 0, 4:8], by_four(bank[BANK["h_T0o"]])).then_inc(S["h_T0o_read"], 1)
                    if later("h"):
                        act.wait_ge(S["h_PV1_made"], made("h") - 1)
                    act.wait_ge(S["h_T1e_made"], made("h"))
                    copy(pT[:, 1, 0:4], by_four(bank[BANK["h_T1e"]])).then_inc(S["h_T1e_read"], 1)
                    if later("h"):
                        act.wait_ge(S["h_PV1_made"], made("h") - 1)
                    act.wait_ge(S["h_T1o_made"], made("h"))
                    copy(pT[:, 1, 4:8], by_four(bank[BANK["h_T1o"]])).then_inc(S["h_T1o_read"], 1)
                    act.wait_ge(S["h_PV0_made"], made("h"))
                    if later("h"):
                        act.wait_ge(S["h_out_made"], made("h") - 1)
                    copy(oT[0][:, 0], by_four(bank[BANK["h_PV0"]])).then_inc(S["h_ohi0"], 1)
                if "k" in stages:
                    act.wait_ge(S["k_Ty0_made"], made("k"))
                    if later("k"):
                        act.wait_ge(S["k_TT0_made"], made("k") - 1)
                    copy(ky1[:, 0], bank[BANK["k_y010"]][:, D:2 * D]).then_inc(S["k_Ty0_read"], 1)
                if "h" in stages:
                    act.wait_ge(S["h_PV1_made"], made("h"))
                    if later("h"):
                        act.wait_ge(S["h_out_made"], made("h") - 1)
                    copy(oT[0][:, 1], by_four(bank[BANK["h_PV1"]])).then_inc(S["h_ohi1"], 1)
                if "m" in stages:
                    act.wait_ge(S["m_xW1_made"], made("m"))
                    if later("m"):
                        act.wait_ge(S["m_sum"], 2 * (made("m") - 1))
                    copy(my[:, 1], bank[BANK["m_xW1"]][:]).then_inc(S["m_xW1_read"], 1)
                if "a" in stages:
                    act.wait_ge(S["a_x2T_made"], made("a"))
                    if "h" in stages:
                        act.wait_ge(S["h_v1_made"], made("h"))
                    copy(xT["h"][0][:], chunks(bank[BANK["a_x2T"]])).then_inc(S["a_x2hi"], 1)

            for t in range(4):
                step(t, stages_at(t))
            with act.Fori(4, pairs) as t:
                step(t, "mahk")
            for t in range(pairs, steps):
                step(t, stages_at(t))

        @block.vector
        def _(dve):
            def gate():
                dve.sem_inc(S["gate"], 1)

            def copy(dst, src):
                return dve.tensor_copy(dst, src)

            dve.wait_ge(S["setup_in"], 16 * n_setup_loads)
            dve.tensor_tensor(bk3_bc[:], bk3_in[:, 0], bk3_in[:, 1], ALU.add).then_inc(S["setup_sum"], 1)
            dve.wait_ge(S["setup_sum"], 1)
            dve.tensor_tensor(bk3_bc[:], bk3_bc[:], bk3_in[:, 2], ALU.add).then_inc(S["setup_sum"], 1)
            dve.wait_ge(S["setup_mm"], 1)
            dve.tensor_copy(u_col[:], bank[2][:, 0:C]).then_inc(S["setup_ev"], 1)
            dve.tensor_copy(cq_col[:], bank[2][:, 2 * C:2 * C + 1]).then_inc(S["setup_ev"], 1)
            dve.tensor_scalar(ke_col[:], bank[2][:, 2 * C + 1:2 * C + 2], kab_col[:, 0:1], None, ALU.add).then_inc(S["setup_ev"], 1)
            dve.wait_ge(S["setup_ev"], 3)
            dve.tensor_copy(kden[:, 0:1], ke_col[:]).then_inc(S["setup_ev"], 1)
            dve.wait_ge(S["setup_hi"], 9)
            def lo(pair, src, *index):
                return dve.tensor_tensor(pair[1][index], src, as_f32(pair[0][index]), ALU.subtract)
            for pair, src in ((Wm, wm_in), (Wv, wv_in), (Wqkv, wqkv_in)):
                lo(pair, src, every).then_inc(S["setup_lo"], 1)
            dve.scalar_tensor_tensor(out=Wo[1][:], in0=wo_in, scalar=LA, in1=as_f32(Wo[0][:]), op0=ALU.mult,
                                     op1=ALU.subtract).then_inc(S["setup_lo"], 1)
            lo(Wy01, wk3_in[:, 0], every, every, slice(0, D))
            lo(Wy01, wk3_in[:, 1], every, every, slice(D, 2 * D))
            lo(A, bank[0][:].rearrange("p (c n) -> p c n", c=C), every).then_inc(S["setup_lo"], 1)
            lo(Wrow, bank[1][:, 0:D].rearrange("p (c n) -> p c n", c=C), every).then_inc(S["setup_lo"], 1)
            lo(Wsj, bank[1][:, D:2 * D].rearrange("p (c n) -> p c n", c=C), every).then_inc(S["setup_lo"], 1)
            lo(Wy2, wk3_in[:, 2], every, every, slice(0, D)).then_inc(S["setup_lo"], 1)
            for i in range(2):
                last = lo(Wy2, bank[2][:, C:2 * C].unsqueeze(2), every, every, slice(D + i, D + i + 1))
            last.then_inc(S["setup_lo"], 1)

            def step(t, stages):
                def made(s):
                    return t - STAGE[s] + 1

                def later(s):
                    return had(t, s)

                def normalize(s, dst, signal):
                    for g in range(G):
                        dve.tensor_scalar(dst[:, g], hh[s][:, g], mv[s][:, g, 0:1], rstd[s][:, g:g + 1],
                                          ALU.subtract, ALU.mult).then_inc(S[signal], 1)

                def mean_variance(s, n):
                    dve.wait_ge(S[s + "_h"], 2 * n)
                    gate()
                    for g in range(G):
                        dve.bn_aggr(mv[s][:, g], stats[s][:, g]).then_inc(S[s + "_mv"], 1)

                def heads_max(g, i):
                    half = "eo"[i]
                    if later("h"):
                        dve.wait_ge(S[f"h_T{g}{half}_made"], made("h") - 1)
                        dve.wait_ge(S[f"h_nmx{g}"], 2 * (made("h") - 1))
                    dve.wait_ge(S[f"h_S{g}{half}_made"], made("h"))
                    gate()
                    for m in range(4):
                        h = 4 * i + m
                        last = dve.tensor_tensor_reduce(hs[:, g, h], bank[BANK[f"h_S{g}{half}"]][:, m * N:(m + 1) * N],
                                                        mneg[:, g], 1.0, -BIG, ALU.add, ALU.max, hmx[:, g, h:h + 1])
                    last.then_inc(S[f"h_S{g}{half}_read"], 1)
                    dve.wait_ge(S[f"h_S{g}{half}_read"], made("h"))
                    heads = slice(4 * i, 4 * i + 4)
                    dve.tensor_scalar(hnmx[:, g, heads], hmx[:, g, heads], -(DH ** -0.5), None, ALU.mult).then_inc(S[f"h_nmx{g}"], 1)

                def heads_mix(g, i):
                    heads = slice(4 * i, 4 * i + 4)
                    dve.wait_ge(S[f"h_e{g}"], HEADS * (made("h") - 1) + 4 * (i + 1))
                    dve.reciprocal(hr[:, g, heads], hden[:, g, heads]).then_inc(S[f"h_r{g}"], 1)
                    dve.wait_ge(S[f"h_r{g}"], 2 * (made("h") - 1) + i + 1)
                    for h in range(4 * i, 4 * i + 4):
                        last = dve.scalar_tensor_tensor(out=hs[:, g, h], in0=hs[:, g, h], scalar=hr[:, g, h:h + 1],
                                                        in1=mix[:, g], op0=ALU.mult, op1=ALU.add)
                    last.then_inc(S[f"h_p{g}"], 1)

                if "m" in stages:
                    dve.wait_ge(S["adj0_in"], 16 * made("m"))
                    dve.tensor_reduce(deg[:], adj0[:], AX.X, ALU.add).then_inc(S["m_deg"], 1)
                    dve.wait_ge(S["m_deg"], 3 * (made("m") - 1) + 1)
                    dve.tensor_scalar(degmax[:], deg[:], EPS_DEG, None, ALU.max).then_inc(S["m_deg"], 1)
                    dve.wait_ge(S["m_deg"], 3 * (made("m") - 1) + 2)
                    dve.reciprocal(rdeg[:], degmax[:]).then_inc(S["m_deg"], 1)
                if "a" in stages:
                    dve.wait_ge(S["m_rstd"], made("a"))
                    if later("a"):
                        dve.wait_ge(S["a_xT_made"], made("a") - 1)
                        dve.wait_ge(S["x1_bias"], made("a") - 1)
                    normalize("m", x1, "x1_made")
                if "k" in stages:
                    dve.wait_ge(S["k_xhi"], made("k"))
                    dve.tensor_tensor(xT["k"][1][:], chunks(bank[BANK["k_xT"]]), as_f32(xT["k"][0][:]), ALU.subtract).then_inc(S["k_xT_read"], 1)
                if "h" in stages:
                    dve.wait_ge(S["h_mneg"], made("h"))
                    heads_max(0, 0)
                    heads_max(0, 1)
                if "a" in stages:
                    dve.wait_ge(S["a_xhi"], made("a"))
                    dve.tensor_tensor(xT["a"][1][:], chunks(bank[BANK["a_xT"]]), as_f32(xT["a"][0][:]), ALU.subtract).then_inc(S["a_xlo"], 1)
                if "h" in stages:
                    heads_max(1, 0)
                if "k" in stages:
                    dve.wait_ge(S["k_y21_made"], made("k"))
                    if later("k"):
                        dve.wait_ge(S["k_Ty1_made"], made("k") - 1)
                        dve.wait_ge(S["k_sj_read"], made("k") - 1)
                    copy(ky2[:, 1], bank[BANK["k_y21"]][:, 0:D + 2]).then_inc(S["k_y21_read"], 1)
                if "h" in stages:
                    heads_max(1, 1)
                    dve.wait_ge(S["h_mix"], made("h"))
                    heads_mix(0, 0)
                    heads_mix(0, 1)
                if "k" in stages:
                    dve.wait_ge(S["k_sj_made"], made("k"))
                    if later("k"):
                        dve.wait_ge(S["k_w"], 2 * (made("k") - 1))
                    for g in range(G):
                        dve.wait_ge(S[f"k_y2{g}_read"], made("k"))
                        last = dve.tensor_scalar(kw[:, g], bank[BANK["k_sj"]][:, g * N:(g + 1) * N], ky2[:, g, D:D + 1],
                                                 ke_col[:, 0:1], ALU.add, ALU.add)
                    last.then_inc(S["k_sj_read"], 1)
                if "h" in stages:
                    heads_mix(1, 0)
                if "k" in stages:
                    dve.wait_ge(S["k_sj_read"], made("k"))
                    if later("k"):
                        dve.wait_ge(S["k_e"], made("k") - 1)
                    dve.scalar_tensor_tensor(out=kl[:], in0=kw[:], scalar=SLOPE, in1=kw[:], op0=ALU.mult, op1=ALU.max).then_inc(S["k_leaky"], 1)
                if "h" in stages:
                    heads_mix(1, 1)
                if "k" in stages:
                    dve.wait_ge(S["k_e"], made("k"))
                    dve.wait_ge(S["adj3_in"], 16 * made("k"))
                    gate()
                    for g in range(G):
                        dve.tensor_tensor_reduce(kw[:, g], kz[:, g], adj3[:, g], 1.0, 0.0, ALU.mult, ALU.add, kden[:, g:g + 1]).then_inc(S["k_w"], 1)
                    dve.wait_ge(S["k_w"], 2 * made("k"))
                    dve.tensor_scalar(kden2[:], kden[:], EPS_ROW, None, ALU.add).then_inc(S["k_den"], 1)
                    dve.wait_ge(S["k_den"], 2 * made("k") - 1)
                    dve.reciprocal(krden[:], kden2[:]).then_inc(S["k_den"], 1)
                    dve.wait_ge(S["k_den"], 2 * made("k"))
                    if later("k"):
                        dve.wait_ge(S["k_T_made"], made("k") - 1)
                    for g in range(G):
                        dve.tensor_scalar(kt[:, g], kw[:, g], krden[:, g:g + 1], None, ALU.mult).then_inc(S["k_tr"], 1)
                if "a" in stages:
                    dve.wait_ge(S["x1_bias"], made("a"))
                    for g in range(G):
                        dve.wait_ge(S[f"a_PV{g}_made"], made("a"))
                        dve.reciprocal(arden[:, g:g + 1], bank[BANK[f"a_PV{g}"]][:, D:D + 1]).then_inc(S["a_rden"], 1)
                    for g in range(G):
                        dve.wait_ge(S["a_rden"], 2 * (made("a") - 1) + g + 1)
                        dve.scalar_tensor_tensor(out=hh["a"][:, g], in0=bank[BANK[f"a_PV{g}"]][:, 0:D], scalar=arden[:, g:g + 1],
                                                 in1=x1b[:, g], op0=ALU.mult, op1=ALU.add).then_inc(S[f"a_PV{g}_read"], 1)
                    for g in range(G):
                        dve.wait_ge(S[f"a_PV{g}_read"], made("a"))
                        dve.bn_stats(stats["a"][:, g], hh["a"][:, g]).then_inc(S["a_h"], 1)
                    mean_variance("a", made("a"))
                if "k" in stages:
                    dve.wait_ge(S["k_T_made"], made("k"))
                    if later("k"):
                        dve.wait_ge(S["k_TT1_made"], made("k") - 1)
                    copy(kT_[:], bank[BANK["k_T"]][:, 0:G * N].rearrange("p (g n) -> p g n", g=G)).then_inc(S["k_T_read"], 1)
                if "h" in stages:
                    dve.wait_ge(S["h_ohi0"], made("h"))
                    dve.tensor_tensor(oT[1][:, 0], by_four(bank[BANK["h_PV0"]]), as_f32(oT[0][:, 0]), ALU.subtract).then_inc(S["h_PV0_read"], 1)
                if "a" in stages:
                    if "h" in stages:
                        dve.wait_ge(S["x2_bias"], made("h"))
                    if later("a"):
                        dve.wait_ge(S["a_x2T_made"], made("a") - 1)
                    dve.wait_ge(S["a_rstd"], made("a"))
                    normalize("a", x2, "x2_made")
                if "k" in stages:
                    dve.wait_ge(S["k_Ty1_made"], made("k"))
                    if later("k"):
                        dve.wait_ge(S["k_TT1_made"], made("k") - 1)
                    copy(ky1[:, 1], bank[BANK["k_y011"]][:, D:2 * D]).then_inc(S["k_Ty1_read"], 1)
                if "h" in stages:
                    dve.wait_ge(S["h_ohi1"], made("h"))
                    dve.tensor_tensor(oT[1][:, 1], by_four(bank[BANK["h_PV1"]]), as_f32(oT[0][:, 1]), ALU.subtract).then_inc(S["h_PV1_read"], 1)
                if "k" in stages:
                    for g in range(G):
                        dve.wait_ge(S[f"k_TT{g}_made"], made("k"))
                        dve.tensor_tensor(ksum[:, g], bank[BANK[f"k_y01{g}"]][:, 0:D], bk3_bc[:], ALU.add).then_inc(S[f"k_TT{g}_read"], 1)
                    dve.wait_ge(S["x3_made"], 2 * made("k"))
                    for g in range(G):
                        dve.wait_ge(S[f"k_TT{g}_read"], made("k"))
                        dve.scalar_tensor_tensor(out=hh["k"][:, g], in0=ksum[:, g], scalar=0.0, in1=x3[:, g],
                                                 op0=ALU.max, op1=ALU.add).then_inc(S["k_sum"], 1)
                    for g in range(G):
                        dve.wait_ge(S["k_sum"], 2 * (made("k") - 1) + g + 1)
                        dve.bn_stats(stats["k"][:, g], hh["k"][:, g]).then_inc(S["k_h"], 1)
                    mean_variance("k", made("k"))
                if "a" in stages:
                    dve.wait_ge(S["a_x2hi"], made("a"))
                    dve.tensor_tensor(xT["h"][1][:], chunks(bank[BANK["a_x2T"]]), as_f32(xT["h"][0][:]), ALU.subtract).then_inc(S["a_x2T_read"], 1)
                if "h" in stages:
                    dve.wait_ge(S["x2_bias"], made("h"))
                    dve.wait_ge(S["h_out_made"], made("h"))
                    dve.tensor_tensor(hh["h"][:], bank[BANK["h_out"]][:].rearrange("p (g n) -> p g n", g=G), x2b[:], ALU.add).then_inc(S["h_out_read"], 1)
                    dve.wait_ge(S["h_out_read"], made("h"))
                    for g in range(G):
                        dve.bn_stats(stats["h"][:, g], hh["h"][:, g]).then_inc(S["h_h"], 1)
                    mean_variance("h", made("h"))
                if "m" in stages:
                    dve.wait_ge(S["x0_in"], 16 * made("m"))
                    dve.wait_ge(S["m_deg"], 3 * made("m"))
                    for g in range(G):
                        dve.wait_ge(S[f"m_ag{g}_made"], made("m"))
                        dve.scalar_tensor_tensor(out=msum[:, g], in0=bank[BANK[f"m_xW{g}"]][:, D:2 * D], scalar=rdeg[:, g:g + 1],
                                                 in1=my[:, g, 0:D], op0=ALU.mult, op1=ALU.add).then_inc(S[f"m_ag{g}_read"], 1)
                    for g in range(G):
                        dve.wait_ge(S[f"m_ag{g}_read"], made("m"))
                        dve.scalar_tensor_tensor(out=hh["m"][:, g], in0=msum[:, g], scalar=0.0, in1=x0[:, g],
                                                 op0=ALU.max, op1=ALU.add).then_inc(S["m_sum"], 1)
                    for g in range(G):
                        dve.wait_ge(S["m_sum"], 2 * (made("m") - 1) + g + 1)
                        dve.bn_stats(stats["m"][:, g], hh["m"][:, g]).then_inc(S["m_h"], 1)
                    mean_variance("m", made("m"))
                if "h" in stages:
                    dve.wait_ge(S["h_rstd"], made("h"))
                    if "k" in stages:
                        dve.wait_ge(S["k_xT_made"], made("k"))
                    normalize("h", x3, "x3_made")
                if "k" in stages:
                    if later("k"):
                        dve.wait_ge(S["y_out"], 16 * (made("k") - 1))
                    dve.wait_ge(S["k_rstd"], made("k"))
                    normalize("k", y, "y_made")

            for t in range(4):
                step(t, stages_at(t))
            with dve.Fori(4, pairs) as t:
                step(t, "mahk")
            for t in range(pairs, steps):
                step(t, stages_at(t))


ARGS = ["x", "x_T", "adj_rows", "adj_T", "nodemask", "nodemask_T", "L0_gnn_W", "L1_gnn_Wq_w", "L1_gnn_Wk_w", "L1_gnn_Wv_w", "L1_gnn_Wv_b",
        "columns", "L2_gnn_W_qkv", "L2_gnn_W_out", "L2_gnn_b_out", "L3_gnn_Wv", "L3_gnn_ab", "L3_gnn_Wk", "L3_gnn_bk"]


def kernel(**inputs):
    import concourse.bacc as bacc
    from concourse.bass_utils import run_bass_kernel_spmd

    a = {n: np.asarray(v) for n, v in inputs.items()}
    a["nodemask"] = a["nodemask"].view(np.uint8)
    a["nodemask_T"] = a["nodemask"].T
    aw = a["L3_gnn_aw"][:, 0]
    vectors = (a["L1_gnn_Wq_b"], a["L1_gnn_Wk_b"], a["L3_gnn_bv"], aw[:D], aw[D:])
    a["columns"] = np.stack([v.reshape(C, 128) for v in vectors]).transpose(2, 0, 1)
    x, adj = a["x"], a["adj"]
    pairs = x.shape[0] // G
    a["x_T"] = x.reshape(pairs, G, N, C, 128).transpose(0, 4, 3, 1, 2).reshape(pairs, 128, C * G * N)
    a["adj_rows"] = adj.reshape(pairs, G, N, N).transpose(0, 2, 1, 3).reshape(pairs, N, G * N)
    a["adj_T"] = adj.reshape(pairs, G, N, N).transpose(0, 3, 1, 2).reshape(pairs, N, G * N)
    w = a["L0_gnn_W"]
    a["L0_gnn_W"] = np.concatenate([w[:, :D].T, w[:, D:].T], axis=1)
    a["L1_gnn_Wv_w"] = a["L1_gnn_Wv_w"].T
    a["L3_gnn_Wv"] = a["L3_gnn_Wv"].T
    a["L2_gnn_W_qkv"] = a["L2_gnn_W_qkv"].reshape(D, HEADS, 3, DH).transpose(0, 2, 1, 3).reshape(D, 3 * INNER)

    nc = bacc.Bacc("TRN2", target_bir_lowering=False, num_devices=1)
    arrays, args = {}, []
    for n in ARGS:
        arrays[f"in_{n}"] = np.ascontiguousarray(a[n])
        args.append(nc.dram_tensor(f"in_{n}", a[n].shape, mybir.dt.from_np(a[n].dtype), kind="ExternalInput").ap())
    out = nc.dram_tensor("out_0", a["x"].shape, F32, kind="ExternalOutput").ap()
    build(nc, *args, out)
    return run_bass_kernel_spmd(nc, [arrays], core_ids=[0]).results[0]["out_0"]
```

```python
from contextlib import ExitStack

import numpy as np

import concourse.bass as bass
from concourse import mybir

F32 = mybir.dt.float32
F32R = mybir.dt.float32r
U8 = mybir.dt.uint8
ALU = mybir.AluOpType
ACT = mybir.ActivationFunctionType
AX = mybir.AxisListType

N = 128
D = 256
C = D // 128
G = 2
HEADS, DH = 8, 64
INNER = HEADS * DH
HOPS = 3
LA = 0.33
EPS_DEG, EPS_LN, EPS_ROW = 1e-6, 1e-5, 1e-12
BIG = float(np.finfo(np.float32).max)
SLOPE = 0.2
STAGE = {"m": 0, "a": 1, "h": 2, "k": 3}

PRODUCTS = [
    ("h_k0", 4), ("h_k1", 7), ("h_q0", 0), ("h_q1", 4), ("k_xT", 2), ("h_v0", 5), ("a_xT", 7), ("k_y20", 1),
    ("k_y21", 5), ("h_S0e", 3), ("h_S0o", 6), ("k_sj", 2), ("a_G", 1), ("h_S1e", 4), ("h_S1o", 3), ("a_v", 5),
    ("k_y010", 1), ("a_S", 7), ("k_y011", 4), ("h_v1", 0), ("m_xW0", 2), ("k_T", 3), ("h_T0e", 7), ("h_T0o", 6),
    ("h_T1e", 5), ("a_PV0", 0), ("a_PV1", 3), ("h_T1o", 7), ("h_PV0", 6), ("h_PV1", 7), ("m_xW1", 5), ("h_out", 6),
    ("a_x2T", 0),
]
BANK = dict(PRODUCTS)
LAST_READ = {"m_xW0": "m_ag0", "m_xW1": "m_ag1", "k_y010": "k_TT0", "k_y011": "k_TT1"}

READS = [n for n, _ in PRODUCTS] + ["m_ag0", "m_ag1", "k_Ty0", "k_Ty1", "k_TT0", "k_TT1"]
OTHER = """x0_in x0T_in adj0_in adj0T_in adj1T_in adj2_in adj3_in mask_in y_out
a_x2hi m_xhi m_xlo m_yhi m_Ahi m_Alo a_phi a_plo a_vhi k_Thi k_yhi k_s k_diag a_xhi a_xlo k_xhi h_ohi
m_deg m_sum m_h m_mv m_ve m_rstd x1_made
a_p a_rden a_h a_mv a_ve a_rstd x2_made x1_bias
h_mrow h_m2 h_mneg h_ex h_sum h_mix h_nmx h_e h_r h_p
h_h h_mv h_ve h_rstd x3_made x2_bias
k_leaky k_e k_w k_den k_tr k_sum k_h k_mv k_ve k_rstd y_made
ident halves in_m in_p in_q in_a in_h in_k weights_mm weights_ev weights_hi weights_lo gate""".split()


WEIGHTS = {"m": 1, "v": 3, "a": 7, "h": 9, "k": 12}


def former(product, stages, before):
    names = [n for n, _ in PRODUCTS]
    i = names.index(product)
    for n in reversed(names[:i]):
        if BANK[n] == BANK[product] and n[0] in stages:
            return n, 0
    for n in reversed(names):
        if before and BANK[n] == BANK[product] and n[0] in before:
            return n, 1
    return None, 0


def build(nc, x, xt, adj, adjt, mask, maskT, wm, wq, wk, wvT, bv, columns, wqkv, wout, bout, wkvT, kab, wk3, bk3, out):
    pairs = x.shape[0] // G
    steps = pairs + len(STAGE) - 1

    def stages_at(t):
        return "".join(s for s, n in STAGE.items() if 0 <= t - n < pairs)

    with ExitStack() as ctx:
        def sb(name, *shape, dt=F32):
            return ctx.enter_context(nc.sbuf_tensor(name, [128, *shape], dt))

        S = {}
        for n in READS:
            S[n + "_made"] = ctx.enter_context(nc.semaphore(n + "_made"))
            if n not in ("k_y010", "k_y011"):
                S[n + "_read"] = ctx.enter_context(nc.semaphore(n + "_read"))
        for n in OTHER:
            S[n] = ctx.enter_context(nc.semaphore(n))
        bank = [ctx.enter_context(nc.psum_tensor(f"bank{b}", [128, 512], F32)) for b in range(8)]

        def parts(name, *shape):
            return sb(name + "_hi", *shape, dt=F32R), sb(name + "_lo", *shape, dt=F32R)

        Wm = parts("Wm", C, 2 * D)
        A = parts("A", C, D)
        Wrow = parts("Wrow", C, 128)
        Wv = parts("Wv", C, D)
        Wqkv = parts("Wqkv", C, 3, INNER)
        Wo = parts("Wo", INNER // 128, D)
        Wy2 = parts("Wy2", C, D + 2)
        Wy01 = parts("Wy01", C, 2 * D)

        ident, ones = sb("identity", 128), sb("ones", 128)
        minus_half = sb("minus_half", G)
        u_col = sb("u_col", C)
        cq_col = sb("cq_col", 1)
        ke_col = sb("ke_col", 1)
        kab_col = sb("kab_col", 1)
        vec_in = sb("vec_in", 5, C)
        bv_bc = sb("bv_bc", D)
        bout_bc = sb("bout_bc", D)
        bk3_in = sb("bk3_in", HOPS, D)
        bk3_bc = sb("bk3_bc", D)

        x0, x1, x1b, x2, x2b, x3 = (sb(n, G, D) for n in "x0 x1 x1b x2 x2b x3".split())
        hh = {s: sb("h_" + s, G, D) for s in "mahk"}
        stats = {s: sb("stats_" + s, G, 6) for s in "mahk"}
        mv = {s: sb("mv_" + s, G, 2) for s in "mahk"}
        ve = {s: sb("ve_" + s, G) for s in "mahk"}
        rstd = {s: sb("rstd_" + s, G) for s in "mahk"}
        xT = {s: parts("xT_" + s, C, G * N) for s in "mahk"}
        x0T, x1T = sb("x0T", C, G * N), sb("x1T", C, G * N)
        adj0, adj0T, adj1T, adj2, adj3 = (sb(n, G, N) for n in "adj0 adj0T adj1T adj2 adj3".split())
        deg, degmax, rdeg = sb("deg", G), sb("degmax", G), sb("rdeg", G)
        mx, adjm = sb("mx", G, D), parts("adjm", G, N)
        msum, my = sb("msum", G, D), parts("my", G, D)
        GT = sb("GT", C, G * N)
        ae, ap = sb("ae", G, N), sb("ap", G, N)
        aP = parts("aP", G, N)
        av = parts("av", G, D + 2)
        arden = sb("arden", G)
        mrow8, mcol8 = sb("mrow8", G, N, dt=U8), sb("mcol8", G, dt=U8)
        mrow, mcol = sb("mrow", G, N), sb("mcol", G)
        m2, mneg, ex, exs, mix = (sb(n, G, N) for n in "m2 mneg ex exs mix".split())
        hmx, hnmx, hden, hr = (sb(n, G, HEADS) for n in "hmx hnmx hden hr".split())
        work = sb("work", 7168)
        qT = work[:, 0:1024].rearrange("p (m n) -> p m n", m=4)
        kT = work[:, 1024:2048].rearrange("p (m n) -> p m n", m=4)
        hv = work[:, 2048:3072].rearrange("p (g f) -> p g f", g=G)
        hs = work[:, 3072:5120].rearrange("p (g h n) -> p g h n", g=G, h=HEADS)
        pT = work[:, 5120:7168].rearrange("p (g h n) -> p g h n", g=G, h=HEADS)
        oT = parts("oT", G, INNER // 128, N)
        ky2, ks, diag = parts("ky2", G, D), sb("ks", G, 2), sb("diag", G, N)
        ky1 = parts("ky1", G, D)
        kz, kl, kw, kt = (sb(n, G, N) for n in "kz kl kw ktr".split())
        kT_ = parts("kT_", G, N)
        kden, kden2, krden = sb("kden", G), sb("kden2", G), sb("krden", G)
        ksum = sb("ksum", G, D)
        y = sb("y", G, D)
        stage3 = sb("stage3", 2048)

        wm_in = work[:, 0:1024].rearrange("p (c n) -> p c n", c=C)
        wq_in = work[:, 1024:1536].rearrange("p (c n) -> p c n", c=C)
        wk_in = work[:, 1536:2048].rearrange("p (c n) -> p c n", c=C)
        wv_in = work[:, 2048:2560].rearrange("p (c n) -> p c n", c=C)
        wkv_in = stage3[:, 1536:2048].rearrange("p (c n) -> p c n", c=C)
        wqkv_in = work[:, 3072:6144].rearrange("p (c i n) -> p c i n", c=C, i=3)
        wo_in = work[:, 6144:7168].rearrange("p (c n) -> p c n", c=4)
        wk3_in = stage3[:, 0:1536].rearrange("p (k c n) -> p k c n", k=HOPS, c=C)
        bq_in, bk_in, kbv_in, awj_in, awi_in = (vec_in[:, i].unsqueeze(2) for i in range(5))

        xg = x.rearrange("(p g) n f -> p n g f", g=G)
        og = out.rearrange("(p g) n f -> p n g f", g=G)
        mrowg = mask.rearrange("(p g) n -> p (g n)", g=G)
        mcolg = maskT.rearrange("n (p g) -> p n g", g=G)

        bank_A, bank_rows, bank_cols = [bank[b] for b in range(8) if b not in (BANK["m_xW0"], BANK["m_xW1"])][:3]

        every = slice(None)

        def as_f32(t):
            return t.bitcast(F32)

        def chunks(t):
            return t[:].rearrange("p (c n) -> p c n", c=2)

        def by_four(t):
            return t[:].rearrange("p (m n) -> p m n", m=4)

        def had(t, stage):
            return not isinstance(t, int) or t > STAGE[stage]

        block = ctx.enter_context(nc.Block())

        @block.sync
        def _(sp):
            def load_x0(p):
                sp.dma_start(x0[:], xg[p]).then_inc(S["x0_in"], 16)

            def load_x0T(p):
                sp.dma_start(x0T[:].rearrange("p c n -> p (c n)"), xt[p]).then_inc(S["x0T_in"], 16)

            def load_adj(tile, name, p, array=adj):
                sp.dma_start(tile[:].rearrange("p g n -> p (g n)"), array[p]).then_inc(S[name], 16)

            def load_mask(p):
                sp.dma_start(mrow8[:], mrowg[p].unsqueeze(0).broadcast_to([128, G * N]).rearrange("q (g n) -> q g n", g=G)).then_inc(S["mask_in"], 16)
                sp.dma_start(mcol8[:], mcolg[p]).then_inc(S["mask_in"], 16)

            def load(signal, dst, src):
                sp.dma_start(dst, src).then_inc(S[signal], 16)

            def load_weight(signal, dst, src):
                load(signal, dst, src.rearrange("(c p) n -> p c n", p=128))

            def load_row(signal, dst, src):
                load(signal, dst, src.broadcast_to([128, D]))

            load_x0T(0)
            load_weight("in_m", wm_in, wm)
            load_weight("in_p", wq_in, wq)
            load_weight("in_p", wk_in, wk)
            load("in_p", vec_in[:], columns)
            load_adj(adj0, "adj0_in", 0)
            load_adj(adj0T, "adj0T_in", 0, adjt)
            load_weight("in_q", wkv_in, wkvT)
            load("in_q", kab_col[:], kab.unsqueeze(0).broadcast_to([128, 1]))
            load_x0(0)
            load_weight("in_a", wv_in, wvT)
            load_row("in_a", bv_bc[:], bv.unsqueeze(0))
            load_adj(adj1T, "adj1T_in", 0, adjt)
            load("in_h", wqkv_in, wqkv.rearrange("(c p) (i n) -> p c i n", p=128, i=3))
            load_weight("in_h", wo_in, wout)
            load_row("in_h", bout_bc[:], bout.unsqueeze(0))
            load_adj(adj2, "adj2_in", 0)
            load_mask(0)
            for k in range(HOPS):
                load_weight("in_k", wk3_in[:, k], wk3[k])
                load_row("in_k", bk3_in[:, k], bk3[k:k + 1, :])
            load_adj(adj3, "adj3_in", 0)

            def gate():
                sp.sem_inc(S["gate"], 1)

            def step(t, stages, more):
                if "m" in stages and "m" in more:
                    sp.wait_ge(S["m_deg"], 3 * t + 1)
                    gate()
                    load_adj(adj0, "adj0_in", t + 1)
                if "h" in stages and "h" in more:
                    p = t - 2
                    sp.wait_ge(S["h_mrow"], 2 * (p + 1))
                    gate()
                    load_mask(p + 1)
                    sp.wait_ge(S["h_ex"], p + 1)
                    gate()
                    sp.wait_ge(S["h_sum"], p + 1)
                    gate()
                    load_adj(adj2, "adj2_in", p + 1)
                if "m" in stages and "m" in more:
                    sp.wait_ge(S["m_xhi"], t + 1)
                    gate()
                    sp.wait_ge(S["m_xlo"], t + 1)
                    gate()
                    load_x0T(t + 1)
                if "k" in stages and "k" in more:
                    p = t - 3
                    sp.wait_ge(S["k_w"], 2 * (p + 1))
                    gate()
                    load_adj(adj3, "adj3_in", p + 1)
                if "a" in stages and "a" in more:
                    p = t - 1
                    sp.wait_ge(S["a_p"], p + 1)
                    gate()
                    load_adj(adj1T, "adj1T_in", p + 1, adjt)
                if "m" in stages and "m" in more:
                    sp.wait_ge(S["m_Ahi"], t + 1)
                    gate()
                    sp.wait_ge(S["m_Alo"], t + 1)
                    gate()
                    load_adj(adj0T, "adj0T_in", t + 1, adjt)
                    sp.wait_ge(S["m_sum"], 2 * (t + 1))
                    gate()
                    load_x0(t + 1)
                if "k" in stages:
                    p = t - 3
                    sp.wait_ge(S["y_made"], 2 * (p + 1))
                    gate()
                    sp.dma_start(og[p], y[:]).then_inc(S["y_out"], 16)

            for t in range(4):
                step(t, stages_at(t), "mahk")
            with sp.Fori(4, pairs - 1) as t:
                step(t, "mahk", "mahk")
            for t in range(pairs - 1, steps):
                more = "".join(s for s, n in STAGE.items() if t + 1 - n < pairs)
                step(t, stages_at(t), more)
            sp.wait_ge(S["y_out"], 16 * pairs)

        loads = {"m": 1, "p": 3, "q": 2, "a": 2, "h": 3, "k": 2 * HOPS}

        @block.gpsimd
        def _(pool):
            pool.memset(ident[:], 0.0).then_inc(S["ident"], 1)
            pool.memset(minus_half[:], -0.5).then_inc(S["halves"], 1)
            pool.memset(ones[:], 1.0).then_inc(S["halves"], 1)
            pool.wait_ge(S["ident"], 1)
            pool.affine_select(out=ident[:], in_=ident[:], compare_op=ALU.not_equal, fill=1.0, base=0,
                               pattern=[[-1, 128]], channel_multiplier=1).then_inc(S["ident"], 1)
            pool.wait_ge(S["halves"], 2)

            def gate():
                pool.sem_inc(S["gate"], 1)

            def inv_std(s, n):
                pool.wait_ge(S[s + "_mv"], 2 * n)
                gate()
                pool.tensor_scalar(ve[s][:], mv[s][:, :, 1], EPS_LN, None, ALU.add).then_inc(S[s + "_ve"], 1)
                pool.wait_ge(S[s + "_ve"], n)
                pool.tensor_tensor(rstd[s][:], ve[s][:], minus_half[:], ALU.pow).then_inc(S[s + "_rstd"], 1)

            def step(t, stages):
                def made(s):
                    return t - STAGE[s] + 1

                def later(s):
                    return had(t, s)

                if "h" in stages:
                    pool.wait_ge(S["mask_in"], 32 * made("h"))
                    if later("h"):
                        pool.wait_ge(S["h_mix"], made("h") - 1)
                        pool.wait_ge(S["h_mneg"], made("h") - 1)
                    gate()
                    pool.tensor_copy(mrow[:], mrow8[:]).then_inc(S["h_mrow"], 1)
                    pool.tensor_copy(mcol[:], mcol8[:]).then_inc(S["h_mrow"], 1)
                    pool.wait_ge(S["h_mrow"], 2 * made("h"))
                    gate()
                    for g in range(G):
                        pool.tensor_scalar(m2[:, g], mrow[:, g], mcol[:, g:g + 1], None, ALU.mult).then_inc(S["h_m2"], 1)
                    pool.wait_ge(S["h_m2"], 2 * made("h"))
                    if later("h"):
                        pool.wait_ge(S["h_S1o_read"], made("h") - 1)
                    gate()
                    pool.tensor_scalar(mneg[:], m2[:], BIG, BIG, ALU.mult, ALU.subtract).then_inc(S["h_mneg"], 1)
                    pool.wait_ge(S["h_ex"], made("h"))
                    if later("h"):
                        pool.wait_ge(S["h_mix"], made("h") - 1)
                    pool.tensor_tensor(exs[:], ex[:], adj2[:], ALU.add).then_inc(S["h_sum"], 1)
                if "m" in stages:
                    pool.wait_ge(S["m_Ahi"], made("m"))
                    pool.tensor_tensor(adjm[1][:], adj0T[:], as_f32(adjm[0][:]), ALU.subtract).then_inc(S["m_Alo"], 1)
                if "h" in stages:
                    pool.wait_ge(S["h_sum"], made("h"))
                    pool.wait_ge(S["h_m2"], 2 * made("h"))
                    if later("h"):
                        pool.wait_ge(S["h_p"], 4 * (made("h") - 1))
                    pool.tensor_tensor(mix[:], exs[:], m2[:], ALU.mult).then_inc(S["h_mix"], 1)
                if "a" in stages:
                    pool.wait_ge(S["x1_made"], 2 * made("a"))
                    if later("a"):
                        pool.wait_ge(S["a_h"], 2 * (made("a") - 1))
                    pool.tensor_tensor(x1b[:], x1[:], bv_bc[:].unsqueeze(1).broadcast_to([128, G, D]), ALU.add).then_inc(S["x1_bias"], 1)
                    pool.wait_ge(S["a_S_read"], made("a"))
                    pool.wait_ge(S["adj1T_in"], 16 * made("a"))
                    if later("a"):
                        pool.wait_ge(S["a_plo"], made("a") - 1)
                    pool.tensor_tensor(ap[:], ae[:], adj1T[:], ALU.mult).then_inc(S["a_p"], 1)
                    pool.wait_ge(S["a_phi"], made("a"))
                    pool.tensor_tensor(aP[1][:], ap[:], as_f32(aP[0][:]), ALU.subtract).then_inc(S["a_plo"], 1)
                if "h" in stages:
                    pool.wait_ge(S["x2_made"], 2 * made("h"))
                    if later("h"):
                        pool.wait_ge(S["h_h"], 2 * (made("h") - 1))
                    pool.tensor_tensor(x2b[:], x2[:], bout_bc[:].unsqueeze(1).broadcast_to([128, G, D]), ALU.add).then_inc(S["x2_bias"], 1)
                if "a" in stages:
                    inv_std("a", made("a"))
                if "h" in stages:
                    inv_std("h", made("h"))
                if "k" in stages:
                    inv_std("k", made("k"))
                if "m" in stages:
                    inv_std("m", made("m"))

            step(0, stages_at(0))
            pool.wait_ge(S["in_a"], 16 * loads["a"])
            step(1, stages_at(1))
            pool.wait_ge(S["in_h"], 16 * loads["h"])
            step(2, stages_at(2))
            step(3, stages_at(3))
            with pool.Fori(4, pairs) as t:
                step(t, "mahk")
            for t in range(pairs, steps):
                step(t, stages_at(t))

        @block.tensor
        def _(pe):
            def product3(o, lhs, rhs, first=True, last=True, skip=False):
                pe.matmul(o, lhs[0], rhs[0], start=first, stop=False, skip_group_check=skip)
                pe.matmul(o, lhs[0], rhs[1], start=False, stop=False, skip_group_check=skip)
                return pe.matmul(o, lhs[1], rhs[0], start=False, stop=last, skip_group_check=skip)

            def products_A():
                pe.wait_ge(S["in_p"], 16 * loads["p"])
                for c in range(C):
                    for o in range(C):
                        pe.matmul(bank_A[:, c * D:(c + 1) * D], wq_in[:, o, c * 128:(c + 1) * 128], wk_in[:, o],
                                  start=o == 0, stop=o == C - 1)

            def products_rows():
                pe.wait_ge(S["in_q"], 16 * loads["q"])
                for c in range(C):
                    for o in range(C):
                        pe.matmul(bank_rows[:, c * 128:(c + 1) * 128], wq_in[:, o, c * 128:(c + 1) * 128],
                                  bk_in[:, o].broadcast_to([128, 128]), start=o == 0, stop=o == C - 1)
                for c in range(C):
                    for o in range(C):
                        pe.matmul(bank_cols[:, c:c + 1], wk_in[:, o, c * 128:(c + 1) * 128], bq_in[:, o],
                                  start=o == 0, stop=o == C - 1)
                    for i, v in enumerate((awi_in, awj_in)):
                        for o in range(C):
                            pe.matmul(bank_cols[:, (1 + i) * C + c:(1 + i) * C + c + 1], wkv_in[:, o, c * 128:(c + 1) * 128], v[:, o],
                                      start=o == 0, stop=o == C - 1)
                for o in range(C):
                    pe.matmul(bank_cols[:, 3 * C:3 * C + 1], bq_in[:, o].broadcast_to([128, 128]), bk_in[:, o],
                              start=o == 0, stop=o == C - 1)
                for i, v in enumerate((awj_in, awi_in)):
                    for o in range(C):
                        mm = pe.matmul(bank_cols[:, 3 * C + 1:3 * C + 2], kbv_in[:, o].broadcast_to([128, 128]), v[:, o],
                                       start=i == 0 and o == 0, stop=i == 1 and o == C - 1)
                mm.then_inc(S["weights_mm"], 1)

            def step(t, stages, before):
                def made(s):
                    return t - STAGE[s] + 1

                def free(name):
                    old, ago = former(name, stages, before)
                    return old and (S[LAST_READ.get(old, old) + "_read"], made(old[0]) - ago)

                def bank_of(name):
                    return bank[BANK[name]]

                def claim(name):
                    if was := free(name):
                        pe.wait_ge(*was)

                def transposes(name, src):
                    if was := free(name):
                        pe.wait_ge(*was)
                    b = bank_of(name).rearrange("p (c g n) -> p c g n", c=C, g=G)
                    for c in range(C):
                        for g in range(G):
                            mm = pe.transpose(b[:, c, g], src[:, g, c * 128:(c + 1) * 128], ident[:])
                    mm.then_inc(S[name + "_made"], 1)

                def part(pair, *index):
                    return tuple(q[index] for q in pair)

                def node_part(s, c, g):
                    return part(xT[s], slice(None), c, slice(g * N, (g + 1) * N))

                def heads_qk(name, i, half):
                    if was := free(name):
                        pe.wait_ge(*was)
                    b = bank_of(name).rearrange("p (m n) -> p m n", m=2)
                    for m in range(2):
                        col = (2 * half + m) * 128
                        for c in range(C):
                            mm = product3(b[:, m], part(Wqkv, slice(None), c, i, slice(col, col + 128)),
                                          part(xT["h"], slice(None), c), c == 0, c == C - 1)
                    mm.then_inc(S[name + "_made"], 1)

                def heads_scores(g):
                    if was := free(f"h_S{g}e"):
                        pe.wait_ge(*was)
                    be = bank_of(f"h_S{g}e")
                    if was := free(f"h_S{g}o"):
                        pe.wait_ge(*was)
                    bo = bank_of(f"h_S{g}o")
                    for m in range(HEADS // 2):
                        for odd, b in ((0, be), (1, bo)):
                            rows = slice(64 * odd, 64 * odd + 64)
                            mm = pe.matmul(b[:, m * N:(m + 1) * N], qT[rows, m, g * N:(g + 1) * N],
                                           kT[rows, m, g * N:(g + 1) * N], start=True, stop=True)
                            if m == HEADS // 2 - 1:
                                mm.then_inc(S[f"h_S{g}{'eo'[odd]}_made"], 1)

                def heads_v(g):
                    for c in range(C):
                        mm = product3(bank_of(f"h_v{g}")[:], node_part("h", c, g), part(Wqkv, every, c, 2), c == 0, c == C - 1)
                    mm.then_inc(S[f"h_v{g}_made"], 1)

                def heads_transpose(g, i):
                    name = f"h_T{g}{'eo'[i]}"
                    if was := free(name):
                        pe.wait_ge(*was)
                    pe.wait_ge(S["h_p"], 4 * (made("h") - 1) + 2 * g + i + 1)
                    for m in range(4):
                        mm = pe.transpose(bank_of(name)[:, m * N:(m + 1) * N], hs[:, g, 4 * i + m], ident[:])
                    mm.then_inc(S[name + "_made"], 1)

                def heads_values(g):
                    if was := free(f"h_PV{g}"):
                        pe.wait_ge(*was)
                    b = bank_of(f"h_PV{g}")
                    pe.wait_ge(S[f"h_T{g}e_read"], made("h"))
                    pe.wait_ge(S[f"h_T{g}o_read"], made("h"))
                    for m in range(HEADS // 2):
                        for odd in range(2):
                            h = 2 * m + odd
                            mm = pe.matmul(b[64 * odd:64 * odd + 64, m * N:(m + 1) * N],
                                           hv[:, g, h * DH:(h + 1) * DH], pT[:, g, 4 * odd + m],
                                           start=True, stop=True)
                    mm.then_inc(S[f"h_PV{g}_made"], 1)

                def heads_out(g):
                    pe.wait_ge(S[f"h_PV{g}_read"], made("h"))
                    for m in range(INNER // 128):
                        mm = product3(bank_of("h_out")[:, g * D:(g + 1) * D], part(oT, every, g, m), part(Wo, every, m),
                                      m == 0, m == INNER // 128 - 1)
                    if g == G - 1:
                        mm.then_inc(S["h_out_made"], 1)

                def hop_two(g):
                    for c in range(C):
                        mm = product3(bank_of(f"k_y2{g}")[:, 0:D + 2], node_part("k", c, g), part(Wy2, every, c), c == 0, c == C - 1)
                    mm.then_inc(S[f"k_y2{g}_made"], 1)

                def hops_zero_one(g):
                    for c in range(C):
                        mm = product3(bank_of(f"k_y01{g}")[:], node_part("k", c, g), part(Wy01, every, c), c == 0, c == C - 1)
                    mm.then_inc(S[f"k_y01{g}_made"], 1)

                def hop(g, name, ready, columns, features):
                    pe.wait_ge(S[ready], made("k"))
                    product3(bank_of(f"k_y01{g}")[:, columns], part(kT_, every, g), part(features, every, g), first=False,
                             skip=True).then_inc(S[f"{name}{g}_made"], 1)

                def mean_weights(g):
                    for c in range(C):
                        mm = product3(bank_of(f"m_xW{g}")[:], node_part("m", c, g), part(Wm, every, c), c == 0, c == C - 1)
                    mm.then_inc(S[f"m_xW{g}_made"], 1)

                def weights(s):
                    if isinstance(t, int) and t == STAGE[s]:
                        pe.wait_ge(S["weights_lo"], WEIGHTS[s])

                if "h" in stages:
                    weights("h")
                    pe.wait_ge(S["a_x2T_read"], made("h"))
                    heads_qk("h_k0", 1, 0)
                    heads_qk("h_k1", 1, 1)
                    heads_qk("h_q0", 0, 0)
                    heads_qk("h_q1", 0, 1)
                if "k" in stages:
                    pe.wait_ge(S["x3_made"], 2 * made("k"))
                    transposes("k_xT", x3)
                if "h" in stages:
                    claim("h_v0")
                    heads_v(0)
                if "a" in stages:
                    pe.wait_ge(S["x1_made"], 2 * made("a"))
                    transposes("a_xT", x1)
                if "k" in stages:
                    claim("k_y20")
                    weights("k")
                    pe.wait_ge(S["k_xT_read"], made("k"))
                    hop_two(0)
                    claim("k_y21")
                    hop_two(1)
                if "h" in stages:
                    for n in ("h_q0", "h_q1", "h_k0", "h_k1"):
                        pe.wait_ge(S[n + "_read"], made("h"))
                    heads_scores(0)
                if "k" in stages:
                    claim("k_sj")
                    pe.wait_ge(S["k_diag"], made("k"))
                    for g in range(G):
                        mm = pe.matmul(bank_of("k_sj")[:, g * N:(g + 1) * N], ones[:], diag[:, g], start=True, stop=True)
                    mm.then_inc(S["k_sj_made"], 1)
                if "a" in stages:
                    claim("a_G")
                    weights("a")
                    pe.wait_ge(S["a_xlo"], made("a"))
                    for o in range(C):
                        for c in range(C):
                            mm = product3(bank_of("a_G")[:, o * G * N:(o + 1) * G * N], part(A, every, c, slice(o * 128, (o + 1) * 128)),
                                          part(xT["a"], every, c), c == 0, c == C - 1)
                    mm.then_inc(S["a_G_made"], 1)
                if "h" in stages:
                    heads_scores(1)
                if "a" in stages:
                    claim("a_v")
                    for g in range(G):
                        for c in range(C):
                            mm = product3(bank_of("a_v")[:, g * D:(g + 1) * D], node_part("a", c, g), part(Wv, every, c), c == 0, c == C - 1)
                    mm.then_inc(S["a_v_made"], 1)
                if "k" in stages:
                    claim("k_y010")
                    hops_zero_one(0)
                if "a" in stages:
                    claim("a_S")
                    b = bank_of("a_S")
                    for c in range(C):
                        product3(b[:, 0:G * N], part(Wrow, every, c), part(xT["a"], every, c), c == 0, False, True)
                    pe.wait_ge(S["a_xT_read"], made("a"))
                    pe.wait_ge(S["a_G_read"], made("a"))
                    for g in range(G):
                        for c in range(C):
                            mm = pe.matmul(b[:, g * N:(g + 1) * N], x1T[:, c, g * N:(g + 1) * N], GT[:, c, g * N:(g + 1) * N],
                                           start=False, stop=c == C - 1, skip_group_check=True)
                    mm.then_inc(S["a_S_made"], 1)
                if "k" in stages:
                    claim("k_y011")
                    hops_zero_one(1)
                if "h" in stages:
                    claim("h_v1")
                    heads_v(1)
                if "m" in stages:
                    claim("m_xW0")
                    weights("m")
                    pe.wait_ge(S["m_xlo"], made("m"))
                    mean_weights(0)
                if "k" in stages:
                    claim("k_T")
                    pe.wait_ge(S["k_tr"], 2 * made("k"))
                    for g in range(G):
                        mm = pe.transpose(bank_of("k_T")[:, g * N:(g + 1) * N], kt[:, g], ident[:])
                    mm.then_inc(S["k_T_made"], 1)
                if "h" in stages:
                    heads_transpose(0, 0)
                    heads_transpose(0, 1)
                    heads_transpose(1, 0)
                if "a" in stages:
                    claim("a_PV0")
                    pe.wait_ge(S["a_plo"], made("a"))
                    pe.wait_ge(S["a_v_read"], made("a"))
                    product3(bank_of("a_PV0")[:, 0:D + 2], part(aP, every, 0), part(av, every, 0)).then_inc(S["a_PV0_made"], 1)
                    claim("a_PV1")
                    product3(bank_of("a_PV1")[:, 0:D + 2], part(aP, every, 1), part(av, every, 1)).then_inc(S["a_PV1_made"], 1)
                if "k" in stages:
                    pe.wait_ge(S["k_T_read"], made("k"))
                    hop(0, "k_Ty", "k_y20_read", slice(D, 2 * D), ky2)
                    hop(1, "k_Ty", "k_y21_read", slice(D, 2 * D), ky2)
                if "h" in stages:
                    heads_transpose(1, 1)
                    pe.wait_ge(S["h_v0_read"], made("h"))
                    heads_values(0)
                    pe.wait_ge(S["h_v1_read"], made("h"))
                    heads_values(1)
                if "k" in stages:
                    hop(0, "k_TT", "k_Ty0_read", slice(0, D), ky1)
                    hop(1, "k_TT", "k_Ty1_read", slice(0, D), ky1)
                if "m" in stages:
                    claim("m_xW1")
                    mean_weights(1)
                if "h" in stages:
                    claim("h_out")
                    heads_out(0)
                if "a" in stages:
                    pe.wait_ge(S["x2_made"], 2 * made("a"))
                    transposes("a_x2T", x2)
                if "h" in stages:
                    heads_out(1)
                if "m" in stages:
                    pe.wait_ge(S["m_Alo"], made("m"))
                    pe.wait_ge(S["m_xW0_read"], made("m"))
                    product3(bank_of("m_xW0")[:, D:2 * D], part(adjm, every, 0), part(my, every, 0), skip=True).then_inc(S["m_ag0_made"], 1)
                    pe.wait_ge(S["m_xW1_read"], made("m"))
                    product3(bank_of("m_xW1")[:, D:2 * D], part(adjm, every, 1), part(my, every, 1), skip=True).then_inc(S["m_ag1_made"], 1)

            products_A()
            step(0, stages_at(0), None)
            products_rows()
            for t in range(1, 4):
                step(t, stages_at(t), stages_at(t - 1))
            with pe.Fori(4, pairs) as t:
                step(t, "mahk", "mahk")
            for t in range(pairs, steps):
                step(t, stages_at(t), stages_at(t - 1))

        @block.scalar
        def _(act):
            def copy(dst, src):
                return act.activation(dst, src, ACT.Copy)

            def weights_mean():
                act.wait_ge(S["in_m"], 16 * loads["m"])
                copy(Wm[0][:], wm_in).then_inc(S["weights_hi"], 1)

            def weights_products():
                act.wait_ge(S["weights_mm"], 1)
                copy(A[0][:], chunks(bank_A)).then_inc(S["weights_hi"], 1)
                copy(Wrow[0][:], bank_rows[:, 0:D].rearrange("p (c n) -> p c n", c=C)).then_inc(S["weights_hi"], 1)
                for i in range(2):
                    copy(Wy2[0][:, :, D + i:D + i + 1], bank_cols[:, (1 + i) * C:(2 + i) * C].unsqueeze(2)).then_inc(S["weights_hi"], 1)

            def weights_values():
                act.wait_ge(S["in_a"], 16 * loads["a"])
                copy(Wv[0][:], wv_in).then_inc(S["weights_hi"], 1)
                act.wait_ge(S["halves"], 2)
                copy(av[0][:, :, D:D + 2], ones[:, 0:2 * G].rearrange("p (g n) -> p g n", g=G)).then_inc(S["weights_hi"], 1)

            def weights_heads():
                act.wait_ge(S["in_h"], 16 * loads["h"])
                copy(Wqkv[0][:], wqkv_in).then_inc(S["weights_hi"], 1)
                act.activation(Wo[0][:], wo_in, ACT.Copy, scale=LA).then_inc(S["weights_hi"], 1)

            def weights_hops():
                act.wait_ge(S["in_k"], 16 * loads["k"])
                for i in range(2):
                    copy(Wy01[0][:, :, i * D:(i + 1) * D], wk3_in[:, i]).then_inc(S["weights_hi"], 1)
                copy(Wy2[0][:, :, 0:D], wk3_in[:, 2]).then_inc(S["weights_hi"], 1)

            def step(t, stages):
                def made(s):
                    return t - STAGE[s] + 1

                def later(s):
                    return had(t, s)

                def heads_exp(g, i):
                    act.wait_ge(S["h_nmx"], 4 * (made("h") - 1) + 2 * g + i + 1)
                    for h in range(4 * i, 4 * i + 4):
                        act.activation(hs[:, g, h], hs[:, g, h], ACT.Exp, bias=hnmx[:, g, h:h + 1], scale=DH ** -0.5,
                                       accum_out=hden[:, g, h:h + 1]).then_inc(S["h_e"], 1)

                if "h" in stages:
                    act.wait_ge(S["h_k0_made"], made("h"))
                    if later("h"):
                        act.wait_ge(S["h_S1o_made"], made("h") - 1)
                        act.wait_ge(S["h_S1e_made"], made("h") - 1)
                    copy(kT[:, 0:2], chunks(bank[BANK["h_k0"]])).then_inc(S["h_k0_read"], 1)
                if "m" in stages:
                    act.wait_ge(S["x0T_in"], 16 * made("m"))
                    if later("m"):
                        act.wait_ge(S["m_xW1_made"], made("m") - 1)
                    copy(xT["m"][0][:], x0T[:]).then_inc(S["m_xhi"], 1)
                if isinstance(t, int) and t == 0:
                    weights_values()
                if "h" in stages:
                    act.wait_ge(S["h_q0_made"], made("h"))
                    if later("h"):
                        act.wait_ge(S["h_S1o_made"], made("h") - 1)
                        act.wait_ge(S["h_S1e_made"], made("h") - 1)
                    copy(qT[:, 0:2], chunks(bank[BANK["h_q0"]])).then_inc(S["h_q0_read"], 1)
                    act.wait_ge(S["h_k1_made"], made("h"))
                    if later("h"):
                        act.wait_ge(S["h_S1o_made"], made("h") - 1)
                        act.wait_ge(S["h_S1e_made"], made("h") - 1)
                    copy(kT[:, 2:4], chunks(bank[BANK["h_k1"]])).then_inc(S["h_k1_read"], 1)
                if "k" in stages:
                    act.wait_ge(S["k_xT_made"], made("k"))
                    if later("k"):
                        act.wait_ge(S["k_y011_made"], made("k") - 1)
                    copy(xT["k"][0][:], chunks(bank[BANK["k_xT"]])).then_inc(S["k_xhi"], 1)
                if "h" in stages:
                    act.wait_ge(S["h_q1_made"], made("h"))
                    if later("h"):
                        act.wait_ge(S["h_S1o_made"], made("h") - 1)
                        act.wait_ge(S["h_S1e_made"], made("h") - 1)
                    copy(qT[:, 2:4], chunks(bank[BANK["h_q1"]])).then_inc(S["h_q1_read"], 1)
                    act.wait_ge(S["h_v0_made"], made("h"))
                    if later("h"):
                        act.wait_ge(S["h_PV0_made"], made("h") - 1)
                    copy(hv[:, 0], bank[BANK["h_v0"]][:]).then_inc(S["h_v0_read"], 1)
                if "a" in stages:
                    act.wait_ge(S["a_xT_made"], made("a"))
                    if later("a"):
                        act.wait_ge(S["a_S_made"], made("a") - 1)
                    copy(xT["a"][0][:], chunks(bank[BANK["a_xT"]])).then_inc(S["a_xhi"], 1)
                if isinstance(t, int) and t == 2:
                    weights_hops()
                if "m" in stages:
                    act.wait_ge(S["adj0T_in"], 16 * made("m"))
                    if later("m"):
                        act.wait_ge(S["m_ag1_made"], made("m") - 1)
                    copy(adjm[0][:], adj0T[:]).then_inc(S["m_Ahi"], 1)
                if "h" in stages:
                    act.wait_ge(S["adj2_in"], 16 * made("h"))
                    if later("h"):
                        act.wait_ge(S["h_sum"], made("h") - 1)
                    act.activation(ex[:], adj2[:], ACT.Exp, scale=-1.0).then_inc(S["h_ex"], 1)
                if "k" in stages:
                    act.wait_ge(S["k_y20_made"], made("k"))
                    if later("k"):
                        act.wait_ge(S["k_Ty0_made"], made("k") - 1)
                    copy(ky2[0][:, 0], bank[BANK["k_y20"]][:, 0:D]).then_inc(S["k_yhi"], 1)
                    act.wait_ge(S["k_y21_made"], made("k"))
                    if later("k"):
                        act.wait_ge(S["k_Ty1_made"], made("k") - 1)
                    copy(ky2[0][:, 1], bank[BANK["k_y21"]][:, 0:D]).then_inc(S["k_yhi"], 1)
                if "a" in stages:
                    act.wait_ge(S["a_xlo"], made("a"))
                    if later("a"):
                        act.wait_ge(S["a_S_made"], made("a") - 1)
                    copy(x1T[:], chunks(bank[BANK["a_xT"]])).then_inc(S["a_xT_read"], 1)
                if "h" in stages:
                    heads_exp(0, 0)
                if "a" in stages:
                    act.wait_ge(S["a_G_made"], made("a"))
                    if later("a"):
                        act.wait_ge(S["a_S_made"], made("a") - 1)
                    for c in range(C):
                        last = act.activation(GT[:, c], bank[BANK["a_G"]][:, c * G * N:(c + 1) * G * N], ACT.Identity, bias=u_col[:, c:c + 1])
                    last.then_inc(S["a_G_read"], 1)
                if "k" in stages:
                    act.wait_ge(S["k_leaky"], made("k"))
                    if later("k"):
                        act.wait_ge(S["k_w"], 2 * (made("k") - 1))
                    act.activation(kz[:], kl[:], ACT.Exp).then_inc(S["k_e"], 1)
                if "h" in stages:
                    heads_exp(0, 1)
                if "a" in stages:
                    act.wait_ge(S["a_v_made"], made("a"))
                    if later("a"):
                        act.wait_ge(S["a_PV1_made"], made("a") - 1)
                    copy(av[0][:, :, 0:D], bank[BANK["a_v"]][:].rearrange("p (g n) -> p g n", g=G)).then_inc(S["a_vhi"], 1)
                if "h" in stages:
                    heads_exp(1, 0)
                if "a" in stages:
                    act.wait_ge(S["a_S_made"], made("a"))
                    if later("a"):
                        act.wait_ge(S["a_p"], made("a") - 1)
                    act.activation(ae[:], bank[BANK["a_S"]][:, 0:G * N].rearrange("p (g n) -> p g n", g=G), ACT.Exp,
                                   bias=cq_col[:, 0:1]).then_inc(S["a_S_read"], 1)
                if "h" in stages:
                    heads_exp(1, 1)
                if "a" in stages:
                    act.wait_ge(S["a_p"], made("a"))
                    if later("a"):
                        act.wait_ge(S["a_PV1_made"], made("a") - 1)
                    copy(aP[0][:], ap[:]).then_inc(S["a_phi"], 1)
                if "k" in stages:
                    act.wait_ge(S["k_T_made"], made("k"))
                    if later("k"):
                        act.wait_ge(S["k_TT1_made"], made("k") - 1)
                    copy(kT_[0][:], bank[BANK["k_T"]][:, 0:G * N].rearrange("p (g n) -> p g n", g=G)).then_inc(S["k_Thi"], 1)
                if "h" in stages:
                    act.wait_ge(S["h_v1_made"], made("h"))
                    if later("h"):
                        act.wait_ge(S["h_PV1_made"], made("h") - 1)
                    copy(hv[:, 1], bank[BANK["h_v1"]][:]).then_inc(S["h_v1_read"], 1)
                    if later("h"):
                        act.wait_ge(S["h_PV0_made"], made("h") - 1)
                    act.wait_ge(S["h_T0e_made"], made("h"))
                    copy(pT[:, 0, 0:4], by_four(bank[BANK["h_T0e"]])).then_inc(S["h_T0e_read"], 1)
                    if later("h"):
                        act.wait_ge(S["h_PV0_made"], made("h") - 1)
                    act.wait_ge(S["h_T0o_made"], made("h"))
                    copy(pT[:, 0, 4:8], by_four(bank[BANK["h_T0o"]])).then_inc(S["h_T0o_read"], 1)
                    if later("h"):
                        act.wait_ge(S["h_PV1_made"], made("h") - 1)
                    act.wait_ge(S["h_T1e_made"], made("h"))
                    copy(pT[:, 1, 0:4], by_four(bank[BANK["h_T1e"]])).then_inc(S["h_T1e_read"], 1)
                if "k" in stages:
                    act.wait_ge(S["k_Ty0_made"], made("k"))
                    if later("k"):
                        act.wait_ge(S["k_TT0_made"], made("k") - 1)
                    copy(ky1[0][:, 0], bank[BANK["k_y010"]][:, D:2 * D]).then_inc(S["k_yhi"], 1)
                if "m" in stages:
                    act.wait_ge(S["m_xW0_made"], made("m"))
                    if later("m"):
                        act.wait_ge(S["m_sum"], 2 * (made("m") - 1))
                        act.wait_ge(S["m_ag0_made"], made("m") - 1)
                    copy(mx[:, 0], bank[BANK["m_xW0"]][:, 0:D])
                    copy(my[0][:, 0], bank[BANK["m_xW0"]][:, D:2 * D]).then_inc(S["m_yhi"], 1)
                if "h" in stages:
                    if later("h"):
                        act.wait_ge(S["h_PV1_made"], made("h") - 1)
                    act.wait_ge(S["h_T1o_made"], made("h"))
                    copy(pT[:, 1, 4:8], by_four(bank[BANK["h_T1o"]])).then_inc(S["h_T1o_read"], 1)
                if "k" in stages:
                    act.wait_ge(S["k_Ty1_made"], made("k"))
                    if later("k"):
                        act.wait_ge(S["k_TT1_made"], made("k") - 1)
                    copy(ky1[0][:, 1], bank[BANK["k_y011"]][:, D:2 * D]).then_inc(S["k_yhi"], 1)
                if "h" in stages:
                    act.wait_ge(S["h_PV0_made"], made("h"))
                    if later("h"):
                        act.wait_ge(S["h_out_made"], made("h") - 1)
                    copy(oT[0][:, 0], by_four(bank[BANK["h_PV0"]])).then_inc(S["h_ohi"], 1)
                    act.wait_ge(S["h_PV1_made"], made("h"))
                    if later("h"):
                        act.wait_ge(S["h_out_made"], made("h") - 1)
                    copy(oT[0][:, 1], by_four(bank[BANK["h_PV1"]])).then_inc(S["h_ohi"], 1)
                if "m" in stages:
                    act.wait_ge(S["m_xW1_made"], made("m"))
                    if later("m"):
                        act.wait_ge(S["m_sum"], 2 * (made("m") - 1))
                        act.wait_ge(S["m_ag1_made"], made("m") - 1)
                    copy(mx[:, 1], bank[BANK["m_xW1"]][:, 0:D])
                    copy(my[0][:, 1], bank[BANK["m_xW1"]][:, D:2 * D]).then_inc(S["m_yhi"], 1)
                if isinstance(t, int) and t == 0:
                    weights_heads()
                if isinstance(t, int) and t == 0:
                    weights_products()
                if "a" in stages:
                    act.wait_ge(S["a_x2T_made"], made("a"))
                    if "h" in stages:
                        act.wait_ge(S["h_v1_made"], made("h"))
                    copy(xT["h"][0][:], chunks(bank[BANK["a_x2T"]])).then_inc(S["a_x2hi"], 1)

            weights_mean()
            for t in range(4):
                step(t, stages_at(t))
            with act.Fori(4, pairs) as t:
                step(t, "mahk")
            for t in range(pairs, steps):
                step(t, stages_at(t))

        @block.vector
        def _(dve):
            def gate():
                dve.sem_inc(S["gate"], 1)

            def copy(dst, src):
                return dve.tensor_copy(dst, src)

            def lo(pair, src, *index):
                dve.tensor_tensor(pair[1][index], src, as_f32(pair[0][index]), ALU.subtract).then_inc(S["weights_lo"], 1)

            def weights_mean():
                dve.wait_ge(S["weights_hi"], WEIGHTS["m"])
                lo(Wm, wm_in, every)

            def weights_products():
                dve.wait_ge(S["weights_hi"], WEIGHTS["h"])
                dve.tensor_copy(u_col[:], bank_cols[:, 0:C]).then_inc(S["weights_ev"], 1)
                dve.tensor_copy(cq_col[:], bank_cols[:, 3 * C:3 * C + 1]).then_inc(S["weights_ev"], 1)
                dve.tensor_scalar(ke_col[:], bank_cols[:, 3 * C + 1:3 * C + 2], kab_col[:, 0:1], None, ALU.add).then_inc(S["weights_ev"], 1)
                dve.wait_ge(S["weights_ev"], 3)
                lo(A, chunks(bank_A), every)
                lo(Wrow, bank_rows[:, 0:D].rearrange("p (c n) -> p c n", c=C), every)
                for i in range(2):
                    lo(Wy2, bank_cols[:, (1 + i) * C:(2 + i) * C].unsqueeze(2), every, every, slice(D + i, D + i + 1))

            def weights_values():
                dve.wait_ge(S["weights_hi"], WEIGHTS["v"])
                lo(Wv, wv_in, every)
                lo(av, ones[:, 0:2 * G].rearrange("p (g n) -> p g n", g=G), every, every, slice(D, D + 2))

            def weights_heads():
                dve.wait_ge(S["weights_hi"], WEIGHTS["h"])
                lo(Wqkv, wqkv_in, every)
                dve.scalar_tensor_tensor(out=Wo[1][:], in0=wo_in, scalar=LA, in1=as_f32(Wo[0][:]), op0=ALU.mult,
                                         op1=ALU.subtract).then_inc(S["weights_lo"], 1)

            def weights_hops():
                dve.wait_ge(S["in_k"], 16 * loads["k"])
                dve.tensor_tensor(bk3_bc[:], bk3_in[:, 0], bk3_in[:, 1], ALU.add).then_inc(S["weights_ev"], 1)
                dve.wait_ge(S["weights_ev"], 4)
                dve.tensor_tensor(bk3_bc[:], bk3_bc[:], bk3_in[:, 2], ALU.add).then_inc(S["weights_ev"], 1)
                dve.wait_ge(S["weights_ev"], 5)
                dve.wait_ge(S["weights_hi"], WEIGHTS["k"])
                lo(Wy01, wk3_in[:, 0], every, every, slice(0, D))
                lo(Wy01, wk3_in[:, 1], every, every, slice(D, 2 * D))
                lo(Wy2, wk3_in[:, 2], every, every, slice(0, D))

            def step(t, stages):
                def made(s):
                    return t - STAGE[s] + 1

                def later(s):
                    return had(t, s)

                def normalize(s, dst, signal):
                    for g in range(G):
                        dve.tensor_scalar(dst[:, g], hh[s][:, g], mv[s][:, g, 0:1], rstd[s][:, g:g + 1],
                                          ALU.subtract, ALU.mult).then_inc(S[signal], 1)

                def mean_variance(s, n):
                    dve.wait_ge(S[s + "_h"], 2 * n)
                    gate()
                    for g in range(G):
                        dve.bn_aggr(mv[s][:, g], stats[s][:, g]).then_inc(S[s + "_mv"], 1)

                def heads_max(g, i):
                    half = "eo"[i]
                    if later("h"):
                        dve.wait_ge(S[f"h_T{g}{half}_made"], made("h") - 1)
                        dve.wait_ge(S["h_nmx"], 4 * (made("h") - 1))
                    dve.wait_ge(S[f"h_S{g}{half}_made"], made("h"))
                    gate()
                    for m in range(4):
                        h = 4 * i + m
                        last = dve.tensor_tensor_reduce(hs[:, g, h], bank[BANK[f"h_S{g}{half}"]][:, m * N:(m + 1) * N],
                                                        mneg[:, g], 1.0, -BIG, ALU.add, ALU.max, hmx[:, g, h:h + 1])
                    last.then_inc(S[f"h_S{g}{half}_read"], 1)
                    dve.wait_ge(S[f"h_S{g}{half}_read"], made("h"))
                    heads = slice(4 * i, 4 * i + 4)
                    dve.tensor_scalar(hnmx[:, g, heads], hmx[:, g, heads], -(DH ** -0.5), None, ALU.mult).then_inc(S["h_nmx"], 1)

                def heads_mix(g, i):
                    heads = slice(4 * i, 4 * i + 4)
                    dve.wait_ge(S["h_e"], HEADS * (G * (made("h") - 1) + g) + 4 * (i + 1))
                    dve.reciprocal(hr[:, g, heads], hden[:, g, heads]).then_inc(S["h_r"], 1)
                    dve.wait_ge(S["h_r"], 4 * (made("h") - 1) + 2 * g + i + 1)
                    for h in range(4 * i, 4 * i + 4):
                        last = dve.scalar_tensor_tensor(out=hs[:, g, h], in0=hs[:, g, h], scalar=hr[:, g, h:h + 1],
                                                        in1=mix[:, g], op0=ALU.mult, op1=ALU.add)
                    last.then_inc(S["h_p"], 1)

                if "a" in stages:
                    dve.wait_ge(S["m_rstd"], made("a"))
                    if later("a"):
                        dve.wait_ge(S["a_xT_made"], made("a") - 1)
                        dve.wait_ge(S["x1_bias"], made("a") - 1)
                    normalize("m", x1, "x1_made")
                if isinstance(t, int) and t == 1:
                    weights_products()
                if "k" in stages:
                    dve.wait_ge(S["k_xhi"], made("k"))
                    dve.tensor_tensor(xT["k"][1][:], chunks(bank[BANK["k_xT"]]), as_f32(xT["k"][0][:]), ALU.subtract).then_inc(S["k_xT_read"], 1)
                if "m" in stages:
                    dve.wait_ge(S["m_xhi"], made("m"))
                    dve.tensor_tensor(xT["m"][1][:], x0T[:], as_f32(xT["m"][0][:]), ALU.subtract).then_inc(S["m_xlo"], 1)
                    dve.wait_ge(S["adj0_in"], 16 * made("m"))
                    dve.tensor_reduce(deg[:], adj0[:], AX.X, ALU.add).then_inc(S["m_deg"], 1)
                    dve.wait_ge(S["m_deg"], 3 * (made("m") - 1) + 1)
                    dve.tensor_scalar(degmax[:], deg[:], EPS_DEG, None, ALU.max).then_inc(S["m_deg"], 1)
                    dve.wait_ge(S["m_deg"], 3 * (made("m") - 1) + 2)
                    dve.reciprocal(rdeg[:], degmax[:]).then_inc(S["m_deg"], 1)
                if isinstance(t, int) and t == 0:
                    weights_values()
                if "a" in stages:
                    dve.wait_ge(S["a_xhi"], made("a"))
                    dve.tensor_tensor(xT["a"][1][:], chunks(bank[BANK["a_xT"]]), as_f32(xT["a"][0][:]), ALU.subtract).then_inc(S["a_xlo"], 1)
                if isinstance(t, int) and t == 1:
                    weights_heads()
                if isinstance(t, int) and t == 2:
                    weights_hops()
                if "k" in stages:
                    for g in range(G):
                        dve.wait_ge(S["k_yhi"], 4 * (made("k") - 1) + g + 1)
                        last = dve.tensor_copy(ks[:, g], bank[BANK[f"k_y2{g}"]][:, D:D + 2])
                    last.then_inc(S["k_s"], 1)
                    dve.wait_ge(S["k_s"], made("k"))
                    if later("k"):
                        dve.wait_ge(S["k_sj_made"], made("k") - 1)
                    for g in range(G):
                        last = dve.tensor_scalar(diag[:, g], ident[:], ks[:, g, 1:2], None, ALU.mult)
                    last.then_inc(S["k_diag"], 1)
                    dve.wait_ge(S["k_yhi"], 4 * (made("k") - 1) + 1)
                    dve.tensor_tensor(ky2[1][:, 0], bank[BANK["k_y20"]][:, 0:D], as_f32(ky2[0][:, 0]), ALU.subtract).then_inc(S["k_y20_read"], 1)
                    dve.wait_ge(S["k_yhi"], 4 * (made("k") - 1) + 2)
                    dve.tensor_tensor(ky2[1][:, 1], bank[BANK["k_y21"]][:, 0:D], as_f32(ky2[0][:, 1]), ALU.subtract).then_inc(S["k_y21_read"], 1)
                if "h" in stages:
                    dve.wait_ge(S["h_mneg"], made("h"))
                    heads_max(0, 0)
                if "k" in stages:
                    dve.wait_ge(S["k_sj_made"], made("k"))
                    if later("k"):
                        dve.wait_ge(S["k_w"], 2 * (made("k") - 1))
                    for g in range(G):
                        last = dve.tensor_scalar(kw[:, g], bank[BANK["k_sj"]][:, g * N:(g + 1) * N], ks[:, g, 0:1],
                                                 ke_col[:, 0:1], ALU.add, ALU.add)
                    last.then_inc(S["k_sj_read"], 1)
                if "h" in stages:
                    heads_max(0, 1)
                if "k" in stages:
                    dve.wait_ge(S["k_sj_read"], made("k"))
                    if later("k"):
                        dve.wait_ge(S["k_e"], made("k") - 1)
                    dve.scalar_tensor_tensor(out=kl[:], in0=kw[:], scalar=SLOPE, in1=kw[:], op0=ALU.mult, op1=ALU.max).then_inc(S["k_leaky"], 1)
                if "h" in stages:
                    dve.wait_ge(S["h_mix"], made("h"))
                    heads_mix(0, 0)
                    heads_max(1, 0)
                    heads_max(1, 1)
                if "k" in stages:
                    dve.wait_ge(S["k_e"], made("k"))
                    dve.wait_ge(S["adj3_in"], 16 * made("k"))
                    gate()
                    for g in range(G):
                        dve.tensor_tensor_reduce(kw[:, g], kz[:, g], adj3[:, g], 1.0, 0.0, ALU.mult, ALU.add, kden[:, g:g + 1]).then_inc(S["k_w"], 1)
                    dve.wait_ge(S["k_w"], 2 * made("k"))
                    dve.tensor_scalar(kden2[:], kden[:], EPS_ROW, None, ALU.add).then_inc(S["k_den"], 1)
                    dve.wait_ge(S["k_den"], 2 * made("k") - 1)
                    dve.reciprocal(krden[:], kden2[:]).then_inc(S["k_den"], 1)
                if "h" in stages:
                    heads_mix(0, 1)
                if "a" in stages:
                    dve.wait_ge(S["a_vhi"], made("a"))
                    dve.tensor_tensor(av[1][:, :, 0:D], bank[BANK["a_v"]][:].rearrange("p (g n) -> p g n", g=G), as_f32(av[0][:, :, 0:D]),
                                      ALU.subtract).then_inc(S["a_v_read"], 1)
                if "k" in stages:
                    dve.wait_ge(S["k_den"], 2 * made("k"))
                    if later("k"):
                        dve.wait_ge(S["k_T_made"], made("k") - 1)
                    for g in range(G):
                        dve.tensor_scalar(kt[:, g], kw[:, g], krden[:, g:g + 1], None, ALU.mult).then_inc(S["k_tr"], 1)
                if "h" in stages:
                    heads_mix(1, 0)
                if "k" in stages:
                    dve.wait_ge(S["k_Thi"], made("k"))
                    dve.tensor_tensor(kT_[1][:], bank[BANK["k_T"]][:, 0:G * N].rearrange("p (g n) -> p g n", g=G), as_f32(kT_[0][:]),
                                      ALU.subtract).then_inc(S["k_T_read"], 1)
                if "h" in stages:
                    heads_mix(1, 1)
                if "a" in stages:
                    dve.wait_ge(S["x1_bias"], made("a"))
                    for g in range(G):
                        dve.wait_ge(S[f"a_PV{g}_made"], made("a"))
                        dve.reciprocal(arden[:, g:g + 1], bank[BANK[f"a_PV{g}"]][:, D:D + 1]).then_inc(S["a_rden"], 1)
                    for g in range(G):
                        dve.wait_ge(S["a_rden"], 2 * (made("a") - 1) + g + 1)
                        dve.scalar_tensor_tensor(out=hh["a"][:, g], in0=bank[BANK[f"a_PV{g}"]][:, 0:D], scalar=arden[:, g:g + 1],
                                                 in1=x1b[:, g], op0=ALU.mult, op1=ALU.add).then_inc(S[f"a_PV{g}_read"], 1)
                    for g in range(G):
                        dve.wait_ge(S[f"a_PV{g}_read"], made("a"))
                        dve.bn_stats(stats["a"][:, g], hh["a"][:, g]).then_inc(S["a_h"], 1)
                    mean_variance("a", made("a"))
                if "k" in stages:
                    dve.wait_ge(S["k_yhi"], 4 * (made("k") - 1) + 3)
                    dve.tensor_tensor(ky1[1][:, 0], bank[BANK["k_y010"]][:, D:2 * D], as_f32(ky1[0][:, 0]), ALU.subtract).then_inc(S["k_Ty0_read"], 1)
                    dve.wait_ge(S["k_yhi"], 4 * (made("k") - 1) + 4)
                    dve.tensor_tensor(ky1[1][:, 1], bank[BANK["k_y011"]][:, D:2 * D], as_f32(ky1[0][:, 1]), ALU.subtract).then_inc(S["k_Ty1_read"], 1)
                if "h" in stages:
                    dve.wait_ge(S["h_ohi"], 2 * (made("h") - 1) + 1)
                    dve.tensor_tensor(oT[1][:, 0], by_four(bank[BANK["h_PV0"]]), as_f32(oT[0][:, 0]), ALU.subtract).then_inc(S["h_PV0_read"], 1)
                if "m" in stages:
                    dve.wait_ge(S["m_yhi"], 2 * (made("m") - 1) + 1)
                    dve.tensor_tensor(my[1][:, 0], bank[BANK["m_xW0"]][:, D:2 * D], as_f32(my[0][:, 0]), ALU.subtract).then_inc(S["m_xW0_read"], 1)
                if "a" in stages:
                    if "h" in stages:
                        dve.wait_ge(S["x2_bias"], made("h"))
                    if later("a"):
                        dve.wait_ge(S["a_x2T_made"], made("a") - 1)
                    dve.wait_ge(S["a_rstd"], made("a"))
                    normalize("a", x2, "x2_made")
                if "h" in stages:
                    dve.wait_ge(S["h_ohi"], 2 * (made("h") - 1) + 2)
                    dve.tensor_tensor(oT[1][:, 1], by_four(bank[BANK["h_PV1"]]), as_f32(oT[0][:, 1]), ALU.subtract).then_inc(S["h_PV1_read"], 1)
                if "k" in stages:
                    for g in range(G):
                        dve.wait_ge(S[f"k_TT{g}_made"], made("k"))
                        dve.tensor_tensor(ksum[:, g], bank[BANK[f"k_y01{g}"]][:, 0:D], bk3_bc[:], ALU.add).then_inc(S[f"k_TT{g}_read"], 1)
                    dve.wait_ge(S["x3_made"], 2 * made("k"))
                    for g in range(G):
                        dve.wait_ge(S[f"k_TT{g}_read"], made("k"))
                        dve.scalar_tensor_tensor(out=hh["k"][:, g], in0=ksum[:, g], scalar=0.0, in1=x3[:, g],
                                                 op0=ALU.max, op1=ALU.add).then_inc(S["k_sum"], 1)
                    for g in range(G):
                        dve.wait_ge(S["k_sum"], 2 * (made("k") - 1) + g + 1)
                        dve.bn_stats(stats["k"][:, g], hh["k"][:, g]).then_inc(S["k_h"], 1)
                    mean_variance("k", made("k"))
                if "m" in stages:
                    dve.wait_ge(S["m_yhi"], 2 * (made("m") - 1) + 2)
                    dve.tensor_tensor(my[1][:, 1], bank[BANK["m_xW1"]][:, D:2 * D], as_f32(my[0][:, 1]), ALU.subtract).then_inc(S["m_xW1_read"], 1)
                if "a" in stages:
                    dve.wait_ge(S["a_x2hi"], made("a"))
                    dve.tensor_tensor(xT["h"][1][:], chunks(bank[BANK["a_x2T"]]), as_f32(xT["h"][0][:]), ALU.subtract).then_inc(S["a_x2T_read"], 1)
                if "h" in stages:
                    dve.wait_ge(S["x2_bias"], made("h"))
                    dve.wait_ge(S["h_out_made"], made("h"))
                    dve.tensor_tensor(hh["h"][:], bank[BANK["h_out"]][:].rearrange("p (g n) -> p g n", g=G), x2b[:], ALU.add).then_inc(S["h_out_read"], 1)
                    dve.wait_ge(S["h_out_read"], made("h"))
                    for g in range(G):
                        dve.bn_stats(stats["h"][:, g], hh["h"][:, g]).then_inc(S["h_h"], 1)
                    mean_variance("h", made("h"))
                if "m" in stages:
                    dve.wait_ge(S["x0_in"], 16 * made("m"))
                    dve.wait_ge(S["m_deg"], 3 * made("m"))
                    for g in range(G):
                        dve.wait_ge(S[f"m_ag{g}_made"], made("m"))
                        dve.scalar_tensor_tensor(out=msum[:, g], in0=bank[BANK[f"m_xW{g}"]][:, D:2 * D], scalar=rdeg[:, g:g + 1],
                                                 in1=mx[:, g], op0=ALU.mult, op1=ALU.add).then_inc(S[f"m_ag{g}_read"], 1)
                    for g in range(G):
                        dve.wait_ge(S[f"m_ag{g}_read"], made("m"))
                        dve.scalar_tensor_tensor(out=hh["m"][:, g], in0=msum[:, g], scalar=0.0, in1=x0[:, g],
                                                 op0=ALU.max, op1=ALU.add).then_inc(S["m_sum"], 1)
                    for g in range(G):
                        dve.wait_ge(S["m_sum"], 2 * (made("m") - 1) + g + 1)
                        dve.bn_stats(stats["m"][:, g], hh["m"][:, g]).then_inc(S["m_h"], 1)
                    mean_variance("m", made("m"))
                if "h" in stages:
                    dve.wait_ge(S["h_rstd"], made("h"))
                    if "k" in stages:
                        dve.wait_ge(S["k_xT_made"], made("k"))
                    normalize("h", x3, "x3_made")
                if "k" in stages:
                    if later("k"):
                        dve.wait_ge(S["y_out"], 16 * (made("k") - 1))
                    dve.wait_ge(S["k_rstd"], made("k"))
                    normalize("k", y, "y_made")

            weights_mean()
            for t in range(4):
                step(t, stages_at(t))
            with dve.Fori(4, pairs) as t:
                step(t, "mahk")
            for t in range(pairs, steps):
                step(t, stages_at(t))


ARGS = ["x", "x_T", "adj_rows", "adj_T", "nodemask", "nodemask_T", "L0_gnn_W", "L1_gnn_Wq_w", "L1_gnn_Wk_w", "L1_gnn_Wv_w", "L1_gnn_Wv_b",
        "columns", "L2_gnn_W_qkv", "L2_gnn_W_out", "L2_gnn_b_out", "L3_gnn_Wv", "L3_gnn_ab", "L3_gnn_Wk", "L3_gnn_bk"]


def kernel(**inputs):
    import concourse.bacc as bacc
    from concourse.bass_utils import run_bass_kernel_spmd

    a = {n: np.asarray(v) for n, v in inputs.items()}
    a["nodemask"] = a["nodemask"].view(np.uint8)
    a["nodemask_T"] = a["nodemask"].T
    aw = a["L3_gnn_aw"][:, 0]
    vectors = (a["L1_gnn_Wq_b"], a["L1_gnn_Wk_b"], a["L3_gnn_bv"], aw[:D], aw[D:])
    a["columns"] = np.stack([v.reshape(C, 128) for v in vectors]).transpose(2, 0, 1)
    x, adj = a["x"], a["adj"]
    pairs = x.shape[0] // G
    a["x_T"] = x.reshape(pairs, G, N, C, 128).transpose(0, 4, 3, 1, 2).reshape(pairs, 128, C * G * N)
    a["adj_rows"] = adj.reshape(pairs, G, N, N).transpose(0, 2, 1, 3).reshape(pairs, N, G * N)
    a["adj_T"] = adj.reshape(pairs, G, N, N).transpose(0, 3, 1, 2).reshape(pairs, N, G * N)
    w = a["L0_gnn_W"]
    a["L0_gnn_W"] = np.concatenate([w[:, :D].T, w[:, D:].T], axis=1)
    a["L1_gnn_Wv_w"] = a["L1_gnn_Wv_w"].T
    a["L3_gnn_Wv"] = a["L3_gnn_Wv"].T
    a["L2_gnn_W_qkv"] = a["L2_gnn_W_qkv"].reshape(D, HEADS, 3, DH).transpose(0, 2, 1, 3).reshape(D, 3 * INNER)

    nc = bacc.Bacc("TRN2", target_bir_lowering=False, num_devices=1)
    arrays, args = {}, []
    for n in ARGS:
        arrays[f"in_{n}"] = np.ascontiguousarray(a[n])
        args.append(nc.dram_tensor(f"in_{n}", a[n].shape, mybir.dt.from_np(a[n].dtype), kind="ExternalInput").ap())
    out = nc.dram_tensor("out_0", a["x"].shape, F32, kind="ExternalOutput").ap()
    build(nc, *args, out)
    return run_bass_kernel_spmd(nc, [arrays], core_ids=[0]).results[0]["out_0"]
```
